# Optimizing a Trainium2 kernel written in Bass

```python
import numpy as np
import jax
import jax.numpy as jnp

def _softmax(x, axis=-1):
    return jax.nn.softmax(x, axis=axis)

def _gelu(x):
    return jax.nn.gelu(x, approximate=True)

def _silu(x):
    return jax.nn.silu(x)

def _sigmoid(x):
    return jax.nn.sigmoid(x)

def _layernorm(x, axis=-1, eps=1e-05):
    m = jnp.mean(x, axis=axis, keepdims=True)
    v = jnp.var(x, axis=axis, keepdims=True)
    return (x - m) / jnp.sqrt(v + eps)

def _scatter_add(tgt, idx, src, axis=0):
    return tgt.at[idx].add(src)

def _segment_sum(src, seg, n):
    return jax.ops.segment_sum(src, seg, n)
kernel_name = 'mk_seq_preln_d1_jaxref_r4_f90dc3'

def setup_inputs(seed: int=0):
    np.random.seed(seed)
    _w = jnp.asarray

    def _L0_attn_setup():
        import jax, jax.numpy as jnp
        import numpy as np
        N_EMBD = 256
        N_HEAD = 16
        N_LAYER = 24
        LAYER_ID = 12
        B, T = (4, 1024)
        Q = 64
        EPS = 1e-05 * 64

        def _static_params():
            C, H = (N_EMBD, N_HEAD)
            r01 = LAYER_ID / (N_LAYER - 1)
            r1a0 = 1.0 - LAYER_ID / N_LAYER
            ddd = np.arange(C, dtype=np.float64) / C
            maa_k = (1.0 - ddd ** r1a0).astype(np.float32).reshape(1, 1, C)
            maa_v = (1.0 - (ddd ** r1a0 + 0.3 * r01)).astype(np.float32).reshape(1, 1, C)
            maa_r = (1.0 - ddd ** (0.5 * r1a0)).astype(np.float32).reshape(1, 1, C)
            maa_g = maa_r.copy()
            h = np.arange(H, dtype=np.float64)
            decay = (-6.0 + 5.0 * (h / (H - 1)) ** (0.7 + 1.3 * r01)).astype(np.float32).reshape(H, 1)
            faaaa = (r01 * (1.0 - h / (H - 1))).astype(np.float32).reshape(H, 1)
            return (maa_k, maa_v, maa_r, maa_g, decay, faaaa)

        def _rwkv_forward(x, time_maa_k, time_maa_v, time_maa_r, time_maa_g, time_decay, time_faaaa, Wr, Wk, Wv, Wg, Wo, ln_w, ln_b):
            Bv, Tv, C = x.shape
            H = N_HEAD
            N = C // H
            nC = Tv // Q
            xx = jnp.pad(x, ((0, 0), (1, 0), (0, 0)))[:, :Tv] - x
            xk = x + xx * time_maa_k
            xv = x + xx * time_maa_v
            xr = x + xx * time_maa_r
            xg = x + xx * time_maa_g
            r = (xr @ Wr.T).reshape(Bv, Tv, H, N).transpose(0, 2, 1, 3)
            k = (xk @ Wk.T).reshape(Bv, Tv, H, N).transpose(0, 2, 3, 1)
            v = (xv @ Wv.T).reshape(Bv, Tv, H, N).transpose(0, 2, 1, 3)
            g = jax.nn.gelu(xg @ Wg.T, approximate=False)
            w = jnp.exp(-jnp.exp(time_decay))[:, 0]
            u = time_faaaa[:, 0]
            q = jnp.arange(Q)
            ws = (w ** Q).reshape(1, H, 1, 1)
            wk = (w[:, None] ** (Q - 1 - q)).reshape(1, H, 1, Q)
            wb = (w[:, None] ** q).reshape(1, H, Q, 1)
            i_idx = q[:, None]
            j_idx = q[None, :]
            e = jnp.maximum(i_idx - j_idx - 1, 0)
            Wmat = jnp.where(i_idx > j_idx, w[:, None, None] ** e, 0.0)
            Wmat = Wmat + jnp.eye(Q, dtype=x.dtype) * u[:, None, None]
            Wmat = Wmat.reshape(1, H, Q, Q)
            rr = r.reshape(Bv, H, nC, Q, N).transpose(2, 0, 1, 3, 4)
            kk = k.reshape(Bv, H, N, nC, Q).transpose(3, 0, 1, 2, 4)
            vv = v.reshape(Bv, H, nC, Q, N).transpose(2, 0, 1, 3, 4)

            def step(state, inp):
                rc, kc, vc = inp
                att = rc @ kc
                yc = att * Wmat @ vc + rc @ state * wb
                new_state = ws * state + kc * wk @ vc
                return (new_state, yc)
            state0 = jnp.zeros((Bv, H, N, N), dtype=x.dtype)
            _, ys = jax.lax.scan(step, state0, (rr, kk, vv))
            y = ys.transpose(1, 2, 0, 3, 4).reshape(Bv, H, Tv, N)
            y = y.transpose(0, 2, 1, 3)
            mean = y.mean(axis=-1, keepdims=True)
            var = y.var(axis=-1, keepdims=True)
            yn = (y - mean) / jnp.sqrt(var + EPS)
            yn = yn * ln_w.reshape(1, 1, H, N) + ln_b.reshape(1, 1, H, N)
            yn = yn.reshape(Bv, Tv, C)
            out = yn * g @ Wo.T
            return out
        key = jax.random.key(seed)
        ks = jax.random.split(key, 8)
        C = N_EMBD
        maa_k, maa_v, maa_r, maa_g, decay, faaaa = _static_params()
        std = 0.02
        return {'x': jax.random.normal(ks[0], (B, T, C), dtype=jnp.float32), 'time_maa_k': jnp.asarray(maa_k), 'time_maa_v': jnp.asarray(maa_v), 'time_maa_r': jnp.asarray(maa_r), 'time_maa_g': jnp.asarray(maa_g), 'time_decay': jnp.asarray(decay), 'time_faaaa': jnp.asarray(faaaa), 'Wr': jax.random.normal(ks[1], (C, C), dtype=jnp.float32) * std, 'Wk': jax.random.normal(ks[2], (C, C), dtype=jnp.float32) * std, 'Wv': jax.random.normal(ks[3], (C, C), dtype=jnp.float32) * std, 'Wg': jax.random.normal(ks[4], (C, C), dtype=jnp.float32) * std, 'Wo': jax.random.normal(ks[5], (C, C), dtype=jnp.float32) * std, 'ln_w': jnp.ones((C,), dtype=jnp.float32), 'ln_b': jnp.zeros((C,), dtype=jnp.float32)}
    _L0_attn_in = _L0_attn_setup()

    def _L0_ffn_setup():
        import jax, jax.numpy as jnp
        import numpy as np
        B, S, H, F, E, K = (4, 512, 256, 896, 8, 2)
        CAP_FACTOR = 1.25

        def _moe_forward(hidden_states, gate_w, w1, w2, w3):
            b, s, h = hidden_states.shape
            dtype = hidden_states.dtype
            x = hidden_states.reshape(-1, h)
            router_logits = x @ gate_w.T
            expert_weights = jax.nn.softmax(router_logits.astype(jnp.float32), axis=1)
            _, selected_experts = jax.lax.top_k(expert_weights, K)
            top_k_idx = selected_experts.reshape(b, s, K)
            probs = expert_weights.reshape(b, s, E)
            capacity = int(s * K / E * CAP_FACTOR)
            expert_mask = jax.nn.one_hot(top_k_idx, E, dtype=jnp.int32)
            mask_fused = expert_mask.reshape(b, s * K, E)
            count_fused = jnp.cumsum(mask_fused, axis=1)
            count = count_fused.reshape(b, s, K, E)
            trunc_mask = expert_mask * (count <= capacity).astype(jnp.int32)
            combined_mask = trunc_mask.sum(axis=2)
            masked_probs = probs * combined_mask
            pos_fused = mask_fused * count_fused
            pos = pos_fused.reshape(b, s, K, E)
            combined_pos = pos.sum(axis=2) * combined_mask
            pos_in_cap = jax.nn.one_hot(combined_pos, capacity + 1, dtype=jnp.int32)
            combine_mask = masked_probs[..., None] * pos_in_cap
            combine_mask = combine_mask[..., 1:].astype(dtype)
            dispatch_mask = (combine_mask != 0).astype(dtype)
            dispatch = jnp.einsum('bsm,bsec->ebcm', hidden_states, dispatch_mask)
            h1 = jnp.einsum('ebcm,emh->ebch', dispatch, w1)
            h3 = jnp.einsum('ebcm,emh->ebch', dispatch, w3)
            expert_out = jnp.einsum('ebch,ehm->ebcm', jax.nn.silu(h1) * h3, w2)
            final = jnp.einsum('ebcm,bsec->bsm', expert_out, combine_mask)
            return final
        key = jax.random.key(seed)
        k1, k2, k3, k4, k5 = jax.random.split(key, 5)
        s_h = 1.0 / np.sqrt(H)
        s_f = 1.0 / np.sqrt(F)
        return {'hidden_states': jax.random.normal(k1, (B, S, H), dtype=jnp.float32), 'gate_w': jax.random.normal(k2, (E, H), dtype=jnp.float32) * s_h, 'w1': jax.random.normal(k3, (E, H, F), dtype=jnp.float32) * s_h, 'w2': jax.random.normal(k4, (E, F, H), dtype=jnp.float32) * s_f, 'w3': jax.random.normal(k5, (E, H, F), dtype=jnp.float32) * s_h}
    _L0_ffn_in = _L0_ffn_setup()
    _d = {'L0_attn_x': _L0_attn_in['x'], 'L0_attn_time_maa_k': _L0_attn_in['time_maa_k'], 'L0_attn_time_maa_v': _L0_attn_in['time_maa_v'], 'L0_attn_time_maa_r': _L0_attn_in['time_maa_r'], 'L0_attn_time_maa_g': _L0_attn_in['time_maa_g'], 'L0_attn_time_decay': _L0_attn_in['time_decay'], 'L0_attn_time_faaaa': _L0_attn_in['time_faaaa'], 'L0_attn_Wr': _L0_attn_in['Wr'], 'L0_attn_Wk': _L0_attn_in['Wk'], 'L0_attn_Wv': _L0_attn_in['Wv'], 'L0_attn_Wg': _L0_attn_in['Wg'], 'L0_attn_Wo': _L0_attn_in['Wo'], 'L0_attn_ln_w': _L0_attn_in['ln_w'], 'L0_attn_ln_b': _L0_attn_in['ln_b'], 'L0_ffn_gate_w': _L0_ffn_in['gate_w'], 'L0_ffn_w1': _L0_ffn_in['w1'], 'L0_ffn_w2': _L0_ffn_in['w2'], 'L0_ffn_w3': _L0_ffn_in['w3']}
    _x0 = _d['L0_attn_x']
    _d['L0_attn_x'] = jax.random.normal(jax.random.fold_in(jax.random.key(seed), 1), (4, 1024, 256), dtype=_x0.dtype)
    del _x0
    return _d

def reference(L0_attn_x, L0_attn_time_maa_k, L0_attn_time_maa_v, L0_attn_time_maa_r, L0_attn_time_maa_g, L0_attn_time_decay, L0_attn_time_faaaa, L0_attn_Wr, L0_attn_Wk, L0_attn_Wv, L0_attn_Wg, L0_attn_Wo, L0_attn_ln_w, L0_attn_ln_b, L0_ffn_gate_w, L0_ffn_w1, L0_ffn_w2, L0_ffn_w3):

    def _L0_attn_ref(x, time_maa_k, time_maa_v, time_maa_r, time_maa_g, time_decay, time_faaaa, Wr, Wk, Wv, Wg, Wo, ln_w, ln_b):
        import jax, jax.numpy as jnp
        import numpy as np
        N_EMBD = 256
        N_HEAD = 16
        N_LAYER = 24
        LAYER_ID = 12
        B, T = (4, 1024)
        Q = 64
        EPS = 1e-05 * 64

        def _static_params():
            C, H = (N_EMBD, N_HEAD)
            r01 = LAYER_ID / (N_LAYER - 1)
            r1a0 = 1.0 - LAYER_ID / N_LAYER
            ddd = np.arange(C, dtype=np.float64) / C
            maa_k = (1.0 - ddd ** r1a0).astype(np.float32).reshape(1, 1, C)
            maa_v = (1.0 - (ddd ** r1a0 + 0.3 * r01)).astype(np.float32).reshape(1, 1, C)
            maa_r = (1.0 - ddd ** (0.5 * r1a0)).astype(np.float32).reshape(1, 1, C)
            maa_g = maa_r.copy()
            h = np.arange(H, dtype=np.float64)
            decay = (-6.0 + 5.0 * (h / (H - 1)) ** (0.7 + 1.3 * r01)).astype(np.float32).reshape(H, 1)
            faaaa = (r01 * (1.0 - h / (H - 1))).astype(np.float32).reshape(H, 1)
            return (maa_k, maa_v, maa_r, maa_g, decay, faaaa)

        def _rwkv_forward(x, time_maa_k, time_maa_v, time_maa_r, time_maa_g, time_decay, time_faaaa, Wr, Wk, Wv, Wg, Wo, ln_w, ln_b):
            Bv, Tv, C = x.shape
            H = N_HEAD
            N = C // H
            nC = Tv // Q
            xx = jnp.pad(x, ((0, 0), (1, 0), (0, 0)))[:, :Tv] - x
            xk = x + xx * time_maa_k
            xv = x + xx * time_maa_v
            xr = x + xx * time_maa_r
            xg = x + xx * time_maa_g
            r = (xr @ Wr.T).reshape(Bv, Tv, H, N).transpose(0, 2, 1, 3)
            k = (xk @ Wk.T).reshape(Bv, Tv, H, N).transpose(0, 2, 3, 1)
            v = (xv @ Wv.T).reshape(Bv, Tv, H, N).transpose(0, 2, 1, 3)
            g = jax.nn.gelu(xg @ Wg.T, approximate=False)
            w = jnp.exp(-jnp.exp(time_decay))[:, 0]
            u = time_faaaa[:, 0]
            q = jnp.arange(Q)
            ws = (w ** Q).reshape(1, H, 1, 1)
            wk = (w[:, None] ** (Q - 1 - q)).reshape(1, H, 1, Q)
            wb = (w[:, None] ** q).reshape(1, H, Q, 1)
            i_idx = q[:, None]
            j_idx = q[None, :]
            e = jnp.maximum(i_idx - j_idx - 1, 0)
            Wmat = jnp.where(i_idx > j_idx, w[:, None, None] ** e, 0.0)
            Wmat = Wmat + jnp.eye(Q, dtype=x.dtype) * u[:, None, None]
            Wmat = Wmat.reshape(1, H, Q, Q)
            rr = r.reshape(Bv, H, nC, Q, N).transpose(2, 0, 1, 3, 4)
            kk = k.reshape(Bv, H, N, nC, Q).transpose(3, 0, 1, 2, 4)
            vv = v.reshape(Bv, H, nC, Q, N).transpose(2, 0, 1, 3, 4)

            def step(state, inp):
                rc, kc, vc = inp
                att = rc @ kc
                yc = att * Wmat @ vc + rc @ state * wb
                new_state = ws * state + kc * wk @ vc
                return (new_state, yc)
            state0 = jnp.zeros((Bv, H, N, N), dtype=x.dtype)
            _, ys = jax.lax.scan(step, state0, (rr, kk, vv))
            y = ys.transpose(1, 2, 0, 3, 4).reshape(Bv, H, Tv, N)
            y = y.transpose(0, 2, 1, 3)
            mean = y.mean(axis=-1, keepdims=True)
            var = y.var(axis=-1, keepdims=True)
            yn = (y - mean) / jnp.sqrt(var + EPS)
            yn = yn * ln_w.reshape(1, 1, H, N) + ln_b.reshape(1, 1, H, N)
            yn = yn.reshape(Bv, Tv, C)
            out = yn * g @ Wo.T
            return out
        return _rwkv_forward(x, time_maa_k, time_maa_v, time_maa_r, time_maa_g, time_decay, time_faaaa, Wr, Wk, Wv, Wg, Wo, ln_w, ln_b)

    def _L0_ffn_ref(hidden_states, gate_w, w1, w2, w3):
        import jax, jax.numpy as jnp
        import numpy as np
        B, S, H, F, E, K = (4, 512, 256, 896, 8, 2)
        CAP_FACTOR = 1.25

        def _moe_forward(hidden_states, gate_w, w1, w2, w3):
            b, s, h = hidden_states.shape
            dtype = hidden_states.dtype
            x = hidden_states.reshape(-1, h)
            router_logits = x @ gate_w.T
            expert_weights = jax.nn.softmax(router_logits.astype(jnp.float32), axis=1)
            _, selected_experts = jax.lax.top_k(expert_weights, K)
            top_k_idx = selected_experts.reshape(b, s, K)
            probs = expert_weights.reshape(b, s, E)
            capacity = int(s * K / E * CAP_FACTOR)
            expert_mask = jax.nn.one_hot(top_k_idx, E, dtype=jnp.int32)
            mask_fused = expert_mask.reshape(b, s * K, E)
            count_fused = jnp.cumsum(mask_fused, axis=1)
            count = count_fused.reshape(b, s, K, E)
            trunc_mask = expert_mask * (count <= capacity).astype(jnp.int32)
            combined_mask = trunc_mask.sum(axis=2)
            masked_probs = probs * combined_mask
            pos_fused = mask_fused * count_fused
            pos = pos_fused.reshape(b, s, K, E)
            combined_pos = pos.sum(axis=2) * combined_mask
            pos_in_cap = jax.nn.one_hot(combined_pos, capacity + 1, dtype=jnp.int32)
            combine_mask = masked_probs[..., None] * pos_in_cap
            combine_mask = combine_mask[..., 1:].astype(dtype)
            dispatch_mask = (combine_mask != 0).astype(dtype)
            dispatch = jnp.einsum('bsm,bsec->ebcm', hidden_states, dispatch_mask)
            h1 = jnp.einsum('ebcm,emh->ebch', dispatch, w1)
            h3 = jnp.einsum('ebcm,emh->ebch', dispatch, w3)
            expert_out = jnp.einsum('ebch,ehm->ebcm', jax.nn.silu(h1) * h3, w2)
            final = jnp.einsum('ebcm,bsec->bsm', expert_out, combine_mask)
            return final
        return _moe_forward(hidden_states, gate_w, w1, w2, w3)
    x = L0_attn_x
    x = x + _L0_attn_ref(_layernorm(x, axis=-1), L0_attn_time_maa_k, L0_attn_time_maa_v, L0_attn_time_maa_r, L0_attn_time_maa_g, L0_attn_time_decay, L0_attn_time_faaaa, L0_attn_Wr, L0_attn_Wk, L0_attn_Wv, L0_attn_Wg, L0_attn_Wo, L0_attn_ln_w, L0_attn_ln_b)
    x = x + _L0_ffn_ref(_layernorm(x, axis=-1), L0_ffn_gate_w, L0_ffn_w1, L0_ffn_w2, L0_ffn_w3)
    return x

_drawn_inputs = setup_inputs


def setup_inputs(seed=0):
    import zlib

    import numpy as np

    out = dict(_drawn_inputs(seed))
    spreads = {'L0_attn_ln_w': (1.0, 0.6), 'L0_attn_ln_b': (0.0, 0.734)}
    factors = {'L0_attn_time_faaaa': 21.352}
    for name, (base, spread) in spreads.items():
        noise = np.random.default_rng([zlib.crc32(name.encode()), seed]).standard_normal(out[name].shape)
        drawn = base * np.exp(spread * noise) if base else spread * noise
        out[name] = jnp.asarray(drawn.astype(out[name].dtype))
    for name, factor in factors.items():
        out[name] = (out[name] * factor).astype(out[name].dtype)
    return out
```

```python
from contextlib import ExitStack

import numpy as np

import concourse.bass as bass
from concourse import mybir

F32 = mybir.dt.float32
F32R = mybir.dt.float32r
I32 = mybir.dt.int32
U32 = mybir.dt.uint32
ALU = mybir.AluOpType
ACT = mybir.ActivationFunctionType
AX_X = mybir.AxisListType.X

P = 128
B, T, C = 4, 1024, 256
NTOK = B * T
H = 16
N = C // H
KT = C // P
Q = P
TPS = 2
W = TPS * Q
STEPS = NTOK // W
SPB = T // W
HG = 4
NG = H // HG
GPS = TPS * NG
HPB = H // KT
LN_EPS = 1e-5
GN_EPS = 1e-5 * 64
E = 8
F = 896
FT = F // P
CAP = T * 2 // E * 5 // 4
SLOTS = B * CAP
ST = SLOTS // P
ROW = C + E + 1
DROP = 1.0e6
CHUNKS = [(0, 4), (4, 4), (8, 2)]
NCH = len(CHUNKS)


class At:

    alone = {}

    def __init__(self, const, reg=None, least=0):
        self.const, self.reg, self.least = const, reg, least

    def __sub__(self, k):
        return At(self.const - k, self.reg, self.least)

    def __add__(self, k):
        return At(self.const + k, self.reg, self.least)

    def count(self, per=1, more=0):
        v = per * self.const + more
        return v if self.reg is None else self.reg * per + v

    def wait(self, eng, sem, per=1, more=0):
        v = self.count(per, more)
        if self.reg is None:
            if v > 0:
                eng.wait_ge(sem, v)
        else:
            assert per * (self.least + self.const) + more > 0
            eng.wait_ge(sem, v)
            if eng in At.alone:
                eng.sem_inc(At.alone[eng], 1)

    def valid(self, n):
        return self.reg is not None or 0 <= self.const < n


class Chain:

    def __init__(self, eng, sem):
        self.eng, self.sem, self.n = eng, sem, 0

    def add(self, ins):
        self.n += 1
        ins.then_inc(self.sem, 1)

    def sync(self):
        self.eng.wait_ge(self.sem, self.n)

    def link(self, ins):
        self.add(ins)
        self.sync()

    def reset(self):
        if self.n:
            self.sync()
            self.eng.sem_inc(self.sem, -self.n)
            self.n = 0


def build(nc, x, maa, decay_row, decay_ch, u_row, wrT, wkT, wvT, wgT, woT, lnw, lnb, gateT, w1, w2, w3, out):
    disp = nc.dram_tensor("disp", [E * SLOTS, ROW], F32).ap()
    persist = ExitStack()
    with persist:
        def tensors(ctx):
            def sb(name, shape, dt=F32):
                return ctx.enter_context(nc.sbuf_tensor(name, shape, dt))

            def ps(name, shape):
                return ctx.enter_context(nc.psum_tensor(name, shape, F32))

            return sb, ps

        sems = {}

        def sem(name):
            if name not in sems:
                sems[name] = persist.enter_context(nc.semaphore(name))
            return sems[name]

        At.alone = {nc.sync: sem("sp_waited"), nc.gpsimd: sem("pool_waited")}
        sb, _ = tensors(persist)
        NW = KT * F
        whi = [[sb(f"whi0_{m}", [P, NW], F32R) for m in range(3)]]
        wlo = [[sb(f"wlo0_{m}", [P, NW], F32R) for m in range(3)]]
        wraw = [sb(f"wraw{k}", [P, NW]) for k in range(2)]
        ident = sb("ident", [P, P])
        with ExitStack() as ctx:
            phase_a(nc, *tensors(ctx), ctx, sem, ident, x, maa, decay_row, decay_ch, u_row,
                    (wrT, wkT, wvT, wgT, woT), lnw, lnb, gateT, disp, out)
        with ExitStack() as ctx:
            sb2, ps2 = tensors(ctx)
            whi.append([sb2(f"whi1_{m}", [P, NW], F32R) for m in range(3)])
            wlo.append([sb2(f"wlo1_{m}", [P, NW], F32R) for m in range(3)])
            phase_b(nc, sb2, ps2, ctx, sem, ident, whi, wlo, wraw, w1, w2, w3, disp, out)


def phase_a(nc, sb, ps, ctx, sem, ident, x, maa, decay_row, decay_ch, u_row, weights, lnw, lnb, gateT, disp, out):
    x_sb = sb("x_sb", [P, (STEPS + 1) * TPS, C])
    w_sb = [sb(f"w_sb{k}", [P, KT, C]) for k in range(5)]
    WR, WK, WV, WG, WO = w_sb
    gate_sb = sb("gate_sb", [P, KT, E])
    maa_sb = sb("maa_sb", [P, 4, KT])
    lnw_sb = sb("lnw_sb", [P, KT])
    lnb_sb = sb("lnb_sb", [P, KT])
    lam_row = sb("lam_row", [P, H])
    lam_ch = sb("lam_ch", [P, KT])
    u_sb = sb("u_sb", [P, H])
    vmean = sb("vmean", [P, KT * H])
    dmask = sb("dmask", [P, H, Q])
    kdecay = sb("kdecay", [P, H])
    rdecay = sb("rdecay", [P, KT, Q])
    sdecay = sb("sdecay", [P, KT])
    blockdiag = sb("blockdiag", [P, P])
    tri = sb("tri", [P, P])
    ones = sb("ones", [P, P])
    lag_i = sb("lag_i", [P, Q], I32)
    lag = sb("lag", [P, Q])
    col_i = sb("col_i", [P, Q], I32)
    colf = sb("colf", [P, Q])
    rest_i = sb("rest_i", [P, 1], I32)
    rest = sb("rest", [P, 1])
    iota_i = sb("iota_i", [P, E], I32)
    iota_e = sb("iota_e", [P, E])
    base_i = sb("base_i", [P, E], I32)
    base = sb("base", [P, E])
    tok = sb("tok", [P, NTOK // P], I32)
    mhalf = sb("mhalf", [P, TPS * H])
    empty = sb("empty", [P, ST, ROW])

    mv1 = sb("mv1", [P, TPS, 2])
    st1 = sb("st1", [P, TPS, 6])
    var1 = sb("var1", [P, TPS])
    rstd1 = sb("rstd1", [P, TPS])
    xn = sb("xn", [P, TPS, C])
    xT = [sb(f"xT{k}", [P, KT, W + 1]) for k in range(2)]
    diff = sb("diff", [P, KT, W])
    mix = [sb(f"mix{k}", [P, KT, W]) for k in range(4)]
    rT = sb("rT", [P, KT, W])
    r_heads = sb("r_heads", [P, KT, HPB, W])
    r_dec = sb("r_dec", [P, KT, W])
    kT = sb("kT", [P, KT, W])
    k_dec = sb("k_dec", [P, TPS, C])
    v = sb("v", [P, TPS, C])
    gT = [sb(f"gT{k}", [P, KT, W]) for k in range(2)]
    attm = [sb(f"attm{k}", [P, HG, Q]) for k in range(4)]
    state = [sb(f"state{k}", [P, KT, P]) for k in range(2)]
    kvm = sb("kvm", [P, KT, P])
    ysq = sb("ysq", [P, TPS, C])
    ssum = sb("ssum", [P, TPS * H])
    gvar = sb("gvar", [P, TPS * H])
    grstd = sb("grstd", [P, TPS * H])
    yn = sb("yn", [P, TPS, C])
    z = sb("z", [P, KT, W])
    zg = sb("zg", [P, KT, W])
    x1 = [sb(f"x1_{k}", [P, TPS, C]) for k in range(2)]
    st2 = sb("st2", [P, TPS, 6])
    mv2 = sb("mv2", [P, TPS, 2])
    var2 = sb("var2", [P, TPS])
    rstd2 = sb("rstd2", [P, TPS])
    row = [sb(f"row{k}", [P, TPS, ROW]) for k in range(2)]
    x2T = sb("x2T", [P, KT, W])
    lmax = sb("lmax", [P, TPS])
    lsub = sb("lsub", [P, TPS, E])
    lexp = sb("lexp", [P, TPS, E])
    lsum = sb("lsum", [P, TPS])
    lrec = sb("lrec", [P, TPS])
    top = sb("top", [P, TPS, 8])
    topi = sb("topi", [P, TPS, 8], U32)
    topf = sb("topf", [P, TPS, 2])
    hot = [[sb(f"hot{k}_{r}", [P, TPS, E]) for k in range(2)] for r in range(2)]
    took = [sb(f"took{r}", [P, TPS, E]) for r in range(2)]
    before = [sb(f"before{r}", [P, TPS, E]) for r in range(2)]
    over = sb("over", [P, TPS, E])
    slotf = sb("slotf", [P, TPS, E])
    pick = [sb(f"pick{k}", [P, TPS, E]) for k in range(2)]
    slot_k = sb("slot_k", [P, 2, TPS])
    slot_i = sb("slot_i", [P, 2, TPS], I32)
    mixt = sb("mixt", [P, KT, W])

    pX = ps("pX", [P, KT, W])
    pO = ps("pO", [P, 512])
    pK = ps("pK", [P, 512])
    pA = ps("pA", [P, KT, W])
    pB = ps("pB", [P, KT, W])
    pS = [ps(f"pS{k}", [P, HG, Q]) for k in range(2)]
    pY = ps("pY", [P, TPS, C])

    pO_tok = pO[:, :].rearrange("p (t c) -> p t c", t=TPS)
    pO_ch = pO[:, :].rearrange("p (k w) -> p k w", k=KT)
    pK_tok = pK[:, :].rearrange("p (t c) -> p t c", t=TPS)
    p_logit = pK[:, 0:TPS * E].rearrange("p (t e) -> p t e", t=TPS)
    p_count = pK[:, TPS * E:2 * TPS * E].rearrange("p (t e) -> p t e", t=TPS)
    pA_tok = pA[:, :, :].rearrange("p a b -> p (a b)").rearrange("p (t c) -> p t c", t=TPS)
    p_kv = pA[:, :, :].rearrange("p a b -> p (a b)").rearrange("p (t k c) -> p t k c", t=TPS, k=KT)

    x_in = sem("x_in")
    const_in = sem("const_in")
    set_dve, set_pool, set_act = sem("set_dve"), sem("set_pool"), sem("set_act")
    empty_out = sem("empty_out")
    stat1_ready, rstd1_ready, xn_ready = sem("stat1_ready"), sem("rstd1_ready"), sem("xn_ready")
    xt_done, xT_ready = sem("xt_done"), sem("xT_ready")
    diff_ready = sem("diff_ready")
    mix_ready = [sem(f"mix_ready{k}") for k in range(4)]
    proj_done = [sem(f"proj_done{k}") for k in range(4)]
    rT_ready, kT_ready, v_ready, gT_ready = sem("rT_ready"), sem("kT_ready"), sem("v_ready"), sem("gT_ready")
    heads_ready, rdec_ready = sem("heads_ready"), sem("rdec_ready")
    kt_done, kdec_ready, kv_done, state_ready = sem("kt_done"), sem("kdec_ready"), sem("kv_done"), sem("state_ready")
    att_done, attm_ready, intra_done = sem("att_done"), sem("attm_ready"), sem("intra_done")
    ysq_ready, ssum_ready, grstd_ready, yn_ready = sem("ysq_ready"), sem("ssum_ready"), sem("grstd_ready"), sem("yn_ready")
    zt_done, z_ready, zg_ready, wo_done = sem("zt_done"), sem("z_ready"), sem("zg_ready"), sem("wo_done")
    x1_ready, x1_out, stat2_ready, rstd2_ready = sem("x1_ready"), sem("x1_out"), sem("stat2_ready"), sem("rstd2_ready")
    xn2_ready, x2t_done, x2T_ready = sem("xn2_ready"), sem("x2t_done"), sem("x2T_ready")
    logit_done, lsub_ready, lexp_ready, took_ready = sem("logit_done"), sem("lsub_ready"), sem("lexp_ready"), sem("took_ready")
    count_done, slot_ready, sent = sem("count_done"), sem("slot_ready"), sem("sent")
    dve_chain, pool_chain = sem("dve_chain"), sem("pool_chain")

    NCONST = 5 + 7
    x_view = x.rearrange("(b t p) c -> b p t c", b=B, p=P)
    out_view = out[0:NTOK, :].rearrange("(s t p) c -> s p t c", t=TPS, p=P)

    def walk(eng, step):
        for s in range(-1, SPB):
            step(At(s))
        with eng.Fori(SPB, STEPS - SPB + 1, SPB) as s0:
            for j in range(SPB):
                step(At(j, s0, SPB))
        for s in range(STEPS, STEPS + 3):
            step(At(s))

    with nc.Block() as block:

        @block.sync
        def _(sp):
            sp.dma_start(x_sb[:, 0:T // P, :], x_view[0]).then_inc(x_in, 16)
            for k in range(5):
                sp.dma_start(w_sb[k][:], weights[k].rearrange("(k p) c -> p k c", p=P)).then_inc(const_in, 16)
            for dst, src in ((gate_sb, gateT.rearrange("(k p) e -> p k e", p=P)), (maa_sb, maa),
                             (lnw_sb, lnw), (lnb_sb, lnb), (lam_row, decay_row), (lam_ch, decay_ch), (u_sb, u_row)):
                sp.dma_start(dst[:], src).then_inc(const_in, 16)
            for b in range(1, B):
                sp.wait_ge(x_in, 16 * b)
                sp.dma_start(x_sb[:, b * T // P:(b + 1) * T // P, :], x_view[b]).then_inc(x_in, 16)
            sp.wait_ge(set_pool, 1)
            for e in range(E):
                sp.dma_start(disp[e * SLOTS:(e + 1) * SLOTS, :].rearrange("(p t) c -> p (t c)", p=P),
                             empty[:, :, :].rearrange("p t c -> p (t c)")).then_inc(empty_out, 16)

            def step(s):
                front, post = s, s - 2
                if post.valid(STEPS):
                    post.wait(sp, x1_ready, 1, 1)
                    post.wait(sp, x1_out, 16)
                    q = post.count()
                    dst = out_view[q] if post.reg is None else out_view[bass.ds(q, 1)].rearrange("o p t c -> p (o t) c")
                    sp.dma_start(dst, x1[post.const % 2][:]).then_inc(x1_out, 16)
                if front.valid(STEPS):
                    front.wait(sp, rT_ready, 1, 1)
                    front.wait(sp, att_done, GPS)
                    if front.const == 0 and front.reg is None:
                        sp.wait_ge(set_dve, 1)
                    for h in range(HPB):
                        sp.dma_start(r_heads[h * N:(h + 1) * N, :, h, :], rT[h * N:(h + 1) * N, :, :]).then_inc(heads_ready, 16)

            walk(sp, step)
            sp.wait_ge(x1_out, 16 * STEPS)

        @block.gpsimd
        def _(pool):
            chain = Chain(pool, pool_chain)
            nc.gpsimd.memset(empty[:], 0.0)
            chain.link(nc.gpsimd.iota(lag_i[:, 0:ST], pattern=[[1, ST]], base=NTOK, channel_multiplier=ST))
            nc.gpsimd.tensor_copy(empty[:, :, ROW - 1].bitcast(I32), lag_i[:, 0:ST]).then_inc(set_pool, 1)
            chain.add(nc.gpsimd.memset(ones[:], 1.0))
            chain.add(nc.gpsimd.memset(mhalf[:], -0.5))
            chain.add(nc.gpsimd.memset(blockdiag[:], 1.0))
            chain.link(nc.gpsimd.memset(x_sb[:, STEPS * TPS:, :], 0.0))
            pool.wait_ge(set_pool, 1)
            chain.add(nc.gpsimd.affine_select(out=ident[:], in_=ones[:], compare_op=ALU.is_equal, fill=0.0,
                                              base=0, pattern=[[1, P]], channel_multiplier=-1))
            chain.add(nc.gpsimd.affine_select(out=tri[:], in_=ones[:], compare_op=ALU.is_ge, fill=0.0,
                                              base=0, pattern=[[1, P]], channel_multiplier=-1))
            bd = blockdiag[:].rearrange("p (g n) -> p g n", n=N)
            chain.link(nc.gpsimd.affine_select(out=bd, in_=bd, compare_op=ALU.is_ge, fill=0.0,
                                               base=0, pattern=[[-N, P // N], [0, N]], channel_multiplier=1))
            chain.link(nc.gpsimd.affine_select(out=bd, in_=bd, compare_op=ALU.is_ge, fill=0.0,
                                               base=N - 1, pattern=[[N, P // N], [0, N]], channel_multiplier=-1))
            chain.add(nc.gpsimd.iota(lag_i[:], pattern=[[1, Q]], base=-1, channel_multiplier=-1))
            chain.add(nc.gpsimd.iota(col_i[:], pattern=[[1, Q]], base=0, channel_multiplier=0))
            chain.add(nc.gpsimd.iota(rest_i[:], pattern=[[0, 1]], base=Q - 1, channel_multiplier=-1))
            chain.add(nc.gpsimd.iota(iota_i[:], pattern=[[1, E]], base=0, channel_multiplier=0))
            chain.add(nc.gpsimd.iota(base_i[:], pattern=[[SLOTS, E]], base=-1, channel_multiplier=0))
            chain.link(nc.gpsimd.iota(tok[:], pattern=[[P, NTOK // P]], base=0, channel_multiplier=1))
            chain.reset()
            nc.gpsimd.engine_nop().then_inc(set_pool, 1)
            pool.wait_ge(set_act, 2)
            nc.gpsimd.affine_select(out=dmask[:], in_=dmask[:], compare_op=ALU.is_gt, fill=0.0,
                                    base=0, pattern=[[0, H], [1, Q]], channel_multiplier=-1).then_inc(set_pool, 1)
            pool.wait_ge(empty_out, 16 * E)

            def step(s):
                nxt, front, att, post, send = s + 1, s, s - 1, s - 2, s - 3
                if post.valid(STEPS):
                    post.wait(pool, stat2_ready, 1, 1)
                    pool.wait_ge(set_pool, 3)
                    chain.link(nc.gpsimd.tensor_scalar(var2[:], mv2[:, :, 1], LN_EPS, None, ALU.add))
                    nc.gpsimd.tensor_tensor(rstd2[:], var2[:], mhalf[:, 0:TPS], ALU.pow).then_inc(rstd2_ready, 1)
                if front.valid(STEPS):
                    g = 3
                    front.wait(pool, diff_ready, 1, 1)
                    front.wait(pool, proj_done[g])
                    pool.wait_ge(set_pool, 3)
                    for k in range(KT):
                        chain.add(nc.gpsimd.tensor_scalar(mixt[:, k, :], diff[:, k, :], maa_sb[:, g, k:k + 1], None, ALU.mult))
                    chain.sync()
                    nc.gpsimd.tensor_tensor(mix[g][:], mixt[:], xT[front.const % 2][:, :, 1:], ALU.add).then_inc(mix_ready[g], 1)
                if att.valid(STEPS):
                    att.wait(pool, ssum_ready, 1, 1)
                    pool.wait_ge(set_pool, 3)
                    chain.link(nc.gpsimd.tensor_scalar(gvar[:], ssum[:], 1.0 / N, GN_EPS, ALU.mult, ALU.add))
                    nc.gpsimd.tensor_tensor(grstd[:], gvar[:], mhalf[:], ALU.pow).then_inc(grstd_ready, 1)
                if nxt.valid(STEPS):
                    nxt.wait(pool, stat1_ready, 1, 1)
                    pool.wait_ge(set_pool, 3)
                    chain.link(nc.gpsimd.tensor_scalar(var1[:], mv1[:, :, 1], LN_EPS, None, ALU.add))
                    nc.gpsimd.tensor_tensor(rstd1[:], var1[:], mhalf[:, 0:TPS], ALU.pow).then_inc(rstd1_ready, 1)
                if front.valid(STEPS):
                    front.wait(pool, intra_done, GPS)
                    front.wait(pool, rT_ready, 1, 1)
                    nc.gpsimd.tensor_tensor(
                        r_dec[:].rearrange("p k (t i) -> p k t i", i=Q), rT[:].rearrange("p k (t i) -> p k t i", i=Q),
                        rdecay[:].unsqueeze(2).to_broadcast([P, KT, TPS, Q]), ALU.mult).then_inc(rdec_ready, 1)
                if att.valid(STEPS):
                    att.wait(pool, wo_done)
                    att.wait(pool, z_ready, 1, 1)
                    nc.gpsimd.tensor_tensor(zg[:], z[:], gT[att.const % 2][:], ALU.mult).then_inc(zg_ready, 1)
                if send.valid(STEPS):
                    send.wait(pool, slot_ready, 1, 1)
                    pool.wait_ge(set_pool, 3)
                    for k in range(2):
                        for t in range(TPS):
                            nc.gpsimd.indirect_dma_start(
                                disp, bass.IndirectOffsetOnAxis(ap=slot_i[:, k, t:t + 1], axis=0),
                                row[send.const % 2][:, t, :], None,
                                bounds_check=E * SLOTS - 1, oob_is_err=False).then_inc(sent, 16)
                chain.reset()

            walk(pool, step)
            pool.wait_ge(sent, 16 * 2 * TPS * STEPS)

        @block.scalar
        def _(act):
            act.wait_ge(const_in, 16 * NCONST)
            nc.scalar.activation(lam_row[:], lam_row[:], ACT.Exp)
            nc.scalar.activation(lam_ch[:], lam_ch[:], ACT.Exp).then_inc(set_act, 1)
            act.wait_ge(set_dve, 2)
            for h in range(H):
                nc.scalar.activation(dmask[:, h, :], lag[:], ACT.Exp, scale=lam_row[:, h:h + 1])
            for k in range(KT):
                nc.scalar.activation(rdecay[:, k, :], colf[:], ACT.Exp, scale=lam_ch[:, k:k + 1])
            nc.scalar.activation(kdecay[:], lam_row[:], ACT.Exp, scale=rest[:, 0:1])
            nc.scalar.activation(sdecay[:], lam_ch[:], ACT.Exp, scale=float(Q)).then_inc(set_act, 1)

            def step(s):
                front, att, post = s, s - 1, s - 2
                if front.valid(STEPS):
                    front.wait(act, xt_done, 1, 1)
                    front.wait(act, mix_ready[2])
                    front.wait(act, mix_ready[3])
                    nc.scalar.copy(xT[front.const % 2][:, :, 1:], pX[:]).then_inc(xT_ready, 1)
                if post.valid(STEPS):
                    post.wait(act, x2t_done, 1, 1)
                    post.wait(act, logit_done)
                    nc.scalar.copy(x2T[:], pO_ch).then_inc(x2T_ready, 1)
                if att.valid(STEPS):
                    att.wait(act, intra_done, GPS, GPS)
                    att.wait(act, yn_ready)
                    nc.scalar.activation(ysq[:], pY[:], ACT.Square).then_inc(ysq_ready, 1)
                if front.valid(STEPS):
                    front.wait(act, proj_done[0], 1, 1)
                    front.wait(act, heads_ready, 16 * HPB)
                    front.wait(act, rdec_ready)
                    nc.scalar.copy(rT[:], pA[:]).then_inc(rT_ready, 1)
                if post.valid(STEPS):
                    post.wait(act, lsub_ready, 1, 1)
                    nc.scalar.activation(lexp[:], lsub[:], ACT.Exp).then_inc(lexp_ready, 1)
                if front.valid(STEPS):
                    front.wait(act, proj_done[1], 1, 1)
                    front.wait(act, att_done, GPS)
                    nc.scalar.copy(kT[:], pB[:]).then_inc(kT_ready, 1)
                    front.wait(act, proj_done[2], 1, 1)
                    front.wait(act, intra_done, GPS)
                    nc.scalar.copy(v[:], pA_tok).then_inc(v_ready, 1)
                    front.wait(act, proj_done[3], 1, 1)
                    front.wait(act, zg_ready, 1, -1)
                    nc.scalar.activation(gT[front.const % 2][:], pB[:], ACT.Gelu).then_inc(gT_ready, 1)
                if att.valid(STEPS):
                    att.wait(act, zt_done, 1, 1)
                    att.wait(act, zg_ready)
                    for k in range(KT):
                        ins = nc.scalar.activation(z[:, k, :], pX[:, k, :], ACT.Identity,
                                                   scale=lnw_sb[:, k:k + 1], bias=lnb_sb[:, k:k + 1])
                    ins.then_inc(z_ready, 1)

            walk(act, step)

        @block.vector
        def _(dve):
            chain = Chain(dve, dve_chain)
            nc.vector.memset(r_heads[:], 0.0).then_inc(set_dve, 1)
            dve.wait_ge(set_pool, 2)
            chain.link(nc.vector.tensor_copy(lag[:], lag_i[:]))
            chain.add(nc.vector.tensor_scalar(lag[:], lag[:], 0.0, None, ALU.max))
            chain.add(nc.vector.tensor_copy(colf[:], col_i[:]))
            chain.add(nc.vector.tensor_copy(rest[:], rest_i[:]))
            chain.add(nc.vector.tensor_copy(iota_e[:], iota_i[:]))
            chain.add(nc.vector.tensor_copy(base[:], base_i[:]))
            chain.add(nc.vector.memset(state[0][:], 0.0))
            chain.add(nc.vector.memset(before[0][:], 0.0))
            dve.wait_ge(const_in, 16 * NCONST)
            wv4 = WV[:].rearrange("p k (h n) -> p (k h) n", n=N)
            chain.link(nc.vector.reduce_sum(vmean[:], wv4, axis=AX_X))
            chain.link(nc.vector.tensor_scalar(vmean[:], vmean[:], 1.0 / N, None, ALU.mult))
            chain.add(nc.vector.tensor_tensor(wv4, wv4, vmean[:].unsqueeze(2).to_broadcast([P, KT * H, N]), ALU.subtract))
            dve.wait_ge(set_act, 1)
            chain.add(nc.vector.tensor_scalar(lam_ch[:], lam_ch[:], 1.0e30, -1.0, ALU.min, ALU.mult))
            chain.sync()
            nc.vector.tensor_scalar(lam_row[:], lam_row[:], 1.0e30, -1.0, ALU.min, ALU.mult).then_inc(set_dve, 1)
            dve.wait_ge(set_pool, 3)
            for h in range(H):
                ins = nc.vector.scalar_tensor_tensor(dmask[:, h, :], ident[:], u_sb[:, h:h + 1], dmask[:, h, :],
                                                     ALU.mult, ALU.add)
            ins.then_inc(set_dve, 1)
            dve.wait_ge(set_dve, 3)
            chain.reset()

            def ln_stats(src, stats, mv):
                for t in range(TPS):
                    chain.add(nc.vector.bn_stats(stats[:, t, :], src[:, t, :]))
                chain.sync()

            def mixing(s, k):
                s.wait(dve, proj_done[k])
                for c in range(KT):
                    ins = nc.vector.scalar_tensor_tensor(mix[k][:, c, :], diff[:, c, :], maa_sb[:, k, c:c + 1],
                                                         xT[s.const % 2][:, c, 1:], ALU.mult, ALU.add)
                ins.then_inc(mix_ready[k], 1)

            def step(s):
                nxt, front, att, post, send = s + 1, s, s - 1, s - 2, s - 3
                par_f, par_p, par_s = front.const % 2, post.const % 2, send.const % 2

                def mask_scores(g):
                    att.wait(dve, att_done, GPS, g + 1)
                    att.wait(dve, intra_done, GPS, g - 3)
                    q = g % NG
                    nc.vector.tensor_tensor(attm[g % 4][:], pS[g % 2][:], dmask[:, q * HG:(q + 1) * HG, :],
                                            ALU.mult).then_inc(attm_ready, 1)

                def next_state(c):
                    last = c == TPS - 1
                    old, new = state[c], state[(c + 1) % 2]
                    if last and att.const % SPB == SPB - 1:
                        nc.vector.memset(new[:], 0.0).then_inc(state_ready, 1)
                        return
                    att.wait(dve, kv_done, 1, 1)
                    att.wait(dve, state_ready, TPS, c)
                    chain.link(nc.vector.tensor_tensor(kvm[:], p_kv[:, c], blockdiag[:].unsqueeze(1).to_broadcast([P, KT, P]), ALU.mult))
                    for k in range(KT):
                        ins = nc.vector.scalar_tensor_tensor(new[:, k, :], old[:, k, :], sdecay[:, k:k + 1], kvm[:, k, :],
                                                             ALU.mult, ALU.add)
                    ins.then_inc(state_ready, 1)

                a, f, o = att.valid(STEPS), front.valid(STEPS), post.valid(STEPS)
                if a:
                    next_state(0)
                if o:
                    post.wait(dve, wo_done, 1, 1)
                    post.wait(dve, x1_out, 16, -16)
                    xs = post.count(TPS)
                    src = x_sb[:, xs:xs + TPS, :] if post.reg is None else x_sb[:, bass.ds(xs, TPS), :]
                    nc.vector.tensor_tensor(x1[par_p][:], src, pO_tok, ALU.add).then_inc(x1_ready, 1)
                    post.wait(dve, x1_ready, 1, 1)
                    ln_stats(x1[par_p], st2, mv2)
                    for t in range(TPS):
                        ins = nc.vector.bn_aggr(mv2[:, t, :], st2[:, t, :])
                    ins.then_inc(stat2_ready, 1)
                if a:
                    mask_scores(0)
                    mask_scores(1)
                    next_state(1)
                    mask_scores(2)
                if o:
                    post.wait(dve, rstd2_ready, 1, 1)
                    post.wait(dve, stat2_ready, 1, 1)
                    post.wait(dve, sent, 16 * 2 * TPS, -16 * 2 * TPS)
                    post.wait(dve, x2t_done, 1, -1)
                    for t in range(TPS):
                        ins = nc.vector.tensor_scalar(row[par_p][:, t, 0:C], x1[par_p][:, t, :], mv2[:, t, 0:1],
                                                      rstd2[:, t:t + 1], ALU.subtract, ALU.mult)
                    ins.then_inc(xn2_ready, 1)
                if a:
                    mask_scores(3)
                if f:
                    xt = xT[par_f]
                    if front.const % SPB == 0:
                        chain.add(nc.vector.memset(xt[:, :, 0:1], 0.0))
                    else:
                        chain.add(nc.vector.tensor_copy(xt[:, :, 0:1], xT[1 - par_f][:, :, W:W + 1]))
                    front.wait(dve, xT_ready, 1, 1)
                    front.wait(dve, mix_ready[3])
                    chain.sync()
                    nc.vector.tensor_tensor(diff[:], xt[:, :, 0:W], xt[:, :, 1:], ALU.subtract).then_inc(diff_ready, 1)
                if a:
                    mask_scores(4)
                if f:
                    front.wait(dve, diff_ready, 1, 1)
                    mixing(front, 0)
                if a:
                    mask_scores(5)
                if f:
                    mixing(front, 1)
                if a:
                    mask_scores(6)
                if f:
                    mixing(front, 2)
                if a:
                    mask_scores(7)
                if send.valid(STEPS):
                    send.wait(dve, count_done, 1, 1)
                    if send.const % SPB == 0 and not (send.reg is None and send.const == 0):
                        chain.link(nc.vector.tensor_scalar(base[:], base[:], float(CAP), None, ALU.add))
                    chain.add(nc.vector.tensor_scalar(over[:], p_count, float(CAP), DROP, ALU.is_gt, ALU.mult))
                    chain.link(nc.vector.tensor_tensor(slotf[:], p_count, base[:].unsqueeze(1).to_broadcast([P, TPS, E]), ALU.add))
                    chain.link(nc.vector.tensor_tensor(slotf[:], slotf[:], over[:], ALU.add))
                    for k in range(2):
                        chain.add(nc.vector.tensor_tensor(pick[k][:], slotf[:], hot[par_s][k][:], ALU.mult))
                    chain.sync()
                    for k in range(2):
                        chain.add(nc.vector.reduce_sum(slot_k[:, k, :], pick[k][:], axis=AX_X))
                    chain.sync()
                    send.wait(dve, sent, 16 * 2 * TPS)
                    nc.vector.tensor_copy(slot_i[:], slot_k[:]).then_inc(slot_ready, 1)
                if o:
                    post.wait(dve, logit_done, 1, 1)
                    chain.link(nc.vector.reduce_max(lmax[:], p_logit, axis=AX_X))
                    nc.vector.tensor_tensor(lsub[:], p_logit, lmax[:].unsqueeze(2).to_broadcast([P, TPS, E]),
                                            ALU.subtract).then_inc(lsub_ready, 1)
                if a:
                    att.wait(dve, ysq_ready, 1, 1)
                    nc.vector.reduce_sum(ssum[:], ysq[:].rearrange("p t (h n) -> p (t h) n", n=N), axis=AX_X).then_inc(ssum_ready, 1)
                if o:
                    post.wait(dve, lexp_ready, 1, 1)
                    prob = row[par_p][:, :, C:C + E]
                    chain.link(nc.vector.reduce_sum(lsum[:], lexp[:], axis=AX_X))
                    chain.link(nc.vector.reciprocal(lrec[:], lsum[:]))
                    ts = post.count(TPS)
                    src = tok[:, ts:ts + TPS] if post.reg is None else tok[:, bass.ds(ts, TPS)]
                    chain.add(nc.vector.tensor_copy(row[par_p][:, :, ROW - 1].bitcast(I32), src))
                    chain.link(nc.vector.tensor_tensor(prob, lexp[:], lrec[:].unsqueeze(2).to_broadcast([P, TPS, E]), ALU.mult))
                    for t in range(TPS):
                        chain.add(nc.vector.max(top[:, t, :], prob[:, t, :]))
                    chain.sync()
                    for t in range(TPS):
                        chain.add(nc.vector.max_index(topi[:, t, :], top[:, t, :], prob[:, t, :]))
                    chain.sync()
                    chain.link(nc.vector.tensor_copy(topf[:], topi[:, :, 0:2]))
                    for k in range(2):
                        chain.add(nc.vector.tensor_tensor(hot[par_p][k][:], iota_e[:].unsqueeze(1).to_broadcast([P, TPS, E]),
                                                          topf[:, :, k:k + 1].to_broadcast([P, TPS, E]), ALU.is_equal))
                    chain.sync()
                    post.wait(dve, count_done, 1, -1)
                    chain.link(nc.vector.tensor_tensor(took[par_p][:], hot[par_p][0][:], hot[par_p][1][:], ALU.add))
                    nc.vector.tensor_tensor(before[par_p][:, 1, :], before[par_p][:, 0, :], took[par_p][:, 0, :],
                                            ALU.add).then_inc(took_ready, 1)
                    post.wait(dve, count_done)
                    following = before[1 - par_p][:, 0, :]
                    if post.const % SPB == SPB - 1:
                        chain.add(nc.vector.memset(following, 0.0))
                    else:
                        post.wait(dve, took_ready, 1, 1)
                        chain.add(nc.vector.tensor_tensor(following, before[par_p][:, 1, :], took[par_p][:, 1, :], ALU.add))
                if nxt.valid(STEPS):
                    if nxt.reg is None:
                        nxt_b = nxt.const // SPB
                        dve.wait_ge(x_in, 16 * min(B, nxt_b + 1))
                        xa = x_sb[:, nxt.const * TPS:(nxt.const + 1) * TPS, :]
                    else:
                        dve.wait_ge(x_in, 16 * B)
                        xa = x_sb[:, bass.ds(nxt.count(TPS), TPS), :]
                    for t in range(TPS):
                        chain.add(nc.vector.bn_stats(st1[:, t, :], xa[:, t, :]))
                    chain.sync()
                    for t in range(TPS):
                        ins = nc.vector.bn_aggr(mv1[:, t, :], st1[:, t, :])
                    ins.then_inc(stat1_ready, 1)
                if a:
                    att.wait(dve, grstd_ready, 1, 1)
                    att.wait(dve, zt_done)
                    nc.vector.tensor_tensor(yn[:].rearrange("p t (h n) -> p (t h) n", n=N),
                                            pY[:].rearrange("p t (h n) -> p (t h) n", n=N),
                                            grstd[:].unsqueeze(2).to_broadcast([P, TPS * H, N]), ALU.mult).then_inc(yn_ready, 1)
                if f:
                    front.wait(dve, kt_done, 1, 1)
                    front.wait(dve, kv_done)
                    nc.vector.tensor_tensor(k_dec[:].rearrange("p t (h n) -> p t h n", n=N),
                                            pK_tok.rearrange("p t (h n) -> p t h n", n=N),
                                            kdecay[:].unsqueeze(1).unsqueeze(3).to_broadcast([P, TPS, H, N]),
                                            ALU.mult).then_inc(kdec_ready, 1)
                if nxt.valid(STEPS):
                    nxt.wait(dve, rstd1_ready, 1, 1)
                    nxt.wait(dve, stat1_ready, 1, 1)
                    nxt.wait(dve, xt_done)
                    for t in range(TPS):
                        ins = nc.vector.tensor_scalar(xn[:, t, :], xa[:, t, :], mv1[:, t, 0:1], rstd1[:, t:t + 1],
                                                      ALU.subtract, ALU.mult)
                    ins.then_inc(xn_ready, 1)
                chain.reset()

            walk(dve, step)

        @block.tensor
        def _(pe):
            pe.wait_ge(const_in, 16 * NCONST)
            pe.wait_ge(set_pool, 2)
            pe.wait_ge(set_dve, 3)

            def project(s, k, dst, w):
                s.wait(pe, mix_ready[k], 1, 1)
                for m in range(KT):
                    for c in range(KT):
                        ins = nc.tensor.matmul(dst[:, m, :], w[:, c, m * P:(m + 1) * P], mix[k][:, c, :],
                                               start=(c == 0), stop=(c == KT - 1))
                ins.then_inc(proj_done[k], 1)

            def step(s):
                front, att, post, send = s, s - 1, s - 2, s - 3
                if front.valid(STEPS):
                    front.wait(pe, xn_ready, 1, 1)
                    front.wait(pe, z_ready, 1, -1)
                    front.wait(pe, xT_ready)
                    for t in range(TPS):
                        for c in range(KT):
                            ins = nc.tensor.transpose(pX[:, c, t * Q:(t + 1) * Q], xn[:, t, c * P:(c + 1) * P], ident[:])
                    ins.then_inc(xt_done, 1)
                if post.valid(STEPS):
                    post.wait(pe, zg_ready, 1, 1)
                    post.wait(pe, x2T_ready)
                    for t in range(TPS):
                        for c in range(KT):
                            ins = nc.tensor.matmul(pO_tok[:, t, :], zg[:, c, t * Q:(t + 1) * Q], WO[:, c, :],
                                                   start=(c == 0), stop=(c == KT - 1))
                    ins.then_inc(wo_done, 1)
                if send.valid(STEPS):
                    send.wait(pe, took_ready, 1, 1)
                    if front.valid(STEPS + 1):
                        front.wait(pe, kdec_ready)
                    send.wait(pe, lsub_ready, 1, 1)
                    r = send.const % 2
                    cnt = pK[:, TPS * E:2 * TPS * E]
                    nc.tensor.matmul(cnt, tri[:], took[r][:].rearrange("p t e -> p (t e)"), start=True, stop=False)
                    nc.tensor.matmul(cnt, ones[:], before[r][:].rearrange("p t e -> p (t e)"), start=False, stop=True).then_inc(count_done, 1)
                if att.valid(STEPS):
                    att.wait(pe, kdec_ready, 1, 1)
                    att.wait(pe, v_ready, 1, 1)
                    for t in range(TPS):
                        for c in range(KT):
                            ins = nc.tensor.matmul(p_kv[:, t, c, :], k_dec[:, t, c * P:(c + 1) * P], v[:, t, c * P:(c + 1) * P],
                                                   start=True, stop=True)
                    ins.then_inc(kv_done, 1)
                    att.wait(pe, yn_ready)
                    att.wait(pe, rdec_ready, 1, 1)
                    att.wait(pe, kT_ready, 1, 1)
                    att.wait(pe, heads_ready, 16 * HPB, 16 * HPB)

                    def across(t):
                        att.wait(pe, state_ready, TPS, t)
                        for c in range(KT):
                            nc.tensor.matmul(pY[:, t, c * P:(c + 1) * P], r_dec[:, c, t * Q:(t + 1) * Q], state[t][:, c, :],
                                             start=(t == 0 and c == 0), stop=False, skip_group_check=True)

                    def scores(g):
                        t, q = divmod(g, NG)
                        c, h = divmod(q * HG, HPB)
                        att.wait(pe, attm_ready, GPS, g - 1)
                        nc.tensor.matmul(pS[g % 2][:], kT[:, c, t * Q:(t + 1) * Q], r_heads[:, c, h:h + HG, t * Q:(t + 1) * Q],
                                         start=True, stop=True).then_inc(att_done, 1)

                    def within(g):
                        t, q = divmod(g, NG)
                        att.wait(pe, attm_ready, GPS, g + 1)
                        for h in range(HG):
                            col = (q * HG + h) * N
                            ins = nc.tensor.matmul(pY[:, t, col:col + N], attm[g % 4][:, h, :], v[:, t, col:col + N],
                                                   start=False, stop=(g == GPS - 1 and h == HG - 1), skip_group_check=True)
                        ins.then_inc(intra_done, 1)

                    across(0)
                    scores(0)
                    for g in range(1, NG + 1):
                        scores(g)
                        within(g - 1)
                if post.valid(STEPS):
                    post.wait(pe, xn2_ready, 1, 1)
                    for t in range(TPS):
                        for c in range(KT):
                            ins = nc.tensor.transpose(pO_ch[:, c, t * Q:(t + 1) * Q], row[post.const % 2][:, t, c * P:(c + 1) * P], ident[:])
                    ins.then_inc(x2t_done, 1)
                if att.valid(STEPS):
                    across(1)
                    for g in range(NG + 1, GPS):
                        scores(g)
                        within(g - 1)
                    within(GPS - 1)
                if post.valid(STEPS):
                    post.wait(pe, x2T_ready, 1, 1)
                    if send.valid(STEPS):
                        send.wait(pe, slot_ready, 1, 1)
                    for t in range(TPS):
                        for c in range(KT):
                            ins = nc.tensor.matmul(p_logit[:, t, :], x2T[:, c, t * Q:(t + 1) * Q], gate_sb[:, c, :],
                                                   start=(c == 0), stop=(c == KT - 1))
                    ins.then_inc(logit_done, 1)
                if front.valid(STEPS):
                    front.wait(pe, state_ready, TPS)
                    project(front, 0, pA, WR)
                    front.wait(pe, gT_ready)
                    project(front, 1, pB, WK)
                    front.wait(pe, mix_ready[2], 1, 1)
                    front.wait(pe, rT_ready, 1, 1)
                    for t in range(TPS):
                        for c in range(KT):
                            ins = nc.tensor.matmul(pA_tok[:, t, :], mix[2][:, c, t * Q:(t + 1) * Q], WV[:, c, :],
                                                   start=(c == 0), stop=(c == KT - 1))
                    ins.then_inc(proj_done[2], 1)
                    front.wait(pe, kT_ready, 1, 1)
                    project(front, 3, pB, WG)
                    if post.valid(STEPS):
                        post.wait(pe, lsub_ready, 1, 1)
                    for t in range(TPS):
                        for c in range(KT):
                            ins = nc.tensor.transpose(pK_tok[:, t, c * P:(c + 1) * P], kT[:, c, t * Q:(t + 1) * Q], ident[:])
                    ins.then_inc(kt_done, 1)
                if att.valid(STEPS):
                    att.wait(pe, yn_ready, 1, 1)
                    if front.valid(STEPS):
                        front.wait(pe, xT_ready, 1, 1)
                    else:
                        att.wait(pe, z_ready)
                    for t in range(TPS):
                        for c in range(KT):
                            ins = nc.tensor.transpose(pX[:, c, t * Q:(t + 1) * Q], yn[:, t, c * P:(c + 1) * P], ident[:])
                    ins.then_inc(zt_done, 1)

            walk(pe, step)


def phase_b(nc, sb, ps, ctx, sem, ident, whi, wlo, wraw, w1, w2, w3, disp, out):
    CW = max(n for _, n in CHUNKS) * P
    xtok = sb("xtok", [P, ST, ROW])
    xh = sb("xh", [P, KT, SLOTS], F32R)
    xl = sb("xl", [P, KT, SLOTS], F32R)
    weight = [sb(f"weight{k}", [P, ST]) for k in range(2)]
    index = [sb(f"index{k}", [P, ST], I32) for k in range(2)]
    gated = [sb(f"gated{k}", [P, CW]) for k in range(2)]
    hid = [sb(f"hid{k}", [P, CW]) for k in range(2)]
    hh = [sb(f"hh{k}", [P, FT, CW], F32R) for k in range(2)]
    hl = [sb(f"hl{k}", [P, FT, CW], F32R) for k in range(2)]
    NY = 4
    ysb = [sb(f"ysb{k}", [P, C]) for k in range(NY)]

    p1 = [ps(f"p1_{k}", [P, CW]) for k in range(2)]
    p3 = [ps(f"p3_{k}", [P, CW]) for k in range(2)]
    py = [ps(f"py{k}", [P, 512]) for k in range(2)]
    pt = [ps(f"pt{k}", [P, 512]) for k in range(2)]

    rows_in, rows_used = sem("rows_in"), sem("rows_used")
    w_in = [sem(f"w_in{k}") for k in range(2)]
    whi_ready, wlo_ready = sem("whi_ready"), sem("wlo_ready")
    turned, xh_ready, xl_ready = sem("turned"), sem("xh_ready"), sem("xl_ready")
    weight_ready, index_ready = sem("weight_ready"), sem("index_ready")
    h_done, gated_ready, hid_ready = sem("h_done"), sem("gated_ready"), sem("hid_ready")
    hh_ready, hl_ready = sem("hh_ready"), sem("hl_ready")
    ffn_done, ysb_ready = sem("ffn_done"), sem("ysb_ready")
    added = [sem(f"added{k}") for k in range(NY)]

    HPE = NCH * FT
    TB = 2 * NCH - 1
    rows_view = disp.rearrange("(e p t) c -> e p (t c)", e=E, p=P)
    w_view = [w1.rearrange("e (k p) f -> e p k f", p=P), w3.rearrange("e (k p) f -> e p k f", p=P),
              w2.rearrange("e (j p) c -> e p j c", p=P)]

    def row_of(view, e):
        i = e.count()
        return view[i] if e.reg is None else view[bass.ds(i, 1)].squeeze(0)

    def pair(e):
        u = e.const % 2
        return e - u, u

    def walk(step):
        return step

    def run(eng, step):
        for e in range(2):
            step(At(e))
        with eng.Fori(2, E - 3, 2) as e0:
            for u in range(2):
                step(At(u, e0, 2))
        for e in range(E - 2, E):
            step(At(e))

    def banks():
        for c, (t0, n) in enumerate(CHUNKS):
            if n * P * KT <= 512:
                yield c, range(KT), range(t0, t0 + n)
            else:
                for k in range(KT):
                    yield c, range(k, k + 1), range(t0, t0 + n)

    BANKS = list(banks())
    assert len(BANKS) == TB
    LAST_BANK = [max(i for i, b in enumerate(BANKS) if b[0] == c) for c in range(NCH)]

    def bank_of(i, n):
        _, ks, ts = BANKS[i]
        w = len(ts) * P
        src = pt[n % 2][:, 0:len(ks) * w].rearrange("p (k s) -> p k s", k=len(ks))
        cut = (slice(None), slice(ks[0], ks[-1] + 1), slice(ts[0] * P, ts[0] * P + w))
        return src, cut

    def added_before(eng, e, more):
        even, u = pair(e)
        for r in range(NY):
            n = len(range(r, ST * u + more, NY))
            even.wait(eng, added[r], 16 * ST // NY, 16 * n)

    with nc.Block() as block:

        @block.sync
        def _(sp):
            def load_rows(e):
                e.wait(sp, turned, TB)
                e.wait(sp, rows_used, 2)
                sp.dma_start(xtok[:].rearrange("p t c -> p (t c)"), row_of(rows_view, e)).then_inc(rows_in, 16)

            def load_weights(e, m):
                even, u = pair(e)
                k = (3 * u + m) % 2
                e.wait(sp, whi_ready, 3, m - 1)
                e.wait(sp, wlo_ready, 3, m - 1)
                dst = wraw[k][:].rearrange("p (k f) -> p k f", k=KT if m < 2 else FT)
                sp.dma_start(dst, row_of(w_view[m], e)).then_inc(w_in[k], 16)

            load_rows(At(0))
            for m in range(3):
                load_weights(At(0), m)

            def step(e):
                nxt = e + 1
                if nxt.valid(E):
                    load_rows(nxt)
                    for m in range(3):
                        load_weights(nxt, m)

            run(sp, step)

        @block.gpsimd
        def _(pool):
            def keep_index(e):
                e.wait(pool, rows_in, 16, 16)
                pool.wait_ge(rows_in, 16)
                nc.gpsimd.tensor_copy(index[e.const % 2][:], xtok[:, :, ROW - 1].bitcast(I32)).then_inc(index_ready, 1)
                e.wait(pool, index_ready, 1, 1)
                pool.sem_inc(rows_used, 1)

            keep_index(At(0))

            def step(e):
                added_before(pool, e, 0)
                even, u = pair(e)
                for t in range(ST):
                    j = ST * u + t
                    e.wait(pool, ysb_ready, ST, t + 1)
                    pool.wait_ge(rows_in, 16)
                    nc.gpsimd.indirect_dma_start(
                        out, bass.IndirectOffsetOnAxis(ap=index[e.const % 2][:, t:t + 1], axis=0),
                        ysb[j % NY][:], None, compute_op=ALU.add).then_inc(added[j % NY], 16)
                    if t == ST - 3 and (e + 1).valid(E):
                        keep_index(e + 1)

            run(pool, step)
            added_before(pool, At(E), 0)

        @block.scalar
        def _(act):
            def split_hi(e, m):
                even, u = pair(e)
                even.wait(act, w_in[(3 * u + m) % 2], 24, 16 * ((3 * u + m) // 2 + 1))
                if m < 2:
                    e.wait(act, h_done, HPE, -HPE)
                else:
                    e.wait(act, ffn_done, ST, -ST)
                nc.scalar.copy(whi[e.const % 2][m][:], wraw[(3 * u + m) % 2][:]).then_inc(whi_ready, 1)

            def turn_hi(e, i):
                u = e.const % 2
                src, cut = bank_of(i, TB * u + i)
                e.wait(act, turned, TB, i + 1)
                nc.scalar.copy(xh[cut], src).then_inc(xh_ready, 1)

            def gate(e, c, f):
                k = (pair(e)[1] * HPE + c * FT + f) % 2
                w = CHUNKS[c][1] * P
                e.wait(act, h_done, HPE, c * FT + f + 1)
                e.wait(act, hid_ready, HPE, c * FT + f - 1)
                nc.scalar.activation(gated[k][:, 0:w], p1[k][:, 0:w], ACT.Silu).then_inc(gated_ready, 1)

            def hidden_hi(e, c, f):
                u = pair(e)[1]
                k = (u * HPE + c * FT + f) % 2
                w = CHUNKS[c][1] * P
                e.wait(act, hid_ready, HPE, c * FT + f + 1)
                if f == 0:
                    free_hidden(act, e, c)
                nc.scalar.copy(hh[(u * NCH + c) % 2][:, f, 0:w], hid[k][:, 0:w]).then_inc(hh_ready, 1)

            def scale_out(e, t):
                j = ST * pair(e)[1] + t
                even, u = pair(e)
                e.wait(act, ffn_done, ST, t + 1)
                e.wait(act, weight_ready, 1, 1)
                if e.reg is not None or ST * e.const + t >= NY:
                    even.wait(act, added[j % NY], 16 * ST // NY, 16 * (j // NY))
                nc.scalar.activation(ysb[j % NY][:], py[j % 2][:, 0:C], ACT.Copy, scale=weight[e.const % 2][:, t:t + 1]).then_inc(ysb_ready, 1)

            def hidden(e, c):
                for f in range(FT):
                    gate(e, c, f)
                    if f:
                        hidden_hi(e, c, f - 1)
                hidden_hi(e, c, FT - 1)

            def scale_chunk(e, c):
                t0, n = CHUNKS[c]
                for t in range(t0, t0 + n):
                    scale_out(e, t)

            for m in range(2):
                split_hi(At(0), m)
            for i in range(TB):
                turn_hi(At(0), i)
            split_hi(At(0), 2)

            def step(e):
                nxt = e + 1
                more = nxt.valid(E)
                hidden(e, 0)
                if more:
                    split_hi(nxt, 0)
                hidden(e, 1)
                scale_chunk(e, 0)
                if more:
                    split_hi(nxt, 1)
                hidden(e, 2)
                scale_chunk(e, 1)
                if more:
                    split_hi(nxt, 2)
                t0, n = CHUNKS[2]
                todo = list(range(TB)) if more else []
                for t in range(t0, t0 + n):
                    for i in todo[:2]:
                        turn_hi(nxt, i)
                    todo = todo[2:]
                    scale_out(e, t)
                for i in todo:
                    turn_hi(nxt, i)

            def free_hidden(eng, e, c):
                n = c - 2 if c >= 2 else c - 2 + NCH
                past = e if c >= 2 else e - 1
                t0, cnt = CHUNKS[n]
                past.wait(eng, ffn_done, ST, t0 + cnt)

            run(act, step)

        @block.vector
        def _(dve):
            def split_lo(e, m):
                u = pair(e)[1]
                k = (3 * u + m) % 2
                e.wait(dve, whi_ready, 3, m + 1)
                nc.vector.tensor_tensor(wlo[e.const % 2][m][:], wraw[k][:], whi[e.const % 2][m][:].bitcast(F32),
                                        ALU.subtract).then_inc(wlo_ready, 1)

            def turn_lo(e, i):
                src, cut = bank_of(i, TB * (e.const % 2) + i)
                e.wait(dve, xh_ready, TB, i + 1)
                nc.vector.tensor_tensor(xl[cut], src, xh[cut].bitcast(F32), ALU.subtract).then_inc(xl_ready, 1)

            def keep_weight(e):
                e.wait(dve, rows_in, 16, 16)
                e.wait(dve, ysb_ready, ST, -ST)
                col = e.count(1, C)
                src = xtok[:, :, col] if e.reg is None else xtok[:, :, bass.ds(col, 1)].squeeze(2)
                nc.vector.tensor_scalar(weight[e.const % 2][:], src, 1.0, None, ALU.mult).then_inc(weight_ready, 1)
                e.wait(dve, weight_ready, 1, 1)
                dve.sem_inc(rows_used, 1)

            def hidden_value(e, c, f):
                k = (pair(e)[1] * HPE + c * FT + f) % 2
                w = CHUNKS[c][1] * P
                e.wait(dve, gated_ready, HPE, c * FT + f + 1)
                e.wait(dve, hl_ready, HPE, c * FT + f - 1)
                nc.vector.tensor_tensor(hid[k][:, 0:w], gated[k][:, 0:w], p3[k][:, 0:w], ALU.mult).then_inc(hid_ready, 1)

            def hidden_lo(e, c, f):
                u = pair(e)[1]
                k = (u * HPE + c * FT + f) % 2
                w = CHUNKS[c][1] * P
                e.wait(dve, hh_ready, HPE, c * FT + f + 1)
                s = (u * NCH + c) % 2
                nc.vector.tensor_tensor(hl[s][:, f, 0:w], hid[k][:, 0:w], hh[s][:, f, 0:w].bitcast(F32),
                                        ALU.subtract).then_inc(hl_ready, 1)

            def hidden(e, c):
                for f in range(FT):
                    hidden_value(e, c, f)
                    if f:
                        hidden_lo(e, c, f - 1)
                hidden_lo(e, c, FT - 1)

            for m in range(2):
                split_lo(At(0), m)
            for i in range(TB):
                turn_lo(At(0), i)
            keep_weight(At(0))
            split_lo(At(0), 2)

            def step(e):
                nxt = e + 1
                more = nxt.valid(E)
                for c in range(NCH):
                    hidden(e, c)
                    if more:
                        split_lo(nxt, c)
                if more:
                    for i in range(TB):
                        turn_lo(nxt, i)
                    keep_weight(nxt)

            run(dve, step)

        @block.tensor
        def _(pe):
            def turn(e, i):
                n = TB * (e.const % 2) + i
                _, ks, ts = BANKS[i]
                e.wait(pe, rows_in, 16, 16)
                e.wait(pe, xl_ready, TB, i - 1)
                src, _ = bank_of(i, n)
                for a, k in enumerate(ks):
                    for b, t in enumerate(ts):
                        ins = nc.tensor.transpose(src[:, a, b * P:(b + 1) * P], xtok[:, t, k * P:(k + 1) * P], ident[:])
                ins.then_inc(turned, 1)

            def up(e, c):
                u = pair(e)[1]
                t0, n = CHUNKS[c]
                w = n * P
                e.wait(pe, xl_ready, TB, LAST_BANK[c] + 1)
                e.wait(pe, wlo_ready, 3, 2)
                hi, lo = whi[e.const % 2], wlo[e.const % 2]
                for f in range(FT):
                    k = (u * HPE + c * FT + f) % 2
                    e.wait(pe, hid_ready, HPE, c * FT + f - 1)
                    for m, dst in ((0, p1[k]), (1, p3[k])):
                        for kt in range(KT):
                            wcut = slice(kt * F + f * P, kt * F + (f + 1) * P)
                            xcut = (slice(None), kt, slice(t0 * P, t0 * P + w))
                            nc.tensor.matmul(dst[:, 0:w], hi[m][:, wcut], xh[xcut], start=(kt == 0), stop=False)
                            nc.tensor.matmul(dst[:, 0:w], hi[m][:, wcut], xl[xcut], start=False, stop=False)
                            ins = nc.tensor.matmul(dst[:, 0:w], lo[m][:, wcut], xh[xcut], start=False, stop=(kt == KT - 1))
                    ins.then_inc(h_done, 1)

            def down(e, t):
                u = pair(e)[1]
                c = next(i for i, (t0, n) in enumerate(CHUNKS) if t0 <= t < t0 + n)
                s = (u * NCH + c) % 2
                j = ST * u + t
                e.wait(pe, hl_ready, HPE, FT * (c + 1))
                e.wait(pe, wlo_ready, 3, 3)
                e.wait(pe, ysb_ready, ST, t - 1)
                off = (t - CHUNKS[c][0]) * P
                hi, lo = whi[e.const % 2][2], wlo[e.const % 2][2]
                for f in range(FT):
                    a, b = hh[s][:, f, off:off + P], hl[s][:, f, off:off + P]
                    cut = slice(f * C, (f + 1) * C)
                    nc.tensor.matmul(py[j % 2][:, 0:C], a, hi[:, cut], start=(f == 0), stop=False)
                    nc.tensor.matmul(py[j % 2][:, 0:C], a, lo[:, cut], start=False, stop=False)
                    ins = nc.tensor.matmul(py[j % 2][:, 0:C], b, hi[:, cut], start=False, stop=(f == FT - 1))
                ins.then_inc(ffn_done, 1)

            def down_chunk(e, c):
                t0, n = CHUNKS[c]
                for t in range(t0, t0 + n):
                    down(e, t)

            for i in range(TB):
                turn(At(0), i)

            def step(e):
                nxt = e + 1
                up(e, 0)
                up(e, 1)
                down_chunk(e, 0)
                up(e, 2)
                down_chunk(e, 1)
                t0, n = CHUNKS[2]
                todo = list(range(TB)) if nxt.valid(E) else []
                for t in range(t0, t0 + n):
                    for i in todo[:2]:
                        turn(nxt, i)
                    todo = todo[2:]
                    down(e, t)
                for i in todo:
                    turn(nxt, i)

            run(pe, step)


def kernel(**inputs):
    import concourse.bacc as bacc
    from concourse.bass_utils import run_bass_kernel_spmd

    a = {k: np.asarray(v) for k, v in inputs.items()}

    def by_channel(v):
        return v.reshape(KT, P).T

    att = "L0_attn_"
    arrays = {
        "x": a[att + "x"].reshape(NTOK, C),
        "maa": np.stack([by_channel(a[att + "time_maa_" + k]) for k in "rkvg"], axis=1),
        "decay_row": np.broadcast_to(a[att + "time_decay"].reshape(1, H), (P, H)),
        "decay_ch": by_channel(np.repeat(a[att + "time_decay"].reshape(H), N)),
        "u_row": np.broadcast_to(a[att + "time_faaaa"].reshape(1, H), (P, H)),
        "wrT": a[att + "Wr"].T, "wkT": a[att + "Wk"].T, "wvT": a[att + "Wv"].T,
        "wgT": a[att + "Wg"].T, "woT": a[att + "Wo"].T,
        "lnw": by_channel(a[att + "ln_w"]), "lnb": by_channel(a[att + "ln_b"]),
        "gateT": a["L0_ffn_gate_w"].T,
        "w1": a["L0_ffn_w1"], "w2": a["L0_ffn_w2"], "w3": a["L0_ffn_w3"],
    }
    arrays = {f"in_{k}": np.ascontiguousarray(v) for k, v in arrays.items()}
    nc = bacc.Bacc("TRN2", target_bir_lowering=False, num_devices=1)
    args = [nc.dram_tensor(k, v.shape, mybir.dt.from_np(v.dtype), kind="ExternalInput").ap() for k, v in arrays.items()]
    args.append(nc.dram_tensor("out", [NTOK + SLOTS, C], F32, kind="ExternalOutput").ap())
    build(nc, *args)
    r = run_bass_kernel_spmd(nc, [arrays], core_ids=[0])
    return r.results[0]["out"][:NTOK].reshape(B, T, C)
```

```python
from contextlib import ExitStack

import numpy as np

import concourse.bass as bass
from concourse import mybir

F32 = mybir.dt.float32
F32R = mybir.dt.float32r
I32 = mybir.dt.int32
U32 = mybir.dt.uint32
ALU = mybir.AluOpType
ACT = mybir.ActivationFunctionType
AX_X = mybir.AxisListType.X

P = 128
B, T, C = 4, 1024, 256
NTOK = B * T
H = 16
N = C // H
KT = C // P
Q = P
TPS = 2
W = TPS * Q
STEPS = NTOK // W
SPB = T // W
HG = 4
NG = H // HG
GPS = TPS * NG
HPB = H // KT
LN_EPS = 1e-5
GN_EPS = 1e-5 * 64
E = 8
F = 896
FT = F // P
CAP = T * 2 // E * 5 // 4
SLOTS = B * CAP
ST = SLOTS // P
ROW = C + E + 1
DROP = 1.0e6
CHUNKS = [(0, 4), (4, 4), (8, 2)]
NCH = len(CHUNKS)


class At:

    alone = {}

    def __init__(self, const, reg=None, least=0):
        self.const, self.reg, self.least = const, reg, least

    def __sub__(self, k):
        return At(self.const - k, self.reg, self.least)

    def __add__(self, k):
        return At(self.const + k, self.reg, self.least)

    def count(self, per=1, more=0):
        v = per * self.const + more
        return v if self.reg is None else self.reg * per + v

    def wait(self, eng, sem, per=1, more=0):
        v = self.count(per, more)
        if self.reg is None:
            if v > 0:
                eng.wait_ge(sem, v)
        else:
            assert per * (self.least + self.const) + more > 0
            eng.wait_ge(sem, v)
            if eng in At.alone:
                eng.sem_inc(At.alone[eng], 1)

    def valid(self, n):
        return self.reg is not None or 0 <= self.const < n


class Chain:

    def __init__(self, eng, sem):
        self.eng, self.sem, self.n = eng, sem, 0

    def add(self, ins):
        self.n += 1
        ins.then_inc(self.sem, 1)

    def sync(self):
        self.eng.wait_ge(self.sem, self.n)

    def link(self, ins):
        self.add(ins)
        self.sync()

    def reset(self):
        if self.n:
            self.sync()
            self.eng.sem_inc(self.sem, -self.n)
            self.n = 0


def build(nc, x, maa, decay_row, decay_ch, u_row, wrT, wkT, wvT, wgT, woT, lnw, lnb, gateT, w1, w2, w3, out):
    disp = nc.dram_tensor("disp", [E * SLOTS, ROW], F32).ap()
    persist = ExitStack()
    with persist:
        def tensors(ctx):
            def sb(name, shape, dt=F32):
                return ctx.enter_context(nc.sbuf_tensor(name, shape, dt))

            def ps(name, shape):
                return ctx.enter_context(nc.psum_tensor(name, shape, F32))

            return sb, ps

        sems = {}

        def sem(name):
            if name not in sems:
                sems[name] = persist.enter_context(nc.semaphore(name))
            return sems[name]

        At.alone = {nc.sync: sem("sp_waited"), nc.gpsimd: sem("pool_waited")}
        sb, _ = tensors(persist)
        NW = KT * F
        whi = [[sb(f"whi0_{m}", [P, NW], F32R) for m in range(3)]]
        wlo = [[sb(f"wlo0_{m}", [P, NW], F32R) for m in range(3)]]
        wraw = [sb(f"wraw{k}", [P, NW]) for k in range(2)]
        ident = sb("ident", [P, P])
        with ExitStack() as ctx:
            phase_a(nc, *tensors(ctx), ctx, sem, ident, x, maa, decay_row, decay_ch, u_row,
                    (wrT, wkT, wvT, wgT, woT), lnw, lnb, gateT, disp, out)
        with ExitStack() as ctx:
            sb2, ps2 = tensors(ctx)
            whi.append([sb2(f"whi1_{m}", [P, NW], F32R) for m in range(3)])
            wlo.append([sb2(f"wlo1_{m}", [P, NW], F32R) for m in range(3)])
            phase_b(nc, sb2, ps2, ctx, sem, ident, whi, wlo, wraw, w1, w2, w3, disp, out)


def phase_a(nc, sb, ps, ctx, sem, ident, x, maa, decay_row, decay_ch, u_row, weights, lnw, lnb, gateT, disp, out):
    x_sb = sb("x_sb", [P, (STEPS + 1) * TPS, C])
    w_sb = [sb(f"w_sb{k}", [P, KT, C]) for k in range(5)]
    WR, WK, WV, WG, WO = w_sb
    gate_sb = sb("gate_sb", [P, KT, E])
    maa_sb = sb("maa_sb", [P, 4, KT])
    lnw_sb = sb("lnw_sb", [P, KT])
    lnb_sb = sb("lnb_sb", [P, KT])
    lam_row = sb("lam_row", [P, H])
    lam_ch = sb("lam_ch", [P, KT])
    u_sb = sb("u_sb", [P, H])
    vmean = sb("vmean", [P, KT * H])
    dmask = sb("dmask", [P, H, Q])
    kdecay = sb("kdecay", [P, H])
    rdecay = sb("rdecay", [P, KT, Q])
    sdecay = sb("sdecay", [P, KT])
    blockdiag = sb("blockdiag", [P, P])
    tri = sb("tri", [P, P])
    ones = sb("ones", [P, P])
    lag_i = sb("lag_i", [P, Q], I32)
    empty_i = sb("empty_i", [P, ST], I32)
    lag = sb("lag", [P, Q])
    col_i = sb("col_i", [P, Q], I32)
    colf = sb("colf", [P, Q])
    rest_i = sb("rest_i", [P, 1], I32)
    rest = sb("rest", [P, 1])
    iota_i = sb("iota_i", [P, E], I32)
    iota_e = sb("iota_e", [P, E])
    base_i = sb("base_i", [P, E], I32)
    base = sb("base", [P, E])
    tok = sb("tok", [P, NTOK // P], I32)
    mhalf = sb("mhalf", [P, TPS])
    gn_eps = sb("gn_eps", [P, 1])
    empty = sb("empty", [P, ST, ROW])

    mv1 = sb("mv1", [P, TPS, 2])
    st1 = sb("st1", [P, TPS, 6])
    var1 = sb("var1", [P, TPS])
    rstd1 = sb("rstd1", [P, TPS])
    xn = sb("xn", [P, TPS, C])
    xT = [sb(f"xT{k}", [P, KT, W + 1]) for k in range(2)]
    diff = sb("diff", [P, KT, W])
    mix = [sb(f"mix{k}", [P, KT, W]) for k in range(4)]
    rT = sb("rT", [P, KT, W])
    r_heads = sb("r_heads", [P, KT, HPB, W])
    r_dec = sb("r_dec", [P, KT, W])
    kT = sb("kT", [P, KT, W])
    k_dec = sb("k_dec", [P, TPS, C])
    v_pad = sb("v_pad", [P, TPS, H // 2, 4, N])
    gT = [sb(f"gT{k}", [P, KT, W]) for k in range(2)]
    attm = [sb(f"attm{k}", [P, HG, Q]) for k in range(4)]
    state = [sb(f"state{k}", [P, KT, P]) for k in range(2)]
    kvm = sb("kvm", [P, KT, P])
    ysq = sb("ysq", [P, KT, W])
    yn = sb("yn", [P, KT, W])
    z = sb("z", [P, KT, W])
    zg = sb("zg", [P, KT, W])
    x1 = [sb(f"x1_{k}", [P, TPS, C]) for k in range(2)]
    st2 = sb("st2", [P, TPS, 6])
    mv2 = sb("mv2", [P, TPS, 2])
    var2 = sb("var2", [P, TPS])
    rstd2 = sb("rstd2", [P, TPS])
    row = [sb(f"row{k}", [P, TPS, ROW]) for k in range(2)]
    x2T = sb("x2T", [P, KT, W])
    lmax = sb("lmax", [P, TPS])
    lsub = sb("lsub", [P, TPS, E])
    lexp = sb("lexp", [P, TPS, E])
    lsum = sb("lsum", [P, TPS])
    lrec = sb("lrec", [P, TPS])
    top = sb("top", [P, TPS, 8])
    topi = sb("topi", [P, TPS, 8], U32)
    topf = sb("topf", [P, TPS, 2])
    hot = [[sb(f"hot{k}_{r}", [P, TPS, E]) for k in range(2)] for r in range(2)]
    took = [sb(f"took{r}", [P, TPS, E]) for r in range(2)]
    before = [sb(f"before{r}", [P, TPS, E]) for r in range(2)]
    over = sb("over", [P, TPS, E])
    slotf = sb("slotf", [P, TPS, E])
    pick = [sb(f"pick{k}", [P, TPS, E]) for k in range(2)]
    slot_k = sb("slot_k", [P, 2, TPS])
    slot_i = sb("slot_i", [P, 2, TPS], I32)
    mixt = sb("mixt", [P, KT, W])

    pX = ps("pX", [P, KT, W])
    pO = ps("pO", [P, 512])
    pK = ps("pK", [P, 512])
    pA = ps("pA", [P, KT, W])
    pB = ps("pB", [P, KT, W])
    pS = [ps(f"pS{k}", [P, HG, Q]) for k in range(2)]
    pY = ps("pY", [P, KT, W])

    pO_tok = pO[:, :].rearrange("p (t c) -> p t c", t=TPS)
    pO_ch = pO[:, :].rearrange("p (k w) -> p k w", k=KT)
    pK_tok = pK[:, :].rearrange("p (t c) -> p t c", t=TPS)
    p_logit = pS[1][:, 0, 0:TPS * E].rearrange("p (t e) -> p t e", t=TPS)
    p_count = pS[0][:, 0, 0:TPS * E].rearrange("p (t e) -> p t e", t=TPS)
    pA_tok = pA[:, :, :].rearrange("p a b -> p (a b)").rearrange("p (t c) -> p t c", t=TPS)
    p_kv = pA[:, :, :].rearrange("p a b -> p (a b)").rearrange("p (t k c) -> p t k c", t=TPS, k=KT)

    x_in = sem("x_in")
    const_in, decay_in = sem("const_in"), sem("decay_in")
    set_dve, set_pool, set_act = sem("set_dve"), sem("set_pool"), sem("set_act")
    empty_out = sem("empty_out")
    stat1_ready, rstd1_ready, xn_ready = sem("stat1_ready"), sem("rstd1_ready"), sem("xn_ready")
    xt_done, xT_ready = sem("xt_done"), sem("xT_ready")
    diff_ready = sem("diff_ready")
    mix_ready = [sem(f"mix_ready{k}") for k in range(4)]
    proj_done = [sem(f"proj_done{k}") for k in range(4)]
    rT_ready, kT_ready, v_ready, gT_ready = sem("rT_ready"), sem("kT_ready"), sem("v_ready"), sem("gT_ready")
    heads_ready, rdec_ready = sem("heads_ready"), sem("rdec_ready")
    kt_done, kdec_ready, kv_done, state_ready = sem("kt_done"), sem("kdec_ready"), sem("kv_done"), sem("state_ready")
    att_done, attm_ready, intra_done = sem("att_done"), sem("attm_ready"), sem("intra_done")
    ysq_ready, ssum_done, gstd_ready, yn_ready = sem("ysq_ready"), sem("ssum_done"), sem("gstd_ready"), sem("yn_ready")
    z_ready, zg_ready, wo_done = sem("z_ready"), sem("zg_ready"), sem("wo_done")
    x1_ready, x1_out, stat2_ready, rstd2_ready = sem("x1_ready"), sem("x1_out"), sem("stat2_ready"), sem("rstd2_ready")
    xn2_ready, x2t_done, x2T_ready = sem("xn2_ready"), sem("x2t_done"), sem("x2T_ready")
    logit_done, lsub_ready, lexp_ready, took_ready = sem("logit_done"), sem("lsub_ready"), sem("lexp_ready"), sem("took_ready")
    count_done, slot_ready, sent = sem("count_done"), sem("slot_ready"), sem("sent")
    dve_chain, pool_chain = sem("dve_chain"), sem("pool_chain")

    NCONST = 5 + 5
    x_view = x.rearrange("(b t p) c -> b p t c", b=B, p=P)
    out_view = out[0:NTOK, :].rearrange("(s t p) c -> s p t c", t=TPS, p=P)

    def walk(eng, step, before={}):
        for s in range(-1, SPB):
            if s in before:
                before[s]()
            step(At(s))
        with eng.Fori(SPB, STEPS - SPB + 1, SPB) as s0:
            for j in range(SPB):
                step(At(j, s0, SPB))
        for s in range(STEPS, STEPS + 3):
            step(At(s))

    with nc.Block() as block:

        @block.sync
        def _(sp):
            sp.dma_start(x_sb[:, 0:TPS, :], x_view[0][:, 0:TPS, :]).then_inc(x_in, 16)
            sp.dma_start(maa_sb[:], maa).then_inc(const_in, 16)
            for k in range(5):
                sp.dma_start(w_sb[k][:], weights[k].rearrange("(k p) c -> p k c", p=P)).then_inc(const_in, 16)
            for dst, src in ((gate_sb, gateT.rearrange("(k p) e -> p k e", p=P)), (lnw_sb, lnw), (lnb_sb, lnb), (u_sb, u_row)):
                sp.dma_start(dst[:], src).then_inc(const_in, 16)
            sp.wait_ge(x_in, 16)
            sp.dma_start(x_sb[:, TPS:T // P, :], x_view[0][:, TPS:, :]).then_inc(x_in, 16)
            for b in range(1, B):
                sp.wait_ge(x_in, 16 * (b + 1))
                sp.dma_start(x_sb[:, b * T // P:(b + 1) * T // P, :], x_view[b]).then_inc(x_in, 16)

            def clear_table():
                sp.wait_ge(set_pool, 3)
                for e in range(E):
                    sp.dma_start(disp[e * SLOTS:(e + 1) * SLOTS, :].rearrange("(p t) c -> p (t c)", p=P),
                                 empty[:, :, :].rearrange("p t c -> p (t c)")).then_inc(empty_out, 16)

            def step(s):
                front, post = s, s - 2
                if post.valid(STEPS):
                    post.wait(sp, x1_ready, 1, 1)
                    post.wait(sp, x1_out, 16)
                    q = post.count()
                    dst = out_view[q] if post.reg is None else out_view[bass.ds(q, 1)].rearrange("o p t c -> p (o t) c")
                    sp.dma_start(dst, x1[post.const % 2][:]).then_inc(x1_out, 16)
                if front.valid(STEPS):
                    front.wait(sp, rT_ready, 1, 1)
                    front.wait(sp, att_done, GPS)
                    if front.const == 0 and front.reg is None:
                        sp.wait_ge(set_dve, 1)
                    for h in range(HPB):
                        sp.dma_start(r_heads[h * N:(h + 1) * N, :, h, :], rT[h * N:(h + 1) * N, :, :]).then_inc(heads_ready, 16)

            walk(sp, step, {1: clear_table})
            sp.wait_ge(x1_out, 16 * STEPS)

        @block.gpsimd
        def _(pool):
            chain = Chain(pool, pool_chain)
            chain.add(nc.gpsimd.memset(ones[:], 1.0))
            chain.add(nc.gpsimd.memset(mhalf[:], -0.5))
            chain.add(nc.gpsimd.iota(lag_i[:], pattern=[[1, Q]], base=-1, channel_multiplier=-1))
            chain.add(nc.gpsimd.iota(col_i[:], pattern=[[1, Q]], base=0, channel_multiplier=0))
            chain.link(nc.gpsimd.iota(rest_i[:], pattern=[[0, 1]], base=Q - 1, channel_multiplier=-1))
            nc.gpsimd.affine_select(out=ident[:], in_=ones[:], compare_op=ALU.is_equal, fill=0.0,
                                    base=0, pattern=[[1, P]], channel_multiplier=-1).then_inc(set_pool, 1)

            def tables():
                chain.add(nc.gpsimd.memset(blockdiag[:], 1.0))
                chain.add(nc.gpsimd.memset(gn_eps[:], GN_EPS))
                chain.add(nc.gpsimd.iota(iota_i[:], pattern=[[1, E]], base=0, channel_multiplier=0))
                chain.add(nc.gpsimd.iota(base_i[:], pattern=[[SLOTS, E]], base=-1, channel_multiplier=0))
                chain.add(nc.gpsimd.iota(empty_i[:], pattern=[[1, ST]], base=NTOK, channel_multiplier=ST))
                chain.add(nc.gpsimd.iota(tok[:], pattern=[[P, NTOK // P]], base=0, channel_multiplier=1))
                chain.add(nc.gpsimd.affine_select(out=tri[:], in_=ones[:], compare_op=ALU.is_ge, fill=0.0,
                                                  base=0, pattern=[[1, P]], channel_multiplier=-1))
                chain.sync()
                bd = blockdiag[:].rearrange("p (g n) -> p g n", n=N)
                chain.link(nc.gpsimd.affine_select(out=bd, in_=bd, compare_op=ALU.is_ge, fill=0.0,
                                                   base=0, pattern=[[-N, P // N], [0, N]], channel_multiplier=1))
                chain.link(nc.gpsimd.affine_select(out=bd, in_=bd, compare_op=ALU.is_ge, fill=0.0,
                                                   base=N - 1, pattern=[[N, P // N], [0, N]], channel_multiplier=-1))
                chain.reset()
                pool.wait_ge(set_act, 2)
                nc.gpsimd.affine_select(out=dmask[:], in_=dmask[:], compare_op=ALU.is_gt, fill=0.0,
                                        base=0, pattern=[[0, H], [1, Q]], channel_multiplier=-1).then_inc(set_pool, 1)

            def empty_rows():
                chain.link(nc.gpsimd.memset(empty[:], 0.0))
                chain.add(nc.gpsimd.tensor_copy(empty[:, :, ROW - 1].bitcast(I32), empty_i[:]))
                chain.link(nc.gpsimd.memset(x_sb[:, STEPS * TPS:, :], 0.0))
                chain.reset()
                nc.gpsimd.engine_nop().then_inc(set_pool, 1)

            def step(s):
                nxt, front, post, send = s + 1, s, s - 2, s - 3
                if post.valid(STEPS):
                    post.wait(pool, wo_done)
                    post.wait(pool, z_ready, 1, 1)
                    nc.gpsimd.tensor_tensor(zg[:], z[:], gT[post.const % 2][:], ALU.mult).then_inc(zg_ready, 1)
                if nxt.valid(STEPS):
                    nxt.wait(pool, stat1_ready, 1, 1)
                    pool.wait_ge(set_pool, 1)
                    chain.link(nc.gpsimd.tensor_scalar(var1[:], mv1[:, :, 1], LN_EPS, None, ALU.add))
                    nc.gpsimd.tensor_tensor(rstd1[:], var1[:], mhalf[:, 0:TPS], ALU.pow).then_inc(rstd1_ready, 1)
                if front.valid(STEPS):
                    g = 3
                    front.wait(pool, diff_ready, 1, 1)
                    front.wait(pool, proj_done[g])
                    pool.wait_ge(set_pool, 1)
                    for k in range(KT):
                        chain.add(nc.gpsimd.tensor_scalar(mixt[:, k, :], diff[:, k, :], maa_sb[:, g, k:k + 1], None, ALU.mult))
                    chain.sync()
                    nc.gpsimd.tensor_tensor(mix[g][:], mixt[:], xT[front.const % 2][:, :, 1:], ALU.add).then_inc(mix_ready[g], 1)
                if post.valid(STEPS):
                    post.wait(pool, stat2_ready, 1, 1)
                    pool.wait_ge(set_pool, 1)
                    chain.link(nc.gpsimd.tensor_scalar(var2[:], mv2[:, :, 1], LN_EPS, None, ALU.add))
                    nc.gpsimd.tensor_tensor(rstd2[:], var2[:], mhalf[:, 0:TPS], ALU.pow).then_inc(rstd2_ready, 1)
                if front.valid(STEPS):
                    front.wait(pool, intra_done, GPS)
                    front.wait(pool, rT_ready, 1, 1)
                    nc.gpsimd.tensor_tensor(
                        r_dec[:].rearrange("p k (t i) -> p k t i", i=Q), rT[:].rearrange("p k (t i) -> p k t i", i=Q),
                        rdecay[:].unsqueeze(2).to_broadcast([P, KT, TPS, Q]), ALU.mult).then_inc(rdec_ready, 1)
                if send.valid(STEPS):
                    send.wait(pool, slot_ready, 1, 1)
                    if send.reg is None and send.const == 0:
                        pool.wait_ge(empty_out, 16 * E)
                    pool.wait_ge(set_pool, 1)
                    for k in range(2):
                        for t in range(TPS):
                            nc.gpsimd.indirect_dma_start(
                                disp, bass.IndirectOffsetOnAxis(ap=slot_i[:, k, t:t + 1], axis=0),
                                row[send.const % 2][:, t, :], None,
                                bounds_check=E * SLOTS - 1, oob_is_err=False).then_inc(sent, 16)
                chain.reset()

            walk(pool, step, {0: tables, 1: empty_rows})
            pool.wait_ge(sent, 16 * 2 * TPS * STEPS)

        @block.scalar
        def _(act):
            for dst, src in ((lam_row, decay_row), (lam_ch, decay_ch)):
                nc.scalar.dma_start(dst[:], src).then_inc(decay_in, 16)
            act.wait_ge(decay_in, 32)
            nc.scalar.activation(lam_row[:], lam_row[:], ACT.Exp)
            nc.scalar.activation(lam_ch[:], lam_ch[:], ACT.Exp).then_inc(set_act, 1)
            act.wait_ge(set_dve, 2)
            for h in range(H):
                nc.scalar.activation(dmask[:, h, :], lag[:], ACT.Exp, scale=lam_row[:, h:h + 1])
            for k in range(KT):
                nc.scalar.activation(rdecay[:, k, :], colf[:], ACT.Exp, scale=lam_ch[:, k:k + 1])
            nc.scalar.activation(kdecay[:], lam_row[:], ACT.Exp, scale=rest[:, 0:1])
            nc.scalar.activation(sdecay[:], lam_ch[:], ACT.Exp, scale=float(Q)).then_inc(set_act, 1)

            def step(s):
                front, att, post, send = s, s - 1, s - 2, s - 3
                if front.valid(STEPS):
                    front.wait(act, xt_done, 1, 1)
                    front.wait(act, mix_ready[2])
                    front.wait(act, mix_ready[3])
                    nc.scalar.copy(xT[front.const % 2][:, :, 1:], pX[:]).then_inc(xT_ready, 1)
                if send.valid(STEPS):
                    send.wait(act, lsub_ready, 1, 1)
                    nc.scalar.activation(lexp[:], lsub[:], ACT.Exp).then_inc(lexp_ready, 1)
                if att.valid(STEPS):
                    att.wait(act, intra_done, GPS, GPS)
                    att.wait(act, ssum_done)
                    nc.scalar.activation(ysq[:], pY[:], ACT.Square).then_inc(ysq_ready, 1)
                if front.valid(STEPS):
                    front.wait(act, proj_done[0], 1, 1)
                    front.wait(act, heads_ready, 16 * HPB)
                    front.wait(act, rdec_ready)
                    nc.scalar.copy(rT[:], pA[:]).then_inc(rT_ready, 1)
                if att.valid(STEPS):
                    att.wait(act, ssum_done, 1, 1)
                    act.wait_ge(set_pool, 2)
                    att.wait(act, z_ready)
                    nc.scalar.activation(yn[:], pX[:], ACT.Sqrt, scale=1.0 / N, bias=gn_eps[:, 0:1]).then_inc(gstd_ready, 1)
                if front.valid(STEPS):
                    front.wait(act, proj_done[1], 1, 1)
                    front.wait(act, att_done, GPS)
                    nc.scalar.copy(kT[:], pB[:]).then_inc(kT_ready, 1)
                if post.valid(STEPS):
                    post.wait(act, x2t_done, 1, 1)
                    post.wait(act, logit_done)
                    nc.scalar.copy(x2T[:], pO_ch).then_inc(x2T_ready, 1)
                if front.valid(STEPS):
                    front.wait(act, proj_done[2], 1, 1)
                    front.wait(act, intra_done, GPS)
                    nc.scalar.copy(v_pad[:, :, :, 0:4:3, :].rearrange("p t m a n -> p (t m) a n"),
                                   pA_tok.rearrange("p t (m a n) -> p (t m) a n", a=2, n=N)).then_inc(v_ready, 1)
                    front.wait(act, proj_done[3], 1, 1)
                    front.wait(act, zg_ready, 1, -1)
                    nc.scalar.activation(gT[front.const % 2][:], pB[:], ACT.Gelu).then_inc(gT_ready, 1)
                if att.valid(STEPS):
                    att.wait(act, yn_ready, 1, 1)
                    att.wait(act, zg_ready)
                    for k in range(KT):
                        ins = nc.scalar.activation(z[:, k, :], yn[:, k, :], ACT.Identity,
                                                   scale=lnw_sb[:, k:k + 1], bias=lnb_sb[:, k:k + 1])
                    ins.then_inc(z_ready, 1)

            walk(act, step)

        @block.vector
        def _(dve):
            chain = Chain(dve, dve_chain)
            dve.wait_ge(set_pool, 1)
            chain.link(nc.vector.tensor_copy(lag[:], lag_i[:]))
            chain.add(nc.vector.tensor_scalar(lag[:], lag[:], 0.0, None, ALU.max))
            chain.add(nc.vector.tensor_copy(colf[:], col_i[:]))
            chain.add(nc.vector.tensor_copy(rest[:], rest_i[:]))
            nc.vector.memset(r_heads[:], 0.0).then_inc(set_dve, 1)
            dve.wait_ge(set_act, 1)
            chain.add(nc.vector.tensor_scalar(lam_ch[:], lam_ch[:], 1.0e30, -1.0, ALU.min, ALU.mult))
            chain.sync()
            nc.vector.tensor_scalar(lam_row[:], lam_row[:], 1.0e30, -1.0, ALU.min, ALU.mult).then_inc(set_dve, 1)
            chain.add(nc.vector.memset(v_pad[:], 0.0))
            chain.add(nc.vector.memset(state[0][:], 0.0))
            chain.add(nc.vector.memset(before[0][:], 0.0))
            chain.reset()

            def center_v():
                dve.wait_ge(const_in, 16 * NCONST)
                dve.wait_ge(set_act, 2)
                wv4 = WV[:].rearrange("p k (h n) -> p (k h) n", n=N)
                chain.link(nc.vector.reduce_sum(vmean[:], wv4, axis=AX_X))
                chain.link(nc.vector.tensor_scalar(vmean[:], vmean[:], 1.0 / N, None, ALU.mult))
                nc.vector.tensor_tensor(wv4, wv4, vmean[:].unsqueeze(2).to_broadcast([P, KT * H, N]), ALU.subtract).then_inc(set_dve, 1)
                chain.reset()

            def bonus():
                dve.wait_ge(set_pool, 2)
                chain.add(nc.vector.tensor_copy(iota_e[:], iota_i[:]))
                chain.add(nc.vector.tensor_copy(base[:], base_i[:]))
                for h in range(H):
                    ins = nc.vector.scalar_tensor_tensor(dmask[:, h, :], ident[:], u_sb[:, h:h + 1], dmask[:, h, :],
                                                         ALU.mult, ALU.add)
                ins.then_inc(set_dve, 1)
                dve.wait_ge(set_dve, 4)
                chain.reset()

            def ln_stats(src, stats, mv):
                for t in range(TPS):
                    chain.add(nc.vector.bn_stats(stats[:, t, :], src[:, t, :]))
                chain.sync()

            def mixing(s, k):
                s.wait(dve, proj_done[k])
                for c in range(KT):
                    ins = nc.vector.scalar_tensor_tensor(mix[k][:, c, :], diff[:, c, :], maa_sb[:, k, c:c + 1],
                                                         xT[s.const % 2][:, c, 1:], ALU.mult, ALU.add)
                ins.then_inc(mix_ready[k], 1)

            def step(s):
                nxt, front, att, post, send = s + 1, s, s - 1, s - 2, s - 3
                par_f, par_p, par_s = front.const % 2, post.const % 2, send.const % 2

                def mask_scores(g):
                    att.wait(dve, att_done, GPS, g + 1)
                    att.wait(dve, intra_done, GPS, g - 3)
                    q = g % NG
                    nc.vector.tensor_tensor(attm[g % 4][:], pS[g % 2][:], dmask[:, q * HG:(q + 1) * HG, :],
                                            ALU.mult).then_inc(attm_ready, 1)

                def next_state(c):
                    last = c == TPS - 1
                    old, new = state[c], state[(c + 1) % 2]
                    if last and att.const % SPB == SPB - 1:
                        nc.vector.memset(new[:], 0.0).then_inc(state_ready, 1)
                        return
                    att.wait(dve, kv_done, 1, 1)
                    att.wait(dve, state_ready, TPS, c)
                    chain.link(nc.vector.tensor_tensor(kvm[:], p_kv[:, c], blockdiag[:].unsqueeze(1).to_broadcast([P, KT, P]), ALU.mult))
                    for k in range(KT):
                        ins = nc.vector.scalar_tensor_tensor(new[:, k, :], old[:, k, :], sdecay[:, k:k + 1], kvm[:, k, :],
                                                             ALU.mult, ALU.add)
                    ins.then_inc(state_ready, 1)

                a, f, o, r = att.valid(STEPS), front.valid(STEPS), post.valid(STEPS), send.valid(STEPS)
                if r:
                    send.wait(dve, logit_done, 1, 1)
                    chain.link(nc.vector.reduce_max(lmax[:], p_logit, axis=AX_X))
                    nc.vector.tensor_tensor(lsub[:], p_logit, lmax[:].unsqueeze(2).to_broadcast([P, TPS, E]),
                                            ALU.subtract).then_inc(lsub_ready, 1)
                if nxt.valid(STEPS):
                    if nxt.reg is None:
                        nxt_b = nxt.const // SPB
                        dve.wait_ge(x_in, 16 * (nxt_b + 2 if nxt.const else 1))
                        xa = x_sb[:, nxt.const * TPS:(nxt.const + 1) * TPS, :]
                    else:
                        dve.wait_ge(x_in, 16 * (B + 1))
                        xa = x_sb[:, bass.ds(nxt.count(TPS), TPS), :]
                    for t in range(TPS):
                        chain.add(nc.vector.bn_stats(st1[:, t, :], xa[:, t, :]))
                    chain.sync()
                    for t in range(TPS):
                        ins = nc.vector.bn_aggr(mv1[:, t, :], st1[:, t, :])
                    ins.then_inc(stat1_ready, 1)
                if a:
                    next_state(0)
                    mask_scores(0)
                    mask_scores(1)
                if f:
                    xt = xT[par_f]
                    if front.const % SPB == 0:
                        chain.add(nc.vector.memset(xt[:, :, 0:1], 0.0))
                    else:
                        chain.add(nc.vector.tensor_copy(xt[:, :, 0:1], xT[1 - par_f][:, :, W:W + 1]))
                    front.wait(dve, xT_ready, 1, 1)
                    front.wait(dve, mix_ready[3])
                    chain.sync()
                    nc.vector.tensor_tensor(diff[:], xt[:, :, 0:W], xt[:, :, 1:], ALU.subtract).then_inc(diff_ready, 1)
                if a:
                    mask_scores(2)
                if nxt.valid(STEPS):
                    nxt.wait(dve, rstd1_ready, 1, 1)
                    nxt.wait(dve, stat1_ready, 1, 1)
                    nxt.wait(dve, xt_done)
                    for t in range(TPS):
                        ins = nc.vector.tensor_scalar(xn[:, t, :], xa[:, t, :], mv1[:, t, 0:1], rstd1[:, t:t + 1],
                                                      ALU.subtract, ALU.mult)
                    ins.then_inc(xn_ready, 1)
                if a:
                    mask_scores(3)
                    next_state(1)
                if f:
                    front.wait(dve, diff_ready, 1, 1)
                    mixing(front, 0)
                if o:
                    post.wait(dve, wo_done, 1, 1)
                    post.wait(dve, x1_out, 16, -16)
                    xs = post.count(TPS)
                    src = x_sb[:, xs:xs + TPS, :] if post.reg is None else x_sb[:, bass.ds(xs, TPS), :]
                    nc.vector.tensor_tensor(x1[par_p][:], src, pO_tok, ALU.add).then_inc(x1_ready, 1)
                    post.wait(dve, x1_ready, 1, 1)
                    ln_stats(x1[par_p], st2, mv2)
                    for t in range(TPS):
                        ins = nc.vector.bn_aggr(mv2[:, t, :], st2[:, t, :])
                    ins.then_inc(stat2_ready, 1)
                if a:
                    for g in range(NG, GPS):
                        mask_scores(g)
                if f:
                    mixing(front, 1)
                if o:
                    post.wait(dve, rstd2_ready, 1, 1)
                    post.wait(dve, stat2_ready, 1, 1)
                    post.wait(dve, sent, 16 * 2 * TPS, -16 * 2 * TPS)
                    post.wait(dve, x2t_done, 1, -1)
                    for t in range(TPS):
                        ins = nc.vector.tensor_scalar(row[par_p][:, t, 0:C], x1[par_p][:, t, :], mv2[:, t, 0:1],
                                                      rstd2[:, t:t + 1], ALU.subtract, ALU.mult)
                    ins.then_inc(xn2_ready, 1)
                if f:
                    mixing(front, 2)
                if r:
                    send.wait(dve, lexp_ready, 1, 1)
                    prob = row[par_s][:, :, C:C + E]
                    chain.link(nc.vector.reduce_sum(lsum[:], lexp[:], axis=AX_X))
                    chain.link(nc.vector.reciprocal(lrec[:], lsum[:]))
                    ts = send.count(TPS)
                    src = tok[:, ts:ts + TPS] if send.reg is None else tok[:, bass.ds(ts, TPS)]
                    chain.add(nc.vector.tensor_copy(row[par_s][:, :, ROW - 1].bitcast(I32), src))
                    chain.link(nc.vector.tensor_tensor(prob, lexp[:], lrec[:].unsqueeze(2).to_broadcast([P, TPS, E]), ALU.mult))
                    for t in range(TPS):
                        chain.add(nc.vector.max(top[:, t, :], prob[:, t, :]))
                    chain.sync()
                    for t in range(TPS):
                        chain.add(nc.vector.max_index(topi[:, t, :], top[:, t, :], prob[:, t, :]))
                    chain.sync()
                    chain.link(nc.vector.tensor_copy(topf[:], topi[:, :, 0:2]))
                    for k in range(2):
                        chain.add(nc.vector.tensor_tensor(hot[par_s][k][:], iota_e[:].unsqueeze(1).to_broadcast([P, TPS, E]),
                                                          topf[:, :, k:k + 1].to_broadcast([P, TPS, E]), ALU.is_equal))
                    chain.sync()
                    send.wait(dve, count_done)
                    chain.link(nc.vector.tensor_tensor(took[par_s][:], hot[par_s][0][:], hot[par_s][1][:], ALU.add))
                    nc.vector.tensor_tensor(before[par_s][:, 1, :], before[par_s][:, 0, :], took[par_s][:, 0, :],
                                            ALU.add).then_inc(took_ready, 1)
                    following = before[1 - par_s][:, 0, :]
                    if send.const % SPB == SPB - 1:
                        chain.add(nc.vector.memset(following, 0.0))
                    else:
                        send.wait(dve, took_ready, 1, 1)
                        chain.add(nc.vector.tensor_tensor(following, before[par_s][:, 1, :], took[par_s][:, 1, :], ALU.add))
                if a:
                    att.wait(dve, gstd_ready, 1, 1)
                    chain.link(nc.vector.reciprocal(yn[:], yn[:]))
                    nc.vector.tensor_tensor(yn[:], pY[:], yn[:], ALU.mult).then_inc(yn_ready, 1)
                if f:
                    front.wait(dve, kt_done, 1, 1)
                    front.wait(dve, kv_done)
                    nc.vector.tensor_tensor(k_dec[:].rearrange("p t (h n) -> p t h n", n=N),
                                            pK_tok.rearrange("p t (h n) -> p t h n", n=N),
                                            kdecay[:].unsqueeze(1).unsqueeze(3).to_broadcast([P, TPS, H, N]),
                                            ALU.mult).then_inc(kdec_ready, 1)
                if r:
                    send.wait(dve, count_done, 1, 1)
                    if send.const % SPB == 0 and not (send.reg is None and send.const == 0):
                        chain.link(nc.vector.tensor_scalar(base[:], base[:], float(CAP), None, ALU.add))
                    chain.add(nc.vector.tensor_scalar(over[:], p_count, float(CAP), DROP, ALU.is_gt, ALU.mult))
                    chain.link(nc.vector.tensor_tensor(slotf[:], p_count, base[:].unsqueeze(1).to_broadcast([P, TPS, E]), ALU.add))
                    chain.link(nc.vector.tensor_tensor(slotf[:], slotf[:], over[:], ALU.add))
                    for k in range(2):
                        chain.add(nc.vector.tensor_tensor(pick[k][:], slotf[:], hot[par_s][k][:], ALU.mult))
                    chain.sync()
                    for k in range(2):
                        chain.add(nc.vector.reduce_sum(slot_k[:, k, :], pick[k][:], axis=AX_X))
                    chain.sync()
                    send.wait(dve, sent, 16 * 2 * TPS)
                    nc.vector.tensor_copy(slot_i[:], slot_k[:]).then_inc(slot_ready, 1)
                chain.reset()

            walk(dve, step, {0: center_v, 1: bonus, 2: lambda: dve.wait_ge(set_pool, 3)})

        @block.tensor
        def _(pe):
            pe.wait_ge(set_pool, 1)

            def project(s, k, dst, w):
                s.wait(pe, mix_ready[k], 1, 1)
                for m in range(KT):
                    for c in range(KT):
                        ins = nc.tensor.matmul(dst[:, m, :], w[:, c, m * P:(m + 1) * P], mix[k][:, c, :],
                                               start=(c == 0), stop=(c == KT - 1))
                ins.then_inc(proj_done[k], 1)

            def v_block(t, c):
                return v_pad[:, t, c * HPB // 2:(c + 1) * HPB // 2, 0:4:3, :]

            def group_norm(att, front):
                att.wait(pe, ysq_ready, 1, 1)
                if front.valid(STEPS):
                    front.wait(pe, xT_ready, 1, 1)
                att.wait(pe, gstd_ready)
                for k in range(KT):
                    ins = nc.tensor.matmul(pX[:, k, :], blockdiag[:], ysq[:, k, :], start=True, stop=True)
                ins.then_inc(ssum_done, 1)

            def step(s):
                front, att, post, send = s, s - 1, s - 2, s - 3
                if s.reg is None and s.const == 1:
                    pe.wait_ge(set_pool, 2)
                if front.valid(STEPS):
                    front.wait(pe, xn_ready, 1, 1)
                    front.wait(pe, gstd_ready, 1, -1)
                    front.wait(pe, xT_ready)
                    for t in range(TPS):
                        for c in range(KT):
                            ins = nc.tensor.transpose(pX[:, c, t * Q:(t + 1) * Q], xn[:, t, c * P:(c + 1) * P], ident[:])
                    ins.then_inc(xt_done, 1)
                if att.valid(STEPS):
                    att.wait(pe, kdec_ready, 1, 1)
                    att.wait(pe, v_ready, 1, 1)
                    for t in range(TPS):
                        for c in range(KT):
                            ins = nc.tensor.matmul(p_kv[:, t, c, :], k_dec[:, t, c * P:(c + 1) * P], v_block(t, c),
                                                   start=True, stop=True)
                    ins.then_inc(kv_done, 1)
                    att.wait(pe, yn_ready)
                    att.wait(pe, rdec_ready, 1, 1)
                    att.wait(pe, kT_ready, 1, 1)
                    att.wait(pe, heads_ready, 16 * HPB, 16 * HPB)

                    def across(t):
                        att.wait(pe, state_ready, TPS, t)
                        for c in range(KT):
                            nc.tensor.matmul(pY[:, c, t * Q:(t + 1) * Q], state[t][:, c, :], r_dec[:, c, t * Q:(t + 1) * Q],
                                             start=(t == 0 and c == 0), stop=False, skip_group_check=True)

                    def scores(g):
                        t, q = divmod(g, NG)
                        c, h = divmod(q * HG, HPB)
                        att.wait(pe, attm_ready, GPS, g - 1)
                        if g == 0 and send.valid(STEPS):
                            send.wait(pe, slot_ready)
                        if g == 1 and send.valid(STEPS):
                            send.wait(pe, lsub_ready, 1, 1)
                        nc.tensor.matmul(pS[g % 2][:], kT[:, c, t * Q:(t + 1) * Q], r_heads[:, c, h:h + HG, t * Q:(t + 1) * Q],
                                         start=True, stop=True).then_inc(att_done, 1)

                    def within(g):
                        t, q = divmod(g, NG)
                        att.wait(pe, attm_ready, GPS, g + 1)
                        for h in range(HG):
                            c, pos = divmod(q * HG + h, HPB)
                            ins = nc.tensor.matmul(pY[pos // 2 * 2 * N:(pos // 2 + 1) * 2 * N, c, t * Q:(t + 1) * Q],
                                                   v_pad[:, t, (q * HG + h) // 2, pos % 2 * 2:(pos % 2 + 1) * 2, :].rearrange("p a n -> p (a n)"),
                                                   attm[g % 4][:, h, :], start=False, stop=(g == GPS - 1 and h == HG - 1), skip_group_check=True)
                        ins.then_inc(intra_done, 1)

                    across(0)
                    scores(0)
                    for g in range(1, NG + 1):
                        scores(g)
                        within(g - 1)
                if post.valid(STEPS):
                    post.wait(pe, zg_ready, 1, 1)
                    post.wait(pe, x2T_ready)
                    for t in range(TPS):
                        for c in range(KT):
                            ins = nc.tensor.matmul(pO_tok[:, t, :], zg[:, c, t * Q:(t + 1) * Q], WO[:, c, :],
                                                   start=(c == 0), stop=(c == KT - 1))
                    ins.then_inc(wo_done, 1)
                if att.valid(STEPS):
                    across(1)
                    for g in range(NG + 1, GPS):
                        scores(g)
                        within(g - 1)
                    within(GPS - 1)
                if front.valid(STEPS):
                    if front.reg is None and front.const == 0:
                        pe.wait_ge(const_in, 16 * NCONST)
                        pe.wait_ge(set_dve, 3)
                    front.wait(pe, state_ready, TPS)
                    project(front, 0, pA, WR)
                if att.valid(STEPS):
                    group_norm(att, front)
                if front.valid(STEPS):
                    front.wait(pe, gT_ready)
                    project(front, 1, pB, WK)
                if post.valid(STEPS):
                    post.wait(pe, xn2_ready, 1, 1)
                    for t in range(TPS):
                        for c in range(KT):
                            ins = nc.tensor.transpose(pO_ch[:, c, t * Q:(t + 1) * Q], row[post.const % 2][:, t, c * P:(c + 1) * P], ident[:])
                    ins.then_inc(x2t_done, 1)
                if send.valid(STEPS):
                    send.wait(pe, took_ready, 1, 1)
                    if att.valid(STEPS):
                        att.wait(pe, attm_ready, GPS, GPS)
                    send.wait(pe, slot_ready)
                    r = send.const % 2
                    cnt = pS[0][:, 0, 0:TPS * E]
                    nc.tensor.matmul(cnt, tri[:], took[r][:].rearrange("p t e -> p (t e)"), start=True, stop=False)
                    nc.tensor.matmul(cnt, ones[:], before[r][:].rearrange("p t e -> p (t e)"), start=False, stop=True).then_inc(count_done, 1)
                if front.valid(STEPS):
                    front.wait(pe, mix_ready[2], 1, 1)
                    front.wait(pe, rT_ready, 1, 1)
                    for t in range(TPS):
                        for c in range(KT):
                            ins = nc.tensor.matmul(pA_tok[:, t, :], mix[2][:, c, t * Q:(t + 1) * Q], WV[:, c, :],
                                                   start=(c == 0), stop=(c == KT - 1))
                    ins.then_inc(proj_done[2], 1)
                    front.wait(pe, kT_ready, 1, 1)
                    front.wait(pe, kdec_ready)
                    for t in range(TPS):
                        for c in range(KT):
                            ins = nc.tensor.transpose(pK_tok[:, t, c * P:(c + 1) * P], kT[:, c, t * Q:(t + 1) * Q], ident[:])
                    ins.then_inc(kt_done, 1)
                    project(front, 3, pB, WG)
                if post.valid(STEPS):
                    post.wait(pe, x2T_ready, 1, 1)
                    if att.valid(STEPS):
                        att.wait(pe, attm_ready, GPS, GPS)
                    for t in range(TPS):
                        for c in range(KT):
                            ins = nc.tensor.matmul(p_logit[:, t, :], x2T[:, c, t * Q:(t + 1) * Q], gate_sb[:, c, :],
                                                   start=(c == 0), stop=(c == KT - 1))
                    ins.then_inc(logit_done, 1)

            walk(pe, step)


def phase_b(nc, sb, ps, ctx, sem, ident, whi, wlo, wraw, w1, w2, w3, disp, out):
    CW = max(n for _, n in CHUNKS) * P
    xtok = sb("xtok", [P, ST, ROW])
    xh = sb("xh", [P, KT, SLOTS], F32R)
    xl = sb("xl", [P, KT, SLOTS], F32R)
    weight = [sb(f"weight{k}", [P, ST]) for k in range(2)]
    index = [sb(f"index{k}", [P, ST], I32) for k in range(2)]
    gated = [sb(f"gated{k}", [P, CW]) for k in range(2)]
    hid = [sb(f"hid{k}", [P, CW]) for k in range(2)]
    hh = [sb(f"hh{k}", [P, FT, CW], F32R) for k in range(2)]
    hl = [sb(f"hl{k}", [P, FT, CW], F32R) for k in range(2)]
    NY = 4
    ysb = [sb(f"ysb{k}", [P, C]) for k in range(NY)]

    p1 = [ps(f"p1_{k}", [P, CW]) for k in range(2)]
    p3 = [ps(f"p3_{k}", [P, CW]) for k in range(2)]
    py = [ps(f"py{k}", [P, 512]) for k in range(2)]
    pt = [ps(f"pt{k}", [P, 512]) for k in range(2)]

    rows_in, rows_used = sem("rows_in"), sem("rows_used")
    w_in = [sem(f"w_in{k}") for k in range(2)]
    whi_ready, wlo_ready = sem("whi_ready"), sem("wlo_ready")
    turned, xh_ready, xl_ready = sem("turned"), sem("xh_ready"), sem("xl_ready")
    weight_ready, index_ready = sem("weight_ready"), sem("index_ready")
    h_done, gated_ready, hid_ready = sem("h_done"), sem("gated_ready"), sem("hid_ready")
    hh_ready, hl_ready = sem("hh_ready"), sem("hl_ready")
    ffn_done, ysb_ready = sem("ffn_done"), sem("ysb_ready")
    added = [sem(f"added{k}") for k in range(NY)]

    HPE = NCH * FT
    TB = 2 * NCH - 1
    rows_view = disp.rearrange("(e p t) c -> e p (t c)", e=E, p=P)
    w_view = [w1.rearrange("e (k p) f -> e p k f", p=P), w3.rearrange("e (k p) f -> e p k f", p=P),
              w2.rearrange("e (j p) c -> e p j c", p=P)]

    def row_of(view, e):
        i = e.count()
        return view[i] if e.reg is None else view[bass.ds(i, 1)].squeeze(0)

    def pair(e):
        u = e.const % 2
        return e - u, u

    def walk(step):
        return step

    def run(eng, step):
        for e in range(2):
            step(At(e))
        with eng.Fori(2, E - 3, 2) as e0:
            for u in range(2):
                step(At(u, e0, 2))
        for e in range(E - 2, E):
            step(At(e))

    def banks():
        for c, (t0, n) in enumerate(CHUNKS):
            if n * P * KT <= 512:
                yield c, range(KT), range(t0, t0 + n)
            else:
                for k in range(KT):
                    yield c, range(k, k + 1), range(t0, t0 + n)

    BANKS = list(banks())
    assert len(BANKS) == TB
    LAST_BANK = [max(i for i, b in enumerate(BANKS) if b[0] == c) for c in range(NCH)]

    def bank_of(i, n):
        _, ks, ts = BANKS[i]
        w = len(ts) * P
        src = pt[n % 2][:, 0:len(ks) * w].rearrange("p (k s) -> p k s", k=len(ks))
        cut = (slice(None), slice(ks[0], ks[-1] + 1), slice(ts[0] * P, ts[0] * P + w))
        return src, cut

    def added_before(eng, e, more):
        even, u = pair(e)
        for r in range(NY):
            n = len(range(r, ST * u + more, NY))
            even.wait(eng, added[r], 16 * ST // NY, 16 * n)

    with nc.Block() as block:

        @block.sync
        def _(sp):
            def load_rows(e):
                e.wait(sp, turned, TB)
                e.wait(sp, rows_used, 2)
                sp.dma_start(xtok[:].rearrange("p t c -> p (t c)"), row_of(rows_view, e)).then_inc(rows_in, 16)

            def load_weights(e, m):
                even, u = pair(e)
                k = (3 * u + m) % 2
                e.wait(sp, whi_ready, 3, m - 1)
                e.wait(sp, wlo_ready, 3, m - 1)
                dst = wraw[k][:].rearrange("p (k f) -> p k f", k=KT if m < 2 else FT)
                sp.dma_start(dst, row_of(w_view[m], e)).then_inc(w_in[k], 16)

            load_rows(At(0))
            for m in range(3):
                load_weights(At(0), m)

            def step(e):
                nxt = e + 1
                if nxt.valid(E):
                    load_rows(nxt)
                    for m in range(3):
                        load_weights(nxt, m)

            run(sp, step)

        @block.gpsimd
        def _(pool):
            def keep_index(e):
                e.wait(pool, rows_in, 16, 16)
                pool.wait_ge(rows_in, 16)
                nc.gpsimd.tensor_copy(index[e.const % 2][:], xtok[:, :, ROW - 1].bitcast(I32)).then_inc(index_ready, 1)
                e.wait(pool, index_ready, 1, 1)
                pool.sem_inc(rows_used, 1)

            keep_index(At(0))

            def step(e):
                added_before(pool, e, 0)
                even, u = pair(e)
                for t in range(ST):
                    j = ST * u + t
                    e.wait(pool, ysb_ready, ST, t + 1)
                    pool.wait_ge(rows_in, 16)
                    nc.gpsimd.indirect_dma_start(
                        out, bass.IndirectOffsetOnAxis(ap=index[e.const % 2][:, t:t + 1], axis=0),
                        ysb[j % NY][:], None, compute_op=ALU.add).then_inc(added[j % NY], 16)
                    if t == ST - 3 and (e + 1).valid(E):
                        keep_index(e + 1)

            run(pool, step)
            added_before(pool, At(E), 0)

        @block.scalar
        def _(act):
            def split_hi(e, m):
                even, u = pair(e)
                even.wait(act, w_in[(3 * u + m) % 2], 24, 16 * ((3 * u + m) // 2 + 1))
                if m < 2:
                    e.wait(act, h_done, HPE, -HPE)
                else:
                    e.wait(act, ffn_done, ST, -ST)
                nc.scalar.copy(whi[e.const % 2][m][:], wraw[(3 * u + m) % 2][:]).then_inc(whi_ready, 1)

            def turn_hi(e, i):
                u = e.const % 2
                src, cut = bank_of(i, TB * u + i)
                e.wait(act, turned, TB, i + 1)
                nc.scalar.copy(xh[cut], src).then_inc(xh_ready, 1)

            def gate(e, c, f):
                k = (pair(e)[1] * HPE + c * FT + f) % 2
                w = CHUNKS[c][1] * P
                e.wait(act, h_done, HPE, c * FT + f + 1)
                e.wait(act, hid_ready, HPE, c * FT + f - 1)
                nc.scalar.activation(gated[k][:, 0:w], p1[k][:, 0:w], ACT.Silu).then_inc(gated_ready, 1)

            def hidden_hi(e, c, f):
                u = pair(e)[1]
                k = (u * HPE + c * FT + f) % 2
                w = CHUNKS[c][1] * P
                e.wait(act, hid_ready, HPE, c * FT + f + 1)
                if f == 0:
                    free_hidden(act, e, c)
                nc.scalar.copy(hh[(u * NCH + c) % 2][:, f, 0:w], hid[k][:, 0:w]).then_inc(hh_ready, 1)

            def scale_out(e, t):
                j = ST * pair(e)[1] + t
                even, u = pair(e)
                e.wait(act, ffn_done, ST, t + 1)
                e.wait(act, weight_ready, 1, 1)
                if e.reg is not None or ST * e.const + t >= NY:
                    even.wait(act, added[j % NY], 16 * ST // NY, 16 * (j // NY))
                nc.scalar.activation(ysb[j % NY][:], py[j % 2][:, 0:C], ACT.Copy, scale=weight[e.const % 2][:, t:t + 1]).then_inc(ysb_ready, 1)

            def hidden(e, c):
                for f in range(FT):
                    gate(e, c, f)
                    if f:
                        hidden_hi(e, c, f - 1)
                hidden_hi(e, c, FT - 1)

            def scale_chunk(e, c):
                t0, n = CHUNKS[c]
                for t in range(t0, t0 + n):
                    scale_out(e, t)

            for m in range(2):
                split_hi(At(0), m)
            for i in range(TB):
                turn_hi(At(0), i)
            split_hi(At(0), 2)

            def step(e):
                nxt = e + 1
                more = nxt.valid(E)
                hidden(e, 0)
                if more:
                    split_hi(nxt, 0)
                hidden(e, 1)
                scale_chunk(e, 0)
                if more:
                    split_hi(nxt, 1)
                hidden(e, 2)
                scale_chunk(e, 1)
                if more:
                    split_hi(nxt, 2)
                t0, n = CHUNKS[2]
                todo = list(range(TB)) if more else []
                for t in range(t0, t0 + n):
                    for i in todo[:2]:
                        turn_hi(nxt, i)
                    todo = todo[2:]
                    scale_out(e, t)
                for i in todo:
                    turn_hi(nxt, i)

            def free_hidden(eng, e, c):
                n = c - 2 if c >= 2 else c - 2 + NCH
                past = e if c >= 2 else e - 1
                t0, cnt = CHUNKS[n]
                past.wait(eng, ffn_done, ST, t0 + cnt)

            run(act, step)

        @block.vector
        def _(dve):
            def split_lo(e, m):
                u = pair(e)[1]
                k = (3 * u + m) % 2
                e.wait(dve, whi_ready, 3, m + 1)
                nc.vector.tensor_tensor(wlo[e.const % 2][m][:], wraw[k][:], whi[e.const % 2][m][:].bitcast(F32),
                                        ALU.subtract).then_inc(wlo_ready, 1)

            def turn_lo(e, i):
                src, cut = bank_of(i, TB * (e.const % 2) + i)
                e.wait(dve, xh_ready, TB, i + 1)
                nc.vector.tensor_tensor(xl[cut], src, xh[cut].bitcast(F32), ALU.subtract).then_inc(xl_ready, 1)

            def keep_weight(e):
                e.wait(dve, rows_in, 16, 16)
                e.wait(dve, ysb_ready, ST, -ST)
                col = e.count(1, C)
                src = xtok[:, :, col] if e.reg is None else xtok[:, :, bass.ds(col, 1)].squeeze(2)
                nc.vector.tensor_scalar(weight[e.const % 2][:], src, 1.0, None, ALU.mult).then_inc(weight_ready, 1)
                e.wait(dve, weight_ready, 1, 1)
                dve.sem_inc(rows_used, 1)

            def hidden_value(e, c, f):
                k = (pair(e)[1] * HPE + c * FT + f) % 2
                w = CHUNKS[c][1] * P
                e.wait(dve, gated_ready, HPE, c * FT + f + 1)
                e.wait(dve, hl_ready, HPE, c * FT + f - 1)
                nc.vector.tensor_tensor(hid[k][:, 0:w], gated[k][:, 0:w], p3[k][:, 0:w], ALU.mult).then_inc(hid_ready, 1)

            def hidden_lo(e, c, f):
                u = pair(e)[1]
                k = (u * HPE + c * FT + f) % 2
                w = CHUNKS[c][1] * P
                e.wait(dve, hh_ready, HPE, c * FT + f + 1)
                s = (u * NCH + c) % 2
                nc.vector.tensor_tensor(hl[s][:, f, 0:w], hid[k][:, 0:w], hh[s][:, f, 0:w].bitcast(F32),
                                        ALU.subtract).then_inc(hl_ready, 1)

            def hidden(e, c):
                for f in range(FT):
                    hidden_value(e, c, f)
                    if f:
                        hidden_lo(e, c, f - 1)
                hidden_lo(e, c, FT - 1)

            for m in range(2):
                split_lo(At(0), m)
            for i in range(TB):
                turn_lo(At(0), i)
            keep_weight(At(0))
            split_lo(At(0), 2)

            def step(e):
                nxt = e + 1
                more = nxt.valid(E)
                for c in range(NCH):
                    hidden(e, c)
                    if more:
                        split_lo(nxt, c)
                if more:
                    for i in range(TB):
                        turn_lo(nxt, i)
                    keep_weight(nxt)

            run(dve, step)

        @block.tensor
        def _(pe):
            def turn(e, i):
                n = TB * (e.const % 2) + i
                _, ks, ts = BANKS[i]
                e.wait(pe, rows_in, 16, 16)
                e.wait(pe, xl_ready, TB, i - 1)
                src, _ = bank_of(i, n)
                for a, k in enumerate(ks):
                    for b, t in enumerate(ts):
                        ins = nc.tensor.transpose(src[:, a, b * P:(b + 1) * P], xtok[:, t, k * P:(k + 1) * P], ident[:])
                ins.then_inc(turned, 1)

            def up(e, c):
                u = pair(e)[1]
                t0, n = CHUNKS[c]
                w = n * P
                e.wait(pe, xl_ready, TB, LAST_BANK[c] + 1)
                e.wait(pe, wlo_ready, 3, 2)
                hi, lo = whi[e.const % 2], wlo[e.const % 2]
                for f in range(FT):
                    k = (u * HPE + c * FT + f) % 2
                    e.wait(pe, hid_ready, HPE, c * FT + f - 1)
                    for m, dst in ((0, p1[k]), (1, p3[k])):
                        for kt in range(KT):
                            wcut = slice(kt * F + f * P, kt * F + (f + 1) * P)
                            xcut = (slice(None), kt, slice(t0 * P, t0 * P + w))
                            nc.tensor.matmul(dst[:, 0:w], hi[m][:, wcut], xh[xcut], start=(kt == 0), stop=False)
                            nc.tensor.matmul(dst[:, 0:w], hi[m][:, wcut], xl[xcut], start=False, stop=False)
                            ins = nc.tensor.matmul(dst[:, 0:w], lo[m][:, wcut], xh[xcut], start=False, stop=(kt == KT - 1))
                    ins.then_inc(h_done, 1)

            def down(e, t):
                u = pair(e)[1]
                c = next(i for i, (t0, n) in enumerate(CHUNKS) if t0 <= t < t0 + n)
                s = (u * NCH + c) % 2
                j = ST * u + t
                e.wait(pe, hl_ready, HPE, FT * (c + 1))
                e.wait(pe, wlo_ready, 3, 3)
                e.wait(pe, ysb_ready, ST, t - 1)
                off = (t - CHUNKS[c][0]) * P
                hi, lo = whi[e.const % 2][2], wlo[e.const % 2][2]
                for f in range(FT):
                    a, b = hh[s][:, f, off:off + P], hl[s][:, f, off:off + P]
                    cut = slice(f * C, (f + 1) * C)
                    nc.tensor.matmul(py[j % 2][:, 0:C], a, hi[:, cut], start=(f == 0), stop=False)
                    nc.tensor.matmul(py[j % 2][:, 0:C], a, lo[:, cut], start=False, stop=False)
                    ins = nc.tensor.matmul(py[j % 2][:, 0:C], b, hi[:, cut], start=False, stop=(f == FT - 1))
                ins.then_inc(ffn_done, 1)

            def down_chunk(e, c):
                t0, n = CHUNKS[c]
                for t in range(t0, t0 + n):
                    down(e, t)

            for i in range(TB):
                turn(At(0), i)

            def step(e):
                nxt = e + 1
                up(e, 0)
                up(e, 1)
                down_chunk(e, 0)
                up(e, 2)
                down_chunk(e, 1)
                t0, n = CHUNKS[2]
                todo = list(range(TB)) if nxt.valid(E) else []
                for t in range(t0, t0 + n):
                    for i in todo[:2]:
                        turn(nxt, i)
                    todo = todo[2:]
                    down(e, t)
                for i in todo:
                    turn(nxt, i)

            run(pe, step)


def kernel(**inputs):
    import concourse.bacc as bacc
    from concourse.bass_utils import run_bass_kernel_spmd

    a = {k: np.asarray(v) for k, v in inputs.items()}

    def by_channel(v):
        return v.reshape(KT, P).T

    att = "L0_attn_"
    arrays = {
        "x": a[att + "x"].reshape(NTOK, C),
        "maa": np.stack([by_channel(a[att + "time_maa_" + k]) for k in "rkvg"], axis=1),
        "decay_row": np.broadcast_to(a[att + "time_decay"].reshape(1, H), (P, H)),
        "decay_ch": by_channel(np.repeat(a[att + "time_decay"].reshape(H), N)),
        "u_row": np.broadcast_to(a[att + "time_faaaa"].reshape(1, H), (P, H)),
        "wrT": a[att + "Wr"].T, "wkT": a[att + "Wk"].T, "wvT": a[att + "Wv"].T,
        "wgT": a[att + "Wg"].T, "woT": a[att + "Wo"].T,
        "lnw": by_channel(a[att + "ln_w"]), "lnb": by_channel(a[att + "ln_b"]),
        "gateT": a["L0_ffn_gate_w"].T,
        "w1": a["L0_ffn_w1"], "w2": a["L0_ffn_w2"], "w3": a["L0_ffn_w3"],
    }
    arrays = {f"in_{k}": np.ascontiguousarray(v) for k, v in arrays.items()}
    nc = bacc.Bacc("TRN2", target_bir_lowering=False, num_devices=1)
    args = [nc.dram_tensor(k, v.shape, mybir.dt.from_np(v.dtype), kind="ExternalInput").ap() for k, v in arrays.items()]
    args.append(nc.dram_tensor("out", [NTOK + SLOTS, C], F32, kind="ExternalOutput").ap())
    build(nc, *args)
    r = run_bass_kernel_spmd(nc, [arrays], core_ids=[0])
    return r.results[0]["out"][:NTOK].reshape(B, T, C)
```

```python
from contextlib import ExitStack

import numpy as np

import concourse.bass as bass
from concourse import mybir

F32 = mybir.dt.float32
F32R = mybir.dt.float32r
I32 = mybir.dt.int32
U32 = mybir.dt.uint32
ALU = mybir.AluOpType
ACT = mybir.ActivationFunctionType
AX_X = mybir.AxisListType.X

P = 128
B, T, C = 4, 1024, 256
NTOK = B * T
H = 16
N = C // H
KT = C // P
Q = P
TPS = 2
W = TPS * Q
STEPS = NTOK // W
SPB = T // W
HG = 4
NG = H // HG
GPS = TPS * NG
HPB = H // KT
LN_EPS = 1e-5
GN_EPS = 1e-5 * 64
E = 8
F = 896
FT = F // P
CAP = T * 2 // E * 5 // 4
SLOTS = B * CAP
ST = SLOTS // P
ROW = C + E + 1
DROP = 1.0e6
WP = 4
NW = KT * F
WPC = NW // WP
RING = 4
CHUNKS = [(0, 2), (2, 4), (6, 4)]
NCH = len(CHUNKS)
LAM_MIN, LAM_MAX, FAR = 1.0e-30, 1.0e3, -1.0e34
REST = CHUNKS[0][1]
COMMON = ST - REST


class At:

    alone = {}

    def __init__(self, const, reg=None, least=0):
        self.const, self.reg, self.least = const, reg, least

    def __sub__(self, k):
        return At(self.const - k, self.reg, self.least)

    def __add__(self, k):
        return At(self.const + k, self.reg, self.least)

    def count(self, per=1, more=0):
        v = per * self.const + more
        return v if self.reg is None else self.reg * per + v

    def wait(self, eng, sem, per=1, more=0):
        v = self.count(per, more)
        if self.reg is None:
            if v > 0:
                eng.wait_ge(sem, v)
        else:
            assert per * (self.least + self.const) + more > 0
            eng.wait_ge(sem, v)
            if eng in At.alone:
                eng.sem_inc(At.alone[eng], 1)

    def valid(self, n):
        return self.reg is not None or 0 <= self.const < n


class Chain:

    def __init__(self, eng, sem):
        self.eng, self.sem, self.n = eng, sem, 0

    def add(self, ins):
        self.n += 1
        ins.then_inc(self.sem, 1)

    def sync(self):
        self.eng.wait_ge(self.sem, self.n)

    def link(self, ins):
        self.add(ins)
        self.sync()

    def reset(self):
        if self.n:
            self.sync()
            self.eng.sem_inc(self.sem, -self.n)
            self.n = 0


def build(nc, x, maa, decay_row, decay_ch, u_row, wrT, wkT, wvT, wgT, woT, lnw, lnb, gateT, w1, w2, w3, out):
    disp = nc.dram_tensor("disp", [E * SLOTS, ROW], F32).ap()
    persist = ExitStack()
    with persist:
        def tensors(ctx):
            def sb(name, shape, dt=F32):
                return ctx.enter_context(nc.sbuf_tensor(name, shape, dt))

            def ps(name, shape):
                return ctx.enter_context(nc.psum_tensor(name, shape, F32))

            return sb, ps

        sems = {}

        def sem(name):
            if name not in sems:
                sems[name] = persist.enter_context(nc.semaphore(name))
            return sems[name]

        At.alone = {nc.sync: sem("sp_waited"), nc.gpsimd: sem("pool_waited")}
        sb, _ = tensors(persist)
        whi = [[sb(f"whi0_{m}", [P, NW], F32R) for m in range(3)]]
        wlo = [[sb(f"wlo0_{m}", [P, NW], F32R) for m in range(3)]]
        wraw = [sb(f"wraw{k}", [P, NW]) for k in range(2)]
        ident = sb("ident", [P, P])
        taken = sb("taken", [P, E], I32)
        with ExitStack() as ctx:
            phase_a(nc, *tensors(ctx), ctx, sem, ident, x, maa, decay_row, decay_ch, u_row,
                    (wrT, wkT, wvT, wgT, woT), lnw, lnb, gateT, disp, out, whi[0], wlo[0], wraw, (w1, w3), taken)
        with ExitStack() as ctx:
            sb2, ps2 = tensors(ctx)
            whi.append([sb2(f"whi1_{m}", [P, NW], F32R) for m in range(3)])
            wlo.append([sb2(f"wlo1_{m}", [P, NW], F32R) for m in range(3)])
            phase_b(nc, sb2, ps2, ctx, sem, ident, whi, wlo, wraw, w1, w2, w3, taken, disp, out)


def expert_views(w1, w3, w2):
    return [w1.rearrange("e (k p) f -> e p k f", p=P), w3.rearrange("e (k p) f -> e p k f", p=P),
            w2.rearrange("e (j p) c -> e p j c", p=P) if w2 is not None else None]


def phase_a(nc, sb, ps, ctx, sem, ident, x, maa, decay_row, decay_ch, u_row, weights, lnw, lnb, gateT, disp, out,
            whi, wlo, wraw, first_w, taken):
    x_ring = sb("x_ring", [P, RING, TPS, C])
    per = KT * C
    staged = [wraw[1][:, k * per:(k + 1) * per].rearrange("p (k c) -> p k c", k=KT) for k in range(NW // per)]
    w_in_sb = [*staged, *[sb(f"w_in_sb{k}", [P, KT, C])[:] for k in range(len(staged), 5)]]
    WV, WO = w_in_sb[2], w_in_sb[4]
    w_hi = [sb(f"w_hi{k}", [P, KT, C], F32R) for k in range(4)]
    w_lo = [sb(f"w_lo{k}", [P, KT, C], F32R) for k in range(4)]
    gate_sb = sb("gate_sb", [P, KT, E])
    maa_sb = sb("maa_sb", [P, 4, KT])
    lnw_sb = sb("lnw_sb", [P, KT])
    lnb_sb = sb("lnb_sb", [P, KT])
    lam_row = sb("lam_row", [P, H])
    lam_ch = sb("lam_ch", [P, KT])
    u_sb = sb("u_sb", [P, H])
    vmean = sb("vmean", [P, KT * H])
    dmask = sb("dmask", [P, H, Q])
    kdecay = sb("kdecay", [P, H])
    rdecay = sb("rdecay", [P, KT, Q])
    sdecay = sb("sdecay", [P, KT])
    blockdiag = sb("blockdiag", [P, P])
    tri = sb("tri", [P, P])
    ones = sb("ones", [P, P])
    lag_i = sb("lag_i", [P, Q], I32)
    empty_i = sb("empty_i", [P, ST // 2], I32)
    lag = sb("lag", [P, Q])
    cut_off = sb("cut_off", [P, Q])
    col_i = sb("col_i", [P, Q], I32)
    colf = sb("colf", [P, Q])
    rest_i = sb("rest_i", [P, 1], I32)
    rest = sb("rest", [P, 1])
    iota_i = sb("iota_i", [P, E], I32)
    iota_e = sb("iota_e", [P, E])
    base_i = sb("base_i", [P, E], I32)
    base0 = sb("base0", [P, E])
    base = sb("base", [P, E])
    tok = sb("tok", [P, NTOK // P], I32)
    mhalf = sb("mhalf", [P, TPS])
    EH = ST // 2
    empty = wraw[0][:, 0:EH * ROW].rearrange("p (t c) -> p t c", c=ROW)

    mv1 = sb("mv1", [P, TPS, 2])
    st1 = sb("st1", [P, TPS, 6])
    var1 = sb("var1", [P, TPS])
    rstd1 = sb("rstd1", [P, TPS])
    xn = sb("xn", [P, TPS, C])
    xT = [sb(f"xT{k}", [P, KT, W + 1]) for k in range(2)]
    diff = sb("diff", [P, KT, W])
    mixed = [sb(f"mixed{k}", [P, KT, W]) for k in range(2)]
    mix_hi = [sb(f"mix_hi{k}", [P, KT, W], F32R) for k in range(4)]
    mix_lo = [sb(f"mix_lo{k}", [P, KT, W], F32R) for k in range(4)]
    rT = sb("rT", [P, KT, W])
    r_heads = sb("r_heads", [P, KT, HPB, W])
    r_dec = sb("r_dec", [P, KT, W])
    kT = sb("kT", [P, KT, W])
    k_dec = sb("k_dec", [P, TPS, C])
    v_pad = sb("v_pad", [P, TPS, H // 2, 4, N])
    gT = [sb(f"gT{k}", [P, KT, W]) for k in range(2)]
    attm = [sb(f"attm{k}", [P, HG, Q]) for k in range(4)]
    state = [sb(f"state{k}", [P, KT, P]) for k in range(2)]
    kvm = sb("kvm", [P, KT, P])
    ysq = sb("ysq", [P, KT, W])
    gvar = sb("gvar", [P, TPS * H])
    grstd = sb("grstd", [P, TPS, C])
    yn = sb("yn", [P, KT, W])
    nmean1 = sb("nmean1", [P, TPS])
    shift1 = sb("shift1", [P, TPS])
    nmean2 = sb("nmean2", [P, TPS])
    shift2 = sb("shift2", [P, TPS])
    z = sb("z", [P, KT, W])
    zg = sb("zg", [P, KT, W])
    x1 = [sb(f"x1_{k}", [P, TPS, C]) for k in range(2)]
    st2 = sb("st2", [P, TPS, 6])
    mv2 = sb("mv2", [P, TPS, 2])
    var2 = sb("var2", [P, TPS])
    rstd2 = sb("rstd2", [P, TPS])
    row = [sb(f"row{k}", [P, TPS, ROW]) for k in range(2)]
    x2T = sb("x2T", [P, KT, W])
    lmax = sb("lmax", [P, TPS])
    lsub = sb("lsub", [P, TPS, E])
    lexp = sb("lexp", [P, TPS, E])
    lsum = sb("lsum", [P, TPS])
    lrec = sb("lrec", [P, TPS])
    top = sb("top", [P, TPS, 8])
    topi = sb("topi", [P, TPS, 8], U32)
    topf = sb("topf", [P, TPS, 2])
    hot = [[sb(f"hot{k}_{r}", [P, TPS, E]) for k in range(2)] for r in range(2)]
    took = [sb(f"took{r}", [P, TPS, E]) for r in range(2)]
    before = [sb(f"before{r}", [P, TPS + 1, E]) for r in range(2)]
    over = sb("over", [P, TPS, E])
    slotf = sb("slotf", [P, TPS, E])
    pick = [sb(f"pick{k}", [P, TPS, E]) for k in range(2)]
    slot_k = sb("slot_k", [P, 2, TPS])
    slot_i = [sb(f"slot_i{k}", [P, 2, TPS], I32) for k in range(2)]
    mixt = sb("mixt", [P, KT, W])

    pX = ps("pX", [P, KT, W])
    pO = ps("pO", [P, 512])
    pK = ps("pK", [P, 512])
    pA = ps("pA", [P, KT, W])
    pB = ps("pB", [P, KT, W])
    pS = [ps(f"pS{k}", [P, HG, Q]) for k in range(2)]
    pY = ps("pY", [P, KT, W])

    SB = 3
    p_score = [pS[0][:], pS[1][:], pK[:, :].rearrange("p (h i) -> p h i", h=HG)]
    p_sums = pX[:, 0, 0:TPS * H].rearrange("p (t h) -> p t h", t=TPS)
    pO_tok = pO[:, :].rearrange("p (t c) -> p t c", t=TPS)
    pO_ch = pO[:, :].rearrange("p (k w) -> p k w", k=KT)
    pK_tok = pK[:, :].rearrange("p (t c) -> p t c", t=TPS)
    p_logit = pS[1][:, 0, 0:TPS * E].rearrange("p (t e) -> p t e", t=TPS)
    p_count = pS[0][:, 0, 0:TPS * E].rearrange("p (t e) -> p t e", t=TPS)
    p_total = pS[0][:, 0, TPS * E:(TPS + 1) * E]
    pA_tok = pA[:, :, :].rearrange("p a b -> p (a b)").rearrange("p (t c) -> p t c", t=TPS)
    p_kv = pA[:, :, :].rearrange("p a b -> p (a b)").rearrange("p (t k c) -> p t k c", t=TPS, k=KT)

    x_in = sem("x_in")
    const_in, late_in, decay_in = sem("const_in"), sem("late_in"), sem("decay_in")
    set_dve, set_pool, set_act = sem("set_dve"), sem("set_pool"), sem("set_act")
    empty_out = sem("empty_out")
    stat1_ready, rstd1_ready, xn_ready = sem("stat1_ready"), sem("rstd1_ready"), sem("xn_ready")
    xt_done, xT_ready = sem("xt_done"), sem("xT_ready")
    diff_ready = sem("diff_ready")
    mixed_ready, hi_ready, mix_ready = [[sem(f"{n}{k}") for k in range(4)] for n in ("mixed_ready", "hi_ready", "mix_ready")]
    w_hi_ready, w_lo_ready = sem("w_hi_ready"), sem("w_lo_ready")
    proj_done = [sem(f"proj_done{k}") for k in range(4)]
    rT_ready, kT_ready, v_ready, gT_ready = sem("rT_ready"), sem("kT_ready"), sem("v_ready"), sem("gT_ready")
    heads_ready, rdec_ready = sem("heads_ready"), sem("rdec_ready")
    kt_done, kdec_ready, kv_done, state_ready = sem("kt_done"), sem("kdec_ready"), sem("kv_done"), sem("state_ready")
    att_done, attm_ready, intra_done = sem("att_done"), sem("attm_ready"), sem("intra_done")
    ysq_ready, ssum_done, gvar_ready, yn_ready = sem("ysq_ready"), sem("ssum_done"), sem("gvar_ready"), sem("yn_ready")
    y_ready, grstd_ready, spread_done = sem("y_ready"), sem("grstd_ready"), sem("spread_done")
    z_ready, zg_ready, wo_done = sem("z_ready"), sem("zg_ready"), sem("wo_done")
    x1_ready, x1_out, stat2_ready, rstd2_ready = sem("x1_ready"), sem("x1_out"), sem("stat2_ready"), sem("rstd2_ready")
    xn2_ready, x2t_done, x2T_ready = sem("xn2_ready"), sem("x2t_done"), sem("x2T_ready")
    logit_done, lsub_ready, lexp_ready, took_ready = sem("logit_done"), sem("lsub_ready"), sem("lexp_ready"), sem("took_ready")
    count_done, slot_ready, sent = sem("count_done"), sem("slot_ready"), [sem(f"sent{k}") for k in range(2)]
    dve_chain, pool_chain = sem("dve_chain"), sem("pool_chain")
    taken_ready = sem("taken_ready")
    w_in = [sem(f"w_in{k}") for k in range(2)]
    whi_ready, wlo_ready = sem("whi_ready"), sem("wlo_ready")

    NCONST, NLATE = 1 + 4, 1 + 4
    x_view = x.rearrange("(s t p) c -> s p t c", t=TPS, p=P)
    out_view = out[0:NTOK, :].rearrange("(s t p) c -> s p t c", t=TPS, p=P)

    def walk(eng, step, before={}):
        for s in range(-1, SPB):
            if s in before:
                before[s]()
            step(At(s))
        with eng.Fori(SPB, STEPS - SPB + 1, SPB) as s0:
            for j in range(SPB):
                step(At(j, s0, SPB))
        for s in range(STEPS, STEPS + 3):
            if s in before:
                before[s]()
            step(At(s))

    with nc.Block() as block:

        @block.sync
        def _(sp):
            sp.dma_start(x_ring[:, 0], x_view[0]).then_inc(x_in, 16)
            sp.dma_start(maa_sb[:], maa).then_inc(const_in, 16)
            for k in range(5):
                sp.dma_start(w_in_sb[k], weights[k].rearrange("(k p) c -> p k c", p=P)).then_inc(const_in if k < 4 else late_in, 16)
            for dst, src in ((gate_sb, gateT.rearrange("(k p) e -> p k e", p=P)), (lnw_sb, lnw), (lnb_sb, lnb), (u_sb, u_row)):
                sp.dma_start(dst[:], src).then_inc(late_in, 16)
            sp.wait_ge(x_in, 16)
            sp.dma_start(x_ring[:, 1:], x_view[1:RING].rearrange("s p t c -> p s t c")).then_inc(x_in, 16)

            def clear_table(half):
                sp.wait_ge(set_pool, 4)
                for e in range(half * E // 2, (half + 1) * E // 2):
                    for h in range(2):
                        first = e * SLOTS + h * EH * P
                        sp.dma_start(disp[first:first + EH * P, :].rearrange("(p t) c -> p (t c)", p=P),
                                     empty.rearrange("p t c -> p (t c)")).then_inc(empty_out, 16)

            def step(s):
                front, post = s, s - 2
                if post.valid(STEPS):
                    post.wait(sp, x1_ready, 1, 1)
                    post.wait(sp, x1_out, 16)
                    q = post.count()
                    dst = out_view[q] if post.reg is None else out_view[bass.ds(q, 1)].rearrange("o p t c -> p (o t) c")
                    sp.dma_start(dst, x1[post.const % 2][:]).then_inc(x1_out, 16)
                    new = post + RING
                    if new.valid(STEPS):
                        q = new.count()
                        src = x_view[q] if new.reg is None else x_view[bass.ds(q, 1)].rearrange("o p t c -> p (o t) c")
                        sp.dma_start(x_ring[:, new.const % RING], src).then_inc(x_in, 16)
                if front.valid(STEPS):
                    front.wait(sp, rT_ready, 1, 1)
                    front.wait(sp, att_done, GPS)
                    if front.const == 0 and front.reg is None:
                        sp.wait_ge(set_pool, 2)
                    for h in range(HPB):
                        sp.dma_start(r_heads[h * N:(h + 1) * N, :, h, :], rT[h * N:(h + 1) * N, :, :]).then_inc(heads_ready, 16)

            def first_weights():
                sp.wait_ge(empty_out, 16 * 2 * E)
                for m in range(2):
                    sp.dma_start(wraw[m][:].rearrange("p (k f) -> p k f", k=KT),
                                 expert_views(*first_w, None)[m][0]).then_inc(w_in[m], 16)

            walk(sp, step, {2: lambda: clear_table(0), 3: lambda: clear_table(1), STEPS: first_weights})
            sp.wait_ge(x1_out, 16 * STEPS)
            sp.wait_ge(x_in, 16 * STEPS)

        @block.gpsimd
        def _(pool):
            chain = Chain(pool, pool_chain)
            chain.add(nc.gpsimd.memset(ones[:], 1.0))
            chain.add(nc.gpsimd.memset(mhalf[:], -0.5))
            chain.add(nc.gpsimd.memset(cut_off[:], 0.0))
            chain.add(nc.gpsimd.iota(lag_i[:], pattern=[[-1, Q]], base=1, channel_multiplier=1))
            chain.add(nc.gpsimd.iota(col_i[:], pattern=[[-1, Q]], base=0, channel_multiplier=0))
            chain.link(nc.gpsimd.iota(rest_i[:], pattern=[[0, 1]], base=1 - Q, channel_multiplier=1))
            chain.add(nc.gpsimd.affine_select(out=cut_off[:], in_=cut_off[:], compare_op=ALU.is_gt, fill=FAR,
                                              base=0, pattern=[[1, Q]], channel_multiplier=-1))
            nc.gpsimd.affine_select(out=ident[:], in_=ones[:], compare_op=ALU.is_equal, fill=0.0,
                                    base=0, pattern=[[1, P]], channel_multiplier=-1).then_inc(set_pool, 1)
            nc.gpsimd.memset(v_pad[:], 0.0)

            def tables():
                nc.gpsimd.memset(r_heads[:], 0.0).then_inc(set_pool, 1)
                chain.add(nc.gpsimd.memset(blockdiag[:], 1.0))
                chain.add(nc.gpsimd.iota(iota_i[:], pattern=[[1, E]], base=0, channel_multiplier=0))
                chain.add(nc.gpsimd.iota(base_i[:], pattern=[[SLOTS, E]], base=-1, channel_multiplier=0))
                chain.add(nc.gpsimd.iota(empty_i[:], pattern=[[1, EH]], base=NTOK, channel_multiplier=EH))
                chain.add(nc.gpsimd.iota(tok[:], pattern=[[P, NTOK // P]], base=0, channel_multiplier=1))
                chain.add(nc.gpsimd.affine_select(out=tri[:], in_=ones[:], compare_op=ALU.is_ge, fill=0.0,
                                                  base=0, pattern=[[1, P]], channel_multiplier=-1))
                chain.sync()
                bd = blockdiag[:].rearrange("p (g n) -> p g n", n=N)
                chain.link(nc.gpsimd.affine_select(out=bd, in_=bd, compare_op=ALU.is_ge, fill=0.0,
                                                   base=0, pattern=[[-N, P // N], [0, N]], channel_multiplier=1))
                chain.link(nc.gpsimd.affine_select(out=bd, in_=bd, compare_op=ALU.is_ge, fill=0.0,
                                                   base=N - 1, pattern=[[N, P // N], [0, N]], channel_multiplier=-1))
                chain.reset()
                nc.gpsimd.engine_nop().then_inc(set_pool, 1)

            def empty_rows():
                chain.link(nc.gpsimd.memset(empty, 0.0))
                chain.link(nc.gpsimd.tensor_copy(empty[:, :, ROW - 1].bitcast(I32), empty_i[:]))
                chain.reset()
                nc.gpsimd.engine_nop().then_inc(set_pool, 1)

            def scatter(send):
                send.wait(pool, slot_ready, 1, 1)
                if send.reg is None and send.const == 0:
                    pool.wait_ge(empty_out, 16 * 2 * E)
                pool.wait_ge(set_pool, 1)
                for k in range(2):
                    for t in range(TPS):
                        nc.gpsimd.indirect_dma_start(
                            disp, bass.IndirectOffsetOnAxis(ap=slot_i[send.const % 2][:, k, t:t + 1], axis=0),
                            row[send.const % 2][:, t, :], None,
                            bounds_check=E * SLOTS - 1, oob_is_err=False).then_inc(sent[send.const % 2], 16)

            def step(s):
                nxt, front, post, send = s + 1, s, s - 2, s - 3
                if post.valid(STEPS):
                    post.wait(pool, wo_done)
                    post.wait(pool, z_ready, 1, 1)
                    nc.gpsimd.tensor_tensor(zg[:], z[:], gT[post.const % 2][:], ALU.mult).then_inc(zg_ready, 1)
                if s.reg is None and s.const == STEPS + 1:
                    scatter(send - 1)
                first = s.reg is None and s.const == 0

                def norm():
                    nxt.wait(pool, stat1_ready, 1, 1)
                    pool.wait_ge(set_pool, 1)
                    chain.add(nc.gpsimd.tensor_scalar(nmean1[:], mv1[:, :, 0], -1.0, None, ALU.mult))
                    chain.link(nc.gpsimd.tensor_scalar(var1[:], mv1[:, :, 1], LN_EPS, None, ALU.add))
                    nxt.wait(pool, xn_ready)
                    chain.link(nc.gpsimd.tensor_tensor(rstd1[:], var1[:], mhalf[:, 0:TPS], ALU.pow))
                    nc.gpsimd.tensor_tensor(shift1[:], nmean1[:], rstd1[:], ALU.mult).then_inc(rstd1_ready, 1)

                if nxt.valid(STEPS) and not first:
                    norm()
                if front.valid(STEPS):
                    front.wait(pool, diff_ready, 1, 1)
                    front.wait(pool, mix_ready[3])
                    pool.wait_ge(set_pool, 1)
                    for k in range(KT):
                        chain.add(nc.gpsimd.tensor_scalar(mixt[:, k, :], diff[:, k, :], maa_sb[:, 3, k:k + 1], None, ALU.mult))
                    chain.sync()
                    nc.gpsimd.tensor_tensor(mixt[:], mixt[:], xT[front.const % 2][:, :, 1:], ALU.add).then_inc(mixed_ready[3], 1)
                if first:
                    norm()
                if post.valid(STEPS):
                    post.wait(pool, stat2_ready, 1, 1)
                    pool.wait_ge(set_pool, 1)
                    chain.add(nc.gpsimd.tensor_scalar(nmean2[:], mv2[:, :, 0], -1.0, None, ALU.mult))
                    chain.link(nc.gpsimd.tensor_scalar(var2[:], mv2[:, :, 1], LN_EPS, None, ALU.add))
                    post.wait(pool, xn2_ready)
                    chain.link(nc.gpsimd.tensor_tensor(rstd2[:], var2[:], mhalf[:, 0:TPS], ALU.pow))
                    nc.gpsimd.tensor_tensor(shift2[:], nmean2[:], rstd2[:], ALU.mult).then_inc(rstd2_ready, 1)
                if front.valid(STEPS):
                    front.wait(pool, hi_ready[3], 1, 1)
                    nc.gpsimd.tensor_tensor(mix_lo[3][:], mixt[:], mix_hi[3][:].bitcast(F32), ALU.subtract).then_inc(mix_ready[3], 1)
                    front.wait(pool, intra_done, GPS)
                    front.wait(pool, rT_ready, 1, 1)
                    if first:
                        pool.wait_ge(set_act, 2)
                    nc.gpsimd.tensor_tensor(
                        r_dec[:].rearrange("p k (t i) -> p k t i", i=Q), rT[:].rearrange("p k (t i) -> p k t i", i=Q),
                        rdecay[:].unsqueeze(2).to_broadcast([P, KT, TPS, Q]), ALU.mult).then_inc(rdec_ready, 1)
                if send.valid(STEPS) and s.const != STEPS:
                    scatter(send)
                if s.reg is None and s.const in (STEPS, STEPS + 1):
                    m = s.const - STEPS
                    for q in range(WP):
                        cut = slice(q * WPC, (q + 1) * WPC)
                        pool.wait_ge(whi_ready, WP * m + q + 1)
                        nc.gpsimd.tensor_tensor(wlo[m][:, cut], wraw[m][:, cut], whi[m][:, cut].bitcast(F32),
                                                ALU.subtract).then_inc(wlo_ready, 1)
                chain.reset()

            walk(pool, step, {0: tables, 1: empty_rows})
            for k in range(2):
                pool.wait_ge(sent[k], 16 * TPS * STEPS)

        @block.scalar
        def _(act):
            for dst, src in ((lam_row, decay_row), (lam_ch, decay_ch)):
                nc.scalar.dma_start(dst[:], src).then_inc(decay_in, 16)
            act.wait_ge(decay_in, 32)
            nc.scalar.activation(lam_row[:], lam_row[:], ACT.Exp)
            nc.scalar.activation(lam_ch[:], lam_ch[:], ACT.Exp).then_inc(set_act, 1)

            def decay_tables():
                act.wait_ge(set_dve, 1)
                nc.scalar.activation(dmask[:], dmask[:], ACT.Exp)
                for k in range(KT):
                    nc.scalar.activation(rdecay[:, k, :], colf[:], ACT.Exp, scale=lam_ch[:, k:k + 1])
                nc.scalar.activation(kdecay[:], lam_row[:], ACT.Exp, scale=rest[:, 0:1])
                nc.scalar.activation(sdecay[:], lam_ch[:], ACT.Exp, scale=-float(Q)).then_inc(set_act, 1)

            def weights_high(ks):
                act.wait_ge(const_in, 16 * NCONST)
                for k in ks:
                    if k == 2:
                        act.wait_ge(set_dve, 2)
                    nc.scalar.copy(w_hi[k][:], w_in_sb[k]).then_inc(w_hi_ready, 1)

            def step(s):
                nxt, front, att, post, send = s + 1, s, s - 1, s - 2, s - 3

                first = s.reg is None and s.const == 0

                def norm():
                    nxt.wait(act, rstd1_ready, 1, 1)
                    nxt.wait(act, xt_done)
                    xa = x_ring[:, nxt.const % RING]
                    for t in range(TPS):
                        ins = nc.scalar.activation(xn[:, t, :], xa[:, t, :], ACT.Identity,
                                                   scale=rstd1[:, t:t + 1], bias=shift1[:, t:t + 1])
                    ins.then_inc(xn_ready, 1)

                def mixing_hi(front, k):
                    front.wait(act, mixed_ready[k], 1, 1)
                    front.wait(act, proj_done[k])
                    nc.scalar.copy(mix_hi[k][:], mixt[:] if k == 3 else mixed[k % 2][:]).then_inc(hi_ready[k], 1)

                if front.valid(STEPS):
                    front.wait(act, xt_done, 1, 1)
                    front.wait(act, mixed_ready[2])
                    front.wait(act, mixed_ready[3])
                    nc.scalar.copy(xT[front.const % 2][:, :, 1:], pX[:]).then_inc(xT_ready, 1)
                    if first:
                        weights_high(range(2, 4))
                if send.valid(STEPS):
                    send.wait(act, lsub_ready, 1, 1)
                    nc.scalar.activation(lexp[:], lsub[:], ACT.Exp).then_inc(lexp_ready, 1)
                if nxt.valid(STEPS) and not first:
                    norm()
                if front.valid(STEPS):
                    for k in (0, 1, 3):
                        if k == 3 and first:
                            decay_tables()
                        mixing_hi(front, k)
                if post.valid(STEPS):
                    post.wait(act, rstd2_ready, 1, 1)
                    post.wait(act, sent[post.const % 2], 16 * TPS, -16 * TPS * (post.const % 2))
                    post.wait(act, x2t_done, 1, -1)
                    for t in range(TPS):
                        ins = nc.scalar.activation(row[post.const % 2][:, t, 0:C], x1[post.const % 2][:, t, :], ACT.Identity,
                                                   scale=rstd2[:, t:t + 1], bias=shift2[:, t:t + 1])
                    ins.then_inc(xn2_ready, 1)
                if att.valid(STEPS):
                    att.wait(act, intra_done, GPS, GPS)
                    att.wait(act, ssum_done)
                    nc.scalar.activation(ysq[:], pY[:], ACT.Square).then_inc(ysq_ready, 1)
                    att.wait(act, z_ready)
                    nc.scalar.copy(yn[:], pY[:]).then_inc(y_ready, 1)
                if front.valid(STEPS):
                    mixing_hi(front, 2)
                if front.valid(STEPS):
                    front.wait(act, proj_done[0], 1, 1)
                    front.wait(act, heads_ready, 16 * HPB)
                    front.wait(act, rdec_ready)
                    nc.scalar.copy(rT[:], pA[:]).then_inc(rT_ready, 1)
                    if first:
                        norm()
                if att.valid(STEPS):
                    att.wait(act, gvar_ready, 1, 1)
                    att.wait(act, spread_done)
                    nc.scalar.activation(grstd[:].rearrange("p t (h n) -> p (t h) n", n=N),
                                         gvar[:].unsqueeze(2).to_broadcast([P, TPS * H, N]), ACT.Sqrt).then_inc(grstd_ready, 1)
                if front.valid(STEPS):
                    front.wait(act, proj_done[1], 1, 1)
                    front.wait(act, att_done, GPS)
                    nc.scalar.copy(kT[:], pB[:]).then_inc(kT_ready, 1)
                if post.valid(STEPS):
                    post.wait(act, x2t_done, 1, 1)
                    post.wait(act, logit_done)
                    nc.scalar.copy(x2T[:], pO_ch).then_inc(x2T_ready, 1)
                if front.valid(STEPS):
                    front.wait(act, proj_done[2], 1, 1)
                    front.wait(act, intra_done, GPS)
                    nc.scalar.copy(v_pad[:, :, :, 0:4:3, :].rearrange("p t m a n -> p (t m) a n"),
                                   pA_tok.rearrange("p t (m a n) -> p (t m) a n", a=2, n=N)).then_inc(v_ready, 1)
                    front.wait(act, proj_done[3], 1, 1)
                    front.wait(act, zg_ready, 1, -1)
                    nc.scalar.activation(gT[front.const % 2][:], pB[:], ACT.Gelu).then_inc(gT_ready, 1)
                if att.valid(STEPS):
                    att.wait(act, yn_ready, 1, 1)
                    act.wait_ge(late_in, 16 * NLATE)
                    att.wait(act, zg_ready)
                    for k in range(KT):
                        ins = nc.scalar.activation(z[:, k, :], yn[:, k, :], ACT.Identity,
                                                   scale=lnw_sb[:, k:k + 1], bias=lnb_sb[:, k:k + 1])
                    ins.then_inc(z_ready, 1)

            def first_high():
                for m in range(2):
                    act.wait_ge(w_in[m], 16)
                    for q in range(WP):
                        cut = slice(q * WPC, (q + 1) * WPC)
                        nc.scalar.copy(whi[m][:, cut], wraw[m][:, cut]).then_inc(whi_ready, 1)

            walk(act, step, {0: lambda: weights_high(range(2)), STEPS: first_high})

        @block.vector
        def _(dve):
            chain = Chain(dve, dve_chain)
            dve.wait_ge(set_pool, 1)
            chain.link(nc.vector.tensor_copy(lag[:], lag_i[:]))
            chain.add(nc.vector.scalar_tensor_tensor(lag[:], lag[:], 0.0, cut_off[:], ALU.min, ALU.add))
            chain.add(nc.vector.tensor_copy(colf[:], col_i[:]))
            chain.add(nc.vector.tensor_copy(rest[:], rest_i[:]))
            chain.add(nc.vector.memset(state[0][:], 0.0))
            chain.add(nc.vector.memset(before[0][:], 0.0))
            chain.reset()

            def decay_logs():
                dve.wait_ge(set_act, 1)
                for lam in (lam_ch, lam_row):
                    chain.add(nc.vector.tensor_scalar(lam[:], lam[:], LAM_MAX, LAM_MIN, ALU.min, ALU.max))
                chain.sync()
                nc.vector.tensor_tensor(dmask[:], lam_row[:].unsqueeze(2).to_broadcast([P, H, Q]),
                                        lag[:].unsqueeze(1).to_broadcast([P, H, Q]), ALU.mult).then_inc(set_dve, 1)

            def weights_low(ks):
                for k in ks:
                    dve.wait_ge(w_hi_ready, k + 1)
                    nc.vector.tensor_tensor(w_lo[k][:], w_in_sb[k], w_hi[k][:].bitcast(F32), ALU.subtract).then_inc(w_lo_ready, 1)

            def center_v():
                dve.wait_ge(const_in, 16 * NCONST)
                wv4 = WV.rearrange("p k (h n) -> p (k h) n", n=N)
                chain.link(nc.vector.reduce_sum(vmean[:], wv4, axis=AX_X))
                chain.link(nc.vector.tensor_scalar(vmean[:], vmean[:], 1.0 / N, None, ALU.mult))
                nc.vector.tensor_tensor(wv4, wv4, vmean[:].unsqueeze(2).to_broadcast([P, KT * H, N]), ALU.subtract).then_inc(set_dve, 1)
                weights_low([0])
                chain.reset()

            def before_first():
                decay_logs()
                center_v()

            def slot_tables():
                dve.wait_ge(set_pool, 3)
                chain.add(nc.vector.tensor_copy(iota_e[:], iota_i[:]))
                chain.add(nc.vector.tensor_copy(base[:], base_i[:]))
                chain.link(nc.vector.tensor_copy(base0[:], base_i[:]))

            def bonus(half):
                dve.wait_ge(late_in, 16 * NLATE)
                dve.wait_ge(set_act, 2)
                for h in range(half * H // 2, (half + 1) * H // 2):
                    ins = nc.vector.scalar_tensor_tensor(dmask[:, h, :], ident[:], u_sb[:, h:h + 1], dmask[:, h, :],
                                                         ALU.mult, ALU.add)
                chain.link(ins)

            def ln_stats(src, stats, mv):
                for t in range(TPS):
                    chain.add(nc.vector.bn_stats(stats[:, t, :], src[:, t, :]))
                chain.sync()

            def mixing(s, k):
                if k == 2:
                    s.wait(dve, mix_ready[0], 1, 1)
                else:
                    s.wait(dve, mix_ready[2 if k == 0 else 1])
                for c in range(KT):
                    ins = nc.vector.scalar_tensor_tensor(mixed[k % 2][:, c, :], diff[:, c, :], maa_sb[:, k, c:c + 1],
                                                         xT[s.const % 2][:, c, 1:], ALU.mult, ALU.add)
                ins.then_inc(mixed_ready[k], 1)

            def mixing_lo(s, k):
                s.wait(dve, hi_ready[k], 1, 1)
                nc.vector.tensor_tensor(mix_lo[k][:], mixed[k % 2][:], mix_hi[k][:].bitcast(F32), ALU.subtract).then_inc(mix_ready[k], 1)

            def step(s):
                nxt, front, att, post, send = s + 1, s, s - 1, s - 2, s - 3
                par_f, par_p, par_s = front.const % 2, post.const % 2, send.const % 2

                def norm_stats():
                    if nxt.reg is None and nxt.const < RING:
                        dve.wait_ge(x_in, 32 if nxt.const else 16)
                    else:
                        nxt.wait(dve, x_in, 16, 16 * (2 - RING + 1))
                    xa = x_ring[:, nxt.const % RING]
                    nxt.wait(dve, rstd1_ready)
                    for t in range(TPS):
                        chain.add(nc.vector.bn_stats(st1[:, t, :], xa[:, t, :]))
                    chain.sync()
                    for t in range(TPS):
                        ins = nc.vector.bn_aggr(mv1[:, t, :], st1[:, t, :])
                    ins.then_inc(stat1_ready, 1)

                def mask_scores(g):
                    att.wait(dve, att_done, GPS, g + 1)
                    att.wait(dve, intra_done, GPS, g - 3)
                    q = g % NG
                    nc.vector.tensor_tensor(attm[g % 4][:], p_score[g % SB], dmask[:, q * HG:(q + 1) * HG, :],
                                            ALU.mult).then_inc(attm_ready, 1)

                def next_state(c):
                    last = c == TPS - 1
                    old, new = state[c], state[(c + 1) % 2]
                    if last and att.const % SPB == SPB - 1:
                        att.wait(dve, state_ready, TPS, c)
                        nc.vector.memset(new[:], 0.0).then_inc(state_ready, 1)
                        return
                    att.wait(dve, kv_done, 1, 1)
                    att.wait(dve, state_ready, TPS, c)
                    chain.link(nc.vector.tensor_tensor(kvm[:], p_kv[:, c], blockdiag[:].unsqueeze(1).to_broadcast([P, KT, P]), ALU.mult))
                    for k in range(KT):
                        ins = nc.vector.scalar_tensor_tensor(new[:, k, :], old[:, k, :], sdecay[:, k:k + 1], kvm[:, k, :],
                                                             ALU.mult, ALU.add)
                    ins.then_inc(state_ready, 1)

                def best_two():
                    send.wait(dve, lexp_ready, 1, 1)
                    prob = row[par_s][:, :, C:C + E]
                    chain.link(nc.vector.reduce_sum(lsum[:], lexp[:], axis=AX_X))
                    chain.link(nc.vector.reciprocal(lrec[:], lsum[:]))
                    ts = send.count(TPS)
                    src = tok[:, ts:ts + TPS] if send.reg is None else tok[:, bass.ds(ts, TPS)]
                    chain.add(nc.vector.tensor_copy(row[par_s][:, :, ROW - 1].bitcast(I32), src))
                    chain.link(nc.vector.tensor_tensor(prob, lexp[:], lrec[:].unsqueeze(2).to_broadcast([P, TPS, E]), ALU.mult))
                    for t in range(TPS):
                        chain.add(nc.vector.max(top[:, t, :], prob[:, t, :]))
                    chain.sync()
                    for t in range(TPS):
                        chain.add(nc.vector.max_index(topi[:, t, :], top[:, t, :], prob[:, t, :]))
                    chain.sync()

                def route():
                    chain.link(nc.vector.tensor_copy(topf[:], topi[:, :, 0:2]))
                    for k in range(2):
                        chain.add(nc.vector.tensor_tensor(hot[par_s][k][:], iota_e[:].unsqueeze(1).to_broadcast([P, TPS, E]),
                                                          topf[:, :, k:k + 1].to_broadcast([P, TPS, E]), ALU.is_equal))
                    chain.sync()
                    send.wait(dve, count_done)
                    chain.link(nc.vector.tensor_tensor(took[par_s][:], hot[par_s][0][:], hot[par_s][1][:], ALU.add))
                    chain.link(nc.vector.tensor_tensor(before[par_s][:, 1, :], before[par_s][:, 0, :], took[par_s][:, 0, :], ALU.add))
                    nc.vector.tensor_tensor(before[par_s][:, 2, :], before[par_s][:, 1, :], took[par_s][:, 1, :],
                                            ALU.add).then_inc(took_ready, 1)
                    following = before[1 - par_s][:, 0, :]
                    if send.const % SPB == SPB - 1:
                        chain.add(nc.vector.memset(following, 0.0))
                    else:
                        send.wait(dve, took_ready, 1, 1)
                        chain.add(nc.vector.tensor_copy(following, before[par_s][:, 2, :]))

                def slots():
                    send.wait(dve, count_done, 1, 1)
                    chain.add(nc.vector.tensor_scalar(over[:], p_count, float(CAP), DROP, ALU.is_gt, ALU.mult))
                    chain.link(nc.vector.tensor_tensor(slotf[:], p_count, base[:].unsqueeze(1).to_broadcast([P, TPS, E]), ALU.add))
                    if send.const % SPB == SPB - 1:
                        chain.link(nc.vector.scalar_tensor_tensor(base[:], p_total, float(CAP), base[:], ALU.min, ALU.add))
                    chain.link(nc.vector.tensor_tensor(slotf[:], slotf[:], over[:], ALU.add))
                    for k in range(2):
                        chain.add(nc.vector.tensor_tensor(pick[k][:], slotf[:], hot[par_s][k][:], ALU.mult))
                    chain.sync()
                    for k in range(2):
                        chain.add(nc.vector.reduce_sum(slot_k[:, k, :], pick[k][:], axis=AX_X))
                    chain.sync()
                    nc.vector.tensor_copy(slot_i[par_s][:], slot_k[:]).then_inc(slot_ready, 1)

                a, f, o, r = att.valid(STEPS), front.valid(STEPS), post.valid(STEPS), send.valid(STEPS)
                if r:
                    send.wait(dve, logit_done, 1, 1)
                    chain.link(nc.vector.reduce_max(lmax[:], p_logit, axis=AX_X))
                    nc.vector.tensor_tensor(lsub[:], p_logit, lmax[:].unsqueeze(2).to_broadcast([P, TPS, E]),
                                            ALU.subtract).then_inc(lsub_ready, 1)
                    if not (a or f):
                        best_two()
                        route()
                        if not o:
                            slots()
                first = s.reg is None and s.const == 0
                if nxt.valid(STEPS) and not first:
                    norm_stats()
                if f:
                    xt = xT[par_f]
                    if front.const % SPB == 0:
                        chain.add(nc.vector.memset(xt[:, :, 0:1], 0.0))
                    else:
                        chain.add(nc.vector.tensor_copy(xt[:, :, 0:1], xT[1 - par_f][:, :, W:W + 1]))
                    front.wait(dve, xT_ready, 1, 1)
                    front.wait(dve, mixed_ready[3])
                    chain.sync()
                    nc.vector.tensor_tensor(diff[:], xt[:, :, 0:W], xt[:, :, 1:], ALU.subtract).then_inc(diff_ready, 1)
                if a:
                    mask_scores(0)
                    next_state(0)
                    mask_scores(1)
                if f:
                    front.wait(dve, diff_ready, 1, 1)
                    mixing(front, 0)
                if a:
                    mask_scores(2)
                if f:
                    mixing(front, 1)
                if a:
                    mask_scores(3)
                    next_state(1)
                if a:
                    mask_scores(4)
                if f:
                    mixing_lo(front, 0)
                if first:
                    weights_low([1])
                if o:
                    post.wait(dve, wo_done, 1, 1)
                    post.wait(dve, x1_out, 16, -16)
                    post.wait(dve, xn2_ready)
                    src = x_ring[:, post.const % RING]
                    nc.vector.tensor_tensor(x1[par_p][:], src, pO_tok, ALU.add).then_inc(x1_ready, 1)
                if a:
                    mask_scores(5)
                if o:
                    post.wait(dve, x1_ready, 1, 1)
                    post.wait(dve, rstd2_ready)
                    ln_stats(x1[par_p], st2, mv2)
                    for t in range(TPS):
                        ins = nc.vector.bn_aggr(mv2[:, t, :], st2[:, t, :])
                    ins.then_inc(stat2_ready, 1)
                    if r and not (a or f):
                        slots()
                if a:
                    mask_scores(6)
                if a:
                    mask_scores(7)
                if f:
                    mixing_lo(front, 1)
                if f:
                    mixing(front, 2)
                if first:
                    norm_stats()
                if r and (a or f):
                    best_two()
                if first:
                    weights_low([2])
                if f:
                    mixing_lo(front, 2)
                if r and (a or f):
                    route()
                if first:
                    weights_low([3])
                if a:
                    att.wait(dve, ssum_done, 1, 1)
                    att.wait(dve, grstd_ready)
                    chain.link(nc.vector.tensor_scalar(gvar[:], pX[:, 0, 0:TPS * H], 1.0 / N, GN_EPS, ALU.mult, ALU.add))
                    nc.vector.reciprocal(gvar[:], gvar[:]).then_inc(gvar_ready, 1)
                if a:
                    att.wait(dve, spread_done, 1, 1)
                    att.wait(dve, y_ready, 1, 1)
                    nc.vector.tensor_tensor(yn[:], yn[:], pX[:], ALU.mult).then_inc(yn_ready, 1)
                if first:
                    bonus(0)
                if f:
                    front.wait(dve, kt_done, 1, 1)
                    front.wait(dve, kv_done)
                    nc.vector.tensor_tensor(k_dec[:].rearrange("p t (h n) -> p t h n", n=N),
                                            pK_tok.rearrange("p t (h n) -> p t h n", n=N),
                                            kdecay[:].unsqueeze(1).unsqueeze(3).to_broadcast([P, TPS, H, N]),
                                            ALU.mult).then_inc(kdec_ready, 1)
                if first:
                    bonus(1)
                    slot_tables()
                if r and (a or f):
                    slots()
                chain.reset()

            walk(dve, step, {0: before_first, 2: lambda: dve.wait_ge(set_pool, 4)})
            nc.vector.tensor_tensor(taken[:], base[:], base0[:], ALU.subtract).then_inc(taken_ready, 1)
            dve.wait_ge(taken_ready, 1)

        @block.tensor
        def _(pe):
            pe.wait_ge(set_pool, 1)

            def project(s, k, dst):
                s.wait(pe, mix_ready[k], 1, 1)
                if s.reg is None and s.const == 0:
                    pe.wait_ge(w_lo_ready, k + 1)
                for m in range(KT):
                    for c in range(KT):
                        cut = slice(m * P, (m + 1) * P)
                        nc.tensor.matmul(dst[:, m, :], w_hi[k][:, c, cut], mix_hi[k][:, c, :], start=(c == 0), stop=False)
                        nc.tensor.matmul(dst[:, m, :], w_hi[k][:, c, cut], mix_lo[k][:, c, :], start=False, stop=False)
                        ins = nc.tensor.matmul(dst[:, m, :], w_lo[k][:, c, cut], mix_hi[k][:, c, :], start=False, stop=(c == KT - 1))
                ins.then_inc(proj_done[k], 1)

            def v_block(t, c):
                return v_pad[:, t, c * HPB // 2:(c + 1) * HPB // 2, 0:4:3, :]

            def group_norm(att, front):
                att.wait(pe, ysq_ready, 1, 1)
                if front.valid(STEPS):
                    front.wait(pe, xT_ready, 1, 1)
                att.wait(pe, yn_ready)
                heads = blockdiag[:].rearrange("p (h n) -> p h n", n=N)[:, :, 0]
                for t in range(TPS):
                    for k in range(KT):
                        ins = nc.tensor.matmul(p_sums[:, t, k * HPB:(k + 1) * HPB], ysq[:, k, t * Q:(t + 1) * Q], heads,
                                               start=True, stop=True)
                ins.then_inc(ssum_done, 1)

            def spread(att):
                att.wait(pe, grstd_ready, 1, 1)
                for t in range(TPS):
                    for k in range(KT):
                        ins = nc.tensor.transpose(pX[:, k, t * Q:(t + 1) * Q], grstd[:, t, k * P:(k + 1) * P], ident[:])
                ins.then_inc(spread_done, 1)

            def step(s):
                front, att, post, send = s, s - 1, s - 2, s - 3

                def count(send):
                    if send.valid(STEPS):
                        send.wait(pe, took_ready, 1, 1)
                        if att.valid(STEPS):
                            att.wait(pe, attm_ready, GPS, GPS)
                        send.wait(pe, slot_ready)
                        r = send.const % 2
                        cnt = pS[0][:, 0, 0:TPS * E]
                        nc.tensor.matmul(pS[0][:, 0, 0:(TPS + 1) * E], ones[:], before[r][:].rearrange("p t e -> p (t e)"), start=True, stop=False)
                        nc.tensor.matmul(cnt, tri[:], took[r][:].rearrange("p t e -> p (t e)"), start=False, stop=True).then_inc(count_done, 1)

                if s.reg is None and s.const == 1:
                    pe.wait_ge(late_in, 16 * NLATE)
                    pe.wait_ge(set_pool, 3)
                if not att.valid(STEPS) and not post.valid(STEPS):
                    count(send)
                if front.valid(STEPS):
                    front.wait(pe, xn_ready, 1, 1)
                    front.wait(pe, yn_ready, 1, -1)
                    front.wait(pe, xT_ready)
                    for t in range(TPS):
                        for c in range(KT):
                            ins = nc.tensor.transpose(pX[:, c, t * Q:(t + 1) * Q], xn[:, t, c * P:(c + 1) * P], ident[:])
                    ins.then_inc(xt_done, 1)
                if att.valid(STEPS):
                    att.wait(pe, kdec_ready, 1, 1)
                    att.wait(pe, v_ready, 1, 1)
                    for t in range(TPS):
                        for c in range(KT):
                            ins = nc.tensor.matmul(p_kv[:, t, c, :], k_dec[:, t, c * P:(c + 1) * P], v_block(t, c),
                                                   start=True, stop=True)
                    ins.then_inc(kv_done, 1)
                    att.wait(pe, y_ready)
                    att.wait(pe, rdec_ready, 1, 1)
                    att.wait(pe, kT_ready, 1, 1)
                    att.wait(pe, heads_ready, 16 * HPB, 16 * HPB)

                    def across(t):
                        att.wait(pe, state_ready, TPS, t)
                        for c in range(KT):
                            nc.tensor.matmul(pY[:, c, t * Q:(t + 1) * Q], state[t][:, c, :], r_dec[:, c, t * Q:(t + 1) * Q],
                                             start=(t == 0 and c == 0), stop=False, skip_group_check=True)

                    def scores(g):
                        t, q = divmod(g, NG)
                        c, h = divmod(q * HG, HPB)
                        att.wait(pe, attm_ready, GPS, g - SB + 1)
                        if g == 0 and send.valid(STEPS):
                            send.wait(pe, slot_ready)
                        if g == 1 and send.valid(STEPS):
                            send.wait(pe, lsub_ready, 1, 1)
                        nc.tensor.matmul(p_score[g % SB], kT[:, c, t * Q:(t + 1) * Q], r_heads[:, c, h:h + HG, t * Q:(t + 1) * Q],
                                         start=True, stop=True).then_inc(att_done, 1)

                    def within(g):
                        t, q = divmod(g, NG)
                        att.wait(pe, attm_ready, GPS, g + 1)
                        for h in range(HG):
                            c, pos = divmod(q * HG + h, HPB)
                            ins = nc.tensor.matmul(pY[pos // 2 * 2 * N:(pos // 2 + 1) * 2 * N, c, t * Q:(t + 1) * Q],
                                                   v_pad[:, t, (q * HG + h) // 2, pos % 2 * 2:(pos % 2 + 1) * 2, :].rearrange("p a n -> p (a n)"),
                                                   attm[g % 4][:, h, :], start=False, stop=(g == GPS - 1 and h == HG - 1), skip_group_check=True)
                        ins.then_inc(intra_done, 1)

                    LEAD = SB - 1
                    across(0)
                    for g in range(LEAD):
                        scores(g)
                    for g in range(LEAD, NG + 1):
                        scores(g)
                        within(g - LEAD)
                if post.valid(STEPS):
                    post.wait(pe, zg_ready, 1, 1)
                    post.wait(pe, x2T_ready)
                    for t in range(TPS):
                        for c in range(KT):
                            ins = nc.tensor.matmul(pO_tok[:, t, :], zg[:, c, t * Q:(t + 1) * Q], WO[:, c, :],
                                                   start=(c == 0), stop=(c == KT - 1))
                    ins.then_inc(wo_done, 1)
                    if not att.valid(STEPS):
                        count(send)
                if att.valid(STEPS):
                    across(1)
                    for g in range(NG + 1, GPS):
                        scores(g)
                        within(g - LEAD)
                    for g in range(GPS - LEAD, GPS):
                        within(g)
                if front.valid(STEPS):
                    front.wait(pe, state_ready, TPS)
                    project(front, 0, pA)
                if att.valid(STEPS):
                    group_norm(att, front)
                if front.valid(STEPS):
                    front.wait(pe, gT_ready)
                    project(front, 1, pB)
                if post.valid(STEPS):
                    post.wait(pe, xn2_ready, 1, 1)
                    for t in range(TPS):
                        for c in range(KT):
                            ins = nc.tensor.transpose(pO_ch[:, c, t * Q:(t + 1) * Q], row[post.const % 2][:, t, c * P:(c + 1) * P], ident[:])
                    ins.then_inc(x2t_done, 1)
                if front.valid(STEPS):
                    front.wait(pe, mix_ready[2], 1, 1)
                    if front.reg is None and front.const == 0:
                        pe.wait_ge(w_lo_ready, 3)
                    front.wait(pe, rT_ready, 1, 1)
                    for t in range(TPS):
                        for c in range(KT):
                            cut = slice(t * Q, (t + 1) * Q)
                            nc.tensor.matmul(pA_tok[:, t, :], mix_hi[2][:, c, cut], w_hi[2][:, c, :], start=(c == 0), stop=False)
                            nc.tensor.matmul(pA_tok[:, t, :], mix_hi[2][:, c, cut], w_lo[2][:, c, :], start=False, stop=False)
                            ins = nc.tensor.matmul(pA_tok[:, t, :], mix_lo[2][:, c, cut], w_hi[2][:, c, :], start=False, stop=(c == KT - 1))
                    ins.then_inc(proj_done[2], 1)
                if att.valid(STEPS):
                    count(send)
                    spread(att)
                if front.valid(STEPS):
                    front.wait(pe, kT_ready, 1, 1)
                    front.wait(pe, kdec_ready)
                    if att.valid(STEPS):
                        att.wait(pe, attm_ready, GPS, GPS)
                    for t in range(TPS):
                        for c in range(KT):
                            ins = nc.tensor.transpose(pK_tok[:, t, c * P:(c + 1) * P], kT[:, c, t * Q:(t + 1) * Q], ident[:])
                    ins.then_inc(kt_done, 1)
                    project(front, 3, pB)
                if post.valid(STEPS):
                    post.wait(pe, x2T_ready, 1, 1)
                    if att.valid(STEPS):
                        att.wait(pe, attm_ready, GPS, GPS)
                    for t in range(TPS):
                        for c in range(KT):
                            ins = nc.tensor.matmul(p_logit[:, t, :], x2T[:, c, t * Q:(t + 1) * Q], gate_sb[:, c, :],
                                                   start=(c == 0), stop=(c == KT - 1))
                    ins.then_inc(logit_done, 1)

            walk(pe, step)


def phase_b(nc, sb, ps, ctx, sem, ident, whi, wlo, wraw, w1, w2, w3, taken, disp, out):
    CW = max(n for _, n in CHUNKS) * P
    xtok = sb("xtok", [P, ST, ROW])
    xh = sb("xh", [P, KT, SLOTS], F32R)
    xl = sb("xl", [P, KT, SLOTS], F32R)
    weight = [sb(f"weight{k}", [P, ST]) for k in range(2)]
    index = [sb(f"index{k}", [P, ST], I32) for k in range(2)]
    gated = [sb(f"gated{k}", [P, CW]) for k in range(2)]
    hid = [sb(f"hid{k}", [P, CW]) for k in range(2)]
    hh = [sb(f"hh{k}", [P, FT, CW], F32R) for k in range(2)]
    hl = [sb(f"hl{k}", [P, FT, CW], F32R) for k in range(2)]
    NY = 4
    ysb = [sb(f"ysb{k}", [P, C]) for k in range(NY)]

    p1 = [ps(f"p1_{k}", [P, CW]) for k in range(2)]
    p3 = [ps(f"p3_{k}", [P, CW]) for k in range(2)]
    py = [ps(f"py{k}", [P, 512]) for k in range(2)]
    pt = [ps(f"pt{k}", [P, 512]) for k in range(2)]

    rows_in, rows_used = [sem(f"rows_in{k}") for k in range(3)], sem("rows_used")
    w_in = [sem(f"w_in{k}") for k in range(2)]
    whi_ready, wlo_ready = sem("whi_ready"), sem("wlo_ready")
    turned, xh_ready, xl_ready = sem("turned"), sem("xh_ready"), sem("xl_ready")
    weight_ready, index_ready = sem("weight_ready"), sem("index_ready")
    h_done, gated_ready, hid_ready = sem("h_done"), sem("gated_ready"), sem("hid_ready")
    hh_ready, hl_ready = sem("hh_ready"), sem("hl_ready")
    ffn_done, ysb_ready, ysb_clear = sem("ffn_done"), sem("ysb_ready"), sem("ysb_clear")
    added = [sem(f"added{k}") for k in range(NY)]

    HPE = NCH * FT
    TB = 2 * NCH - 1
    rows_view = disp.rearrange("(e t p) c -> e p t c", e=E, p=P)
    w_view = expert_views(w1, w3, w2)

    def row_of(view, e):
        i = e.count()
        return view[i] if e.reg is None else view[bass.ds(i, 1)].squeeze(0)

    def pair(e):
        u = e.const % 2
        return e - u, u

    def where_taken(eng, e, tiles, work, other):
        i = e.count()
        n = eng.value_load(taken[0:1, i:i + 1] if e.reg is None else taken[0:1, bass.ds(i, 1)])
        with eng.If(n > tiles * P):
            work()
        with eng.Else():
            other()

    def pass_over(eng, e, *signals):
        for s, at, per, by in signals:
            e.wait(eng, s, per, at)
            eng.sem_inc(s, by)

    def run(eng, step):
        for e in range(2):
            step(At(e))
        with eng.Fori(2, E - 3, 2) as e0:
            for u in range(2):
                step(At(u, e0, 2))
        for e in range(E - 2, E):
            step(At(e))

    def banks():
        for c, (t0, n) in [*enumerate(CHUNKS)][1:] + [(0, CHUNKS[0])]:
            if n * P * KT <= 512:
                yield c, range(KT), range(t0, t0 + n)
            else:
                for k in range(KT):
                    yield c, range(k, k + 1), range(t0, t0 + n)

    ROW_LOADS = [CHUNKS[1], CHUNKS[2], CHUNKS[0]]

    BANKS = list(banks())
    assert len(BANKS) == TB
    LAST_BANK = [max(i for i, b in enumerate(BANKS) if b[0] == c) for c in range(NCH)]

    def bank_of(i, n):
        _, ks, ts = BANKS[i]
        w = len(ts) * P
        src = pt[n % 2][:, 0:len(ks) * w].rearrange("p (k s) -> p k s", k=len(ks))
        cut = (slice(None), slice(ks[0], ks[-1] + 1), slice(ts[0] * P, ts[0] * P + w))
        return src, cut

    def added_before(eng, e, more):
        even, u = pair(e)
        for r in range(NY):
            n = len(range(r, ST * u + more, NY))
            even.wait(eng, added[r], 16 * ST // NY, 16 * n)

    with nc.Block() as block:

        @block.sync
        def _(sp):
            def load_rows(e):
                e.wait(sp, turned, TB)
                e.wait(sp, rows_used, 2)
                for k, (t0, n) in enumerate(ROW_LOADS):
                    src = (t0 - REST) % ST
                    sp.dma_start(xtok[:, t0:t0 + n, :], row_of(rows_view, e)[:, src:src + n, :]).then_inc(rows_in[k], 16)

            def load_weights(e, m):
                even, u = pair(e)
                k = (3 * u + m) % 2
                e.wait(sp, wlo_ready, 3 * WP, WP * (m - 1))
                dst = wraw[k][:].rearrange("p (k f) -> p k f", k=KT if m < 2 else FT)
                sp.dma_start(dst, row_of(w_view[m], e)).then_inc(w_in[k], 16)

            load_rows(At(0))
            load_weights(At(0), 2)

            def step(e):
                nxt = e + 1
                if nxt.valid(E):
                    for m in range(2):
                        load_weights(nxt, m)
                    load_rows(nxt)
                    load_weights(nxt, 2)

            run(sp, step)

        @block.gpsimd
        def _(pool):
            def keep_index(e):
                for k in range(3):
                    e.wait(pool, rows_in[k], 16, 16)
                pool.wait_ge(rows_in[0], 16)
                nc.gpsimd.tensor_copy(index[e.const % 2][:], xtok[:, :, ROW - 1].bitcast(I32)).then_inc(index_ready, 1)
                e.wait(pool, index_ready, 1, 1)
                pool.sem_inc(rows_used, 1)

            def split_lo(e, m):
                u = pair(e)[1]
                k = (3 * u + m) % 2
                for q in range(WP):
                    cut = slice(q * WPC, (q + 1) * WPC)
                    e.wait(pool, whi_ready, 3 * WP, WP * m + q + 1)
                    pool.wait_ge(rows_in[0], 16)
                    nc.gpsimd.tensor_tensor(wlo[e.const % 2][m][:, cut], wraw[k][:, cut], whi[e.const % 2][m][:, cut].bitcast(F32),
                                            ALU.subtract).then_inc(wlo_ready, 1)

            pool.wait_ge(ysb_clear, REST)
            keep_index(At(0))
            split_lo(At(0), 2)

            def step(e):
                if (e + 1).valid(E):
                    for m in range(3):
                        split_lo(e + 1, m)
                added_before(pool, e, 0)
                u = pair(e)[1]

                def add(t):
                    j = ST * u + t
                    e.wait(pool, ysb_ready, ST, t + 1)
                    pool.wait_ge(rows_in[0], 16)
                    nc.gpsimd.indirect_dma_start(
                        out, bass.IndirectOffsetOnAxis(ap=index[e.const % 2][:, t:t + 1], axis=0),
                        ysb[j % NY][:], None, compute_op=ALU.add).then_inc(added[j % NY], 16)

                for t in range(ST):
                    add(t)
                    if t == ST - 3 and (e + 1).valid(E):
                        keep_index(e + 1)

            run(pool, step)
            added_before(pool, At(E), 0)

        @block.scalar
        def _(act):
            def split_hi(e, m, q):
                even, u = pair(e)
                cut = slice(q * WPC, (q + 1) * WPC)
                even.wait(act, w_in[(3 * u + m) % 2], 24, 16 * ((3 * u + m) // 2 + 1))
                if m < 2:
                    e.wait(act, h_done, HPE, -HPE)
                else:
                    e.wait(act, ffn_done, ST, -ST)
                nc.scalar.copy(whi[e.const % 2][m][:, cut], wraw[(3 * u + m) % 2][:, cut]).then_inc(whi_ready, 1)

            def turn_hi(e, i):
                u = e.const % 2
                src, cut = bank_of(i, TB * u + i)
                e.wait(act, turned, TB, i + 1)
                nc.scalar.copy(xh[cut], src).then_inc(xh_ready, 1)

            def gate(e, c, f):
                k = (pair(e)[1] * HPE + c * FT + f) % 2
                w = CHUNKS[c][1] * P
                e.wait(act, h_done, HPE, c * FT + f + 1)
                e.wait(act, hid_ready, HPE, c * FT + f - 1)
                nc.scalar.activation(gated[k][:, 0:w], p1[k][:, 0:w], ACT.Silu).then_inc(gated_ready, 1)

            def hidden_hi(e, c, f):
                u = pair(e)[1]
                k = (u * HPE + c * FT + f) % 2
                w = CHUNKS[c][1] * P
                e.wait(act, hid_ready, HPE, c * FT + f + 1)
                if f == 0:
                    free_hidden(act, e, c)
                nc.scalar.copy(hh[(u * NCH + c) % 2][:, f, 0:w], hid[k][:, 0:w]).then_inc(hh_ready, 1)

            def scale_out(e, t):
                j = ST * pair(e)[1] + t
                even, u = pair(e)
                e.wait(act, ffn_done, ST, t + 1)
                e.wait(act, weight_ready, 1, 1)
                if e.reg is not None or ST * e.const + t >= NY:
                    even.wait(act, added[j % NY], 16 * ST // NY, 16 * (j // NY))
                nc.scalar.activation(ysb[j % NY][:], py[j % 2][:, 0:C], ACT.Copy, scale=weight[e.const % 2][:, t:t + 1]).then_inc(ysb_ready, 1)

            def hidden(e, c, pieces):
                for f in range(FT):
                    gate(e, c, f)
                    if f:
                        hidden_hi(e, c, f - 1)
                        if pieces:
                            split_hi(e + 1, *pieces.pop(0))
                hidden_hi(e, c, FT - 1)

            def scale_chunk(e, c):
                t0, n = CHUNKS[c]
                for t in range(t0, t0 + n):
                    scale_out(e, t)

            def scale_rest(e, t):
                def work():
                    scale_out(e, t)
                    if t + 1 < REST:
                        scale_rest(e, t + 1)

                where_taken(act, e, COMMON + t, work, lambda: pass_over(act, e, (ysb_ready, t, ST, REST - t)))

            act.wait_ge(ysb_clear, REST)
            for i in range(TB - 1):
                turn_hi(At(0), i)
            for q in range(WP):
                split_hi(At(0), 2, q)

            def step(e):
                nxt = e + 1
                more = nxt.valid(E)
                pieces = [(m, q) for m in range(3) for q in range(WP)] if more else []

                def hidden_rest():
                    turn_hi(e, TB - 1)
                    hidden(e, 0, [])

                where_taken(act, e, COMMON, hidden_rest, lambda: pass_over(
                    act, e, (xh_ready, TB - 1, TB, 1), (gated_ready, 0, HPE, FT), (hh_ready, 0, HPE, FT)))
                hidden(e, 1, pieces)
                scale_rest(e, 0)
                hidden(e, 2, pieces)
                assert not pieces
                scale_chunk(e, 1)
                t0, n = CHUNKS[2]
                todo = list(range(TB - 1)) if more else []
                for t in range(t0, t0 + n):
                    if todo:
                        turn_hi(nxt, todo.pop(0))
                    scale_out(e, t)
                assert not todo

            def free_hidden(eng, e, c):
                n = c - 2 if c >= 2 else c - 2 + NCH
                past = e if c >= 2 else e - 1
                t0, cnt = CHUNKS[n]
                past.wait(eng, ffn_done, ST, t0 + cnt)

            run(act, step)

        @block.vector
        def _(dve):
            def turn_lo(e, i):
                src, cut = bank_of(i, TB * (e.const % 2) + i)
                e.wait(dve, xh_ready, TB, i + 1)
                nc.vector.tensor_tensor(xl[cut], src, xh[cut].bitcast(F32), ALU.subtract).then_inc(xl_ready, 1)

            def keep_weight(e):
                for k in range(3):
                    e.wait(dve, rows_in[k], 16, 16)
                e.wait(dve, ysb_ready, ST, -ST)
                col = e.count(1, C)
                src = xtok[:, :, col] if e.reg is None else xtok[:, :, bass.ds(col, 1)].squeeze(2)
                nc.vector.tensor_scalar(weight[e.const % 2][:], src, 1.0, None, ALU.mult).then_inc(weight_ready, 1)
                e.wait(dve, weight_ready, 1, 1)
                dve.sem_inc(rows_used, 1)

            def hidden_value(e, c, f):
                k = (pair(e)[1] * HPE + c * FT + f) % 2
                w = CHUNKS[c][1] * P
                e.wait(dve, gated_ready, HPE, c * FT + f + 1)
                e.wait(dve, hl_ready, HPE, c * FT + f - 1)
                nc.vector.tensor_tensor(hid[k][:, 0:w], gated[k][:, 0:w], p3[k][:, 0:w], ALU.mult).then_inc(hid_ready, 1)

            def hidden_lo(e, c, f):
                u = pair(e)[1]
                k = (u * HPE + c * FT + f) % 2
                w = CHUNKS[c][1] * P
                e.wait(dve, hh_ready, HPE, c * FT + f + 1)
                s = (u * NCH + c) % 2
                nc.vector.tensor_tensor(hl[s][:, f, 0:w], hid[k][:, 0:w], hh[s][:, f, 0:w].bitcast(F32),
                                        ALU.subtract).then_inc(hl_ready, 1)

            def hidden(e, c):
                for f in range(FT):
                    hidden_value(e, c, f)
                    if f:
                        hidden_lo(e, c, f - 1)
                hidden_lo(e, c, FT - 1)

            for k in range(REST):
                nc.vector.memset(ysb[k][:], 0.0).then_inc(ysb_clear, 1)
            for i in range(TB - 1):
                turn_lo(At(0), i)
            keep_weight(At(0))

            def step(e):
                nxt = e + 1
                more = nxt.valid(E)

                def hidden_rest():
                    turn_lo(e, TB - 1)
                    hidden(e, 0)

                where_taken(dve, e, COMMON, hidden_rest, lambda: pass_over(
                    dve, e, (xl_ready, TB - 1, TB, 1), (hid_ready, 0, HPE, FT), (hl_ready, 0, HPE, FT)))
                hidden(e, 1)
                hidden(e, 2)
                if more:
                    for i in range(TB - 1):
                        turn_lo(nxt, i)
                    keep_weight(nxt)

            run(dve, step)

        @block.tensor
        def _(pe):
            def turn(e, i):
                n = TB * (e.const % 2) + i
                _, ks, ts = BANKS[i]
                e.wait(pe, rows_in[next(k for k, (t0, n) in enumerate(ROW_LOADS) if t0 <= ts[0] < t0 + n)], 16, 16)
                e.wait(pe, xl_ready, TB, i - 1)
                src, _ = bank_of(i, n)
                for a, k in enumerate(ks):
                    for b, t in enumerate(ts):
                        ins = nc.tensor.transpose(src[:, a, b * P:(b + 1) * P], xtok[:, t, k * P:(k + 1) * P], ident[:])
                ins.then_inc(turned, 1)

            def up(e, c):
                u = pair(e)[1]
                t0, n = CHUNKS[c]
                w = n * P
                e.wait(pe, xl_ready, TB, LAST_BANK[c] + 1)
                e.wait(pe, wlo_ready, 3 * WP, 2 * WP)
                hi, lo = whi[e.const % 2], wlo[e.const % 2]
                for f in range(FT):
                    k = (u * HPE + c * FT + f) % 2
                    e.wait(pe, hid_ready, HPE, c * FT + f - 1)
                    for m, dst in ((0, p1[k]), (1, p3[k])):
                        for kt in range(KT):
                            wcut = slice(kt * F + f * P, kt * F + (f + 1) * P)
                            xcut = (slice(None), kt, slice(t0 * P, t0 * P + w))
                            nc.tensor.matmul(dst[:, 0:w], hi[m][:, wcut], xh[xcut], start=(kt == 0), stop=False)
                            nc.tensor.matmul(dst[:, 0:w], hi[m][:, wcut], xl[xcut], start=False, stop=False)
                            ins = nc.tensor.matmul(dst[:, 0:w], lo[m][:, wcut], xh[xcut], start=False, stop=(kt == KT - 1))
                    ins.then_inc(h_done, 1)

            def down(e, t):
                u = pair(e)[1]
                c = next(i for i, (t0, n) in enumerate(CHUNKS) if t0 <= t < t0 + n)
                s = (u * NCH + c) % 2
                j = ST * u + t
                e.wait(pe, hl_ready, HPE, FT * (c + 1))
                e.wait(pe, wlo_ready, 3 * WP, 3 * WP)
                e.wait(pe, ysb_ready, ST, t - 1)
                off = (t - CHUNKS[c][0]) * P
                hi, lo = whi[e.const % 2][2], wlo[e.const % 2][2]
                for f in range(FT):
                    a, b = hh[s][:, f, off:off + P], hl[s][:, f, off:off + P]
                    cut = slice(f * C, (f + 1) * C)
                    nc.tensor.matmul(py[j % 2][:, 0:C], a, hi[:, cut], start=(f == 0), stop=False)
                    nc.tensor.matmul(py[j % 2][:, 0:C], a, lo[:, cut], start=False, stop=False)
                    ins = nc.tensor.matmul(py[j % 2][:, 0:C], b, hi[:, cut], start=False, stop=(f == FT - 1))
                ins.then_inc(ffn_done, 1)

            def down_chunk(e, c):
                t0, n = CHUNKS[c]
                for t in range(t0, t0 + n):
                    down(e, t)

            def down_rest(e, t):
                def work():
                    down(e, t)
                    if t + 1 < REST:
                        down_rest(e, t + 1)

                where_taken(pe, e, COMMON + t, work, lambda: pass_over(pe, e, (ffn_done, t, ST, REST - t)))

            for i in range(TB - 1):
                turn(At(0), i)

            def step(e):
                nxt = e + 1

                def up_rest():
                    turn(e, TB - 1)
                    up(e, 0)

                where_taken(pe, e, COMMON, up_rest, lambda: pass_over(pe, e, (turned, TB - 1, TB, 1), (h_done, 0, HPE, FT)))
                up(e, 1)
                down_rest(e, 0)
                up(e, 2)
                down_chunk(e, 1)
                t0, n = CHUNKS[2]
                todo = list(range(TB - 1)) if nxt.valid(E) else []
                for t in range(t0, t0 + n):
                    if todo:
                        turn(nxt, todo.pop(0))
                    down(e, t)
                assert not todo

            run(pe, step)


def kernel(**inputs):
    import concourse.bacc as bacc
    from concourse.bass_utils import run_bass_kernel_spmd

    a = {k: np.asarray(v) for k, v in inputs.items()}

    def by_channel(v):
        return v.reshape(KT, P).T

    att = "L0_attn_"
    arrays = {
        "x": np.concatenate([a[att + "x"].reshape(NTOK, C), np.zeros((TPS * W, C), np.float32)]),
        "maa": np.stack([by_channel(a[att + "time_maa_" + k]) for k in "rkvg"], axis=1),
        "decay_row": np.broadcast_to(a[att + "time_decay"].reshape(1, H), (P, H)),
        "decay_ch": by_channel(np.repeat(a[att + "time_decay"].reshape(H), N)),
        "u_row": np.broadcast_to(a[att + "time_faaaa"].reshape(1, H), (P, H)),
        "wrT": a[att + "Wr"].T, "wkT": a[att + "Wk"].T, "wvT": a[att + "Wv"].T,
        "wgT": a[att + "Wg"].T, "woT": a[att + "Wo"].T,
        "lnw": by_channel(a[att + "ln_w"]), "lnb": by_channel(a[att + "ln_b"]),
        "gateT": a["L0_ffn_gate_w"].T,
        "w1": a["L0_ffn_w1"], "w2": a["L0_ffn_w2"], "w3": a["L0_ffn_w3"],
    }
    arrays = {f"in_{k}": np.ascontiguousarray(v) for k, v in arrays.items()}
    nc = bacc.Bacc("TRN2", target_bir_lowering=False, num_devices=1)
    args = [nc.dram_tensor(k, v.shape, mybir.dt.from_np(v.dtype), kind="ExternalInput").ap() for k, v in arrays.items()]
    args.append(nc.dram_tensor("out", [NTOK + SLOTS, C], F32, kind="ExternalOutput").ap())
    build(nc, *args)
    r = run_bass_kernel_spmd(nc, [arrays], core_ids=[0])
    return r.results[0]["out"][:NTOK].reshape(B, T, C)
```
